# Optimizing a Trainium2 kernel written in Bass

```python
import numpy as np
import jax
import jax.numpy as jnp

def _softmax(x, axis=-1):
    return jax.nn.softmax(x, axis=axis)

def _gelu(x):
    return jax.nn.gelu(x, approximate=True)

def _silu(x):
    return jax.nn.silu(x)

def _sigmoid(x):
    return jax.nn.sigmoid(x)

def _layernorm(x, axis=-1, eps=1e-05):
    m = jnp.mean(x, axis=axis, keepdims=True)
    v = jnp.var(x, axis=axis, keepdims=True)
    return (x - m) / jnp.sqrt(v + eps)

def _scatter_add(tgt, idx, src, axis=0):
    return tgt.at[idx].add(src)

def _segment_sum(src, seg, n):
    return jax.ops.segment_sum(src, seg, n)
kernel_name = 'mk_perceiver_d2_seqx_r8_c7b535'

def setup_inputs(seed: int=0):
    np.random.seed(seed)
    _w = jnp.asarray

    def _rec_inputs():
        import jax
        import jax.numpy as jnp
        _rk = jax.random.key(seed)
        x = -0.0002928 + 1 * jax.random.normal(jax.random.fold_in(_rk, 1), (64, 32, 256), jnp.float32)
        _lenS = 32 - jax.random.randint(jax.random.fold_in(_rk, 7), (64,), 0, max(1, 32 // 4) + 1, jnp.int32)
        _lenS2 = 257 - jax.random.randint(jax.random.fold_in(_rk, 8), (64,), 0, max(1, 257 // 4) + 1, jnp.int32)
        _ctx_2048P = jax.random.normal(jax.random.fold_in(_rk, 11), (64, 16, 256), jnp.float32)
        _ctx_2048c = jax.random.dirichlet(jax.random.fold_in(_rk, 511), 0.3 * jnp.ones((16,), jnp.float32), (64, 257))
        _ctx_2048t = jnp.einsum('bsk,bkd->bsd', _ctx_2048c, _ctx_2048P)
        _ctx_2048t = _ctx_2048t * jax.lax.rsqrt(jnp.mean(jnp.square(_ctx_2048t)) + 1e-12) * 0.953939
        ctx_2048 = 4.13588e-05 + 0.999923 * (_ctx_2048t + 0.3 * jax.random.normal(jax.random.fold_in(_rk, 611), (64, 257, 256), jnp.float32))
        _validS = jnp.arange(32)[None, :] < _lenS[:, None]
        _validS2 = jnp.arange(257)[None, :] < _lenS2[:, None]
        _causal = jnp.tril(jnp.ones((32, 32), dtype=bool))
        mask_1xSxS2_ff0 = jnp.where(jnp.ones((1, 32, 257), dtype=bool), 0.0, -1000000000.0).astype(jnp.float32)
        return (x, ctx_2048, mask_1xSxS2_ff0)
    x, ctx_2048, mask_1xSxS2_ff0 = _rec_inputs()

    def _L0_xattn_setup():
        import jax, jax.numpy as jnp
        import numpy as np
        H = 256
        NH = 16
        NKV = 4
        HD = 128
        GROUPS = NH // NKV
        EPS = 1e-06
        B, S, SE = (1, 256, 512)

        def _rmsnorm(x, w, eps=EPS):
            xf = x.astype(jnp.float32)
            var = jnp.mean(xf * xf, axis=-1, keepdims=True)
            return (xf * jax.lax.rsqrt(var + eps)).astype(x.dtype) * w
        key = jax.random.key(seed)
        ks = jax.random.split(key, 12)
        sc = 0.02
        return {'hidden_states': jax.random.normal(ks[0], (B, S, H), jnp.float32), 'encoder_hidden_states': jax.random.normal(ks[1], (B, SE, H), jnp.float32), 'attention_mask': jnp.zeros((B, S, SE), jnp.float32), 'Wq': jax.random.normal(ks[2], (H, NH * HD), jnp.float32) * sc, 'bq': jax.random.normal(ks[3], (NH * HD,), jnp.float32) * sc, 'Wk': jax.random.normal(ks[4], (H, NKV * HD), jnp.float32) * sc, 'bk': jax.random.normal(ks[5], (NKV * HD,), jnp.float32) * sc, 'Wv': jax.random.normal(ks[6], (H, NKV * HD), jnp.float32) * sc, 'bv': jax.random.normal(ks[7], (NKV * HD,), jnp.float32) * sc, 'Wo': jax.random.normal(ks[8], (NH * HD, H), jnp.float32) * sc, 'qn_w': jnp.ones((HD,), jnp.float32), 'kn_w': jnp.ones((HD,), jnp.float32)}
    _L0_xattn_all = _L0_xattn_setup()
    _L0_xattn_in = {k: v for k, v in _L0_xattn_all.items() if k in ('Wq', 'bq', 'Wk', 'bk', 'Wv', 'bv', 'Wo', 'qn_w', 'kn_w')}
    del _L0_xattn_all

    def _L0_attn_setup():
        import jax, jax.numpy as jnp
        import numpy as np
        NUM_HEADS = 16
        key = jax.random.key(seed)
        ks = jax.random.split(key, 6)
        B, N, E = (2, 256, 256)
        QK, V, M = (256, 256, 512)
        x = jax.random.normal(ks[0], (B, N, E), dtype=jnp.float32)
        Wq = jax.random.normal(ks[1], (QK, E), dtype=jnp.float32) * 0.02
        k_weight = jax.random.normal(ks[2], (M, QK), dtype=jnp.float32) * 0.05
        v_weight = jax.random.normal(ks[3], (M, V), dtype=jnp.float32) * 0.05
        Wg = jax.random.normal(ks[4], (V, E), dtype=jnp.float32) * 0.02
        Wout = jax.random.normal(ks[5], (E, V), dtype=jnp.float32) * 0.02
        return {'x': x, 'Wq': Wq, 'k_weight': k_weight, 'v_weight': v_weight, 'Wg': Wg, 'Wout': Wout}
    _L0_attn_all = _L0_attn_setup()
    _L0_attn_in = {k: v for k, v in _L0_attn_all.items() if k in ('Wq', 'k_weight', 'v_weight', 'Wg', 'Wout')}
    del _L0_attn_all

    def _L0_ffn_setup():
        import jax, jax.numpy as jnp
        import numpy as np
        B, S, DIM = (2, 256, 256)
        INTER = 128
        E = 8
        K = 2
        N_SHARED = 1
        ROUTE_SCALE = 1.0
        key = jax.random.key(seed)
        ks = jax.random.split(key, 8)
        s_in = 1.0 / np.sqrt(DIM)
        s_hid = 1.0 / np.sqrt(INTER)
        return {'x': jax.random.normal(ks[0], (B, S, DIM), dtype=jnp.float32), 'gate_w': jax.random.normal(ks[1], (E, DIM), dtype=jnp.float32) * s_in, 'w1': jax.random.normal(ks[2], (E, INTER, DIM), dtype=jnp.float32) * s_in, 'w2': jax.random.normal(ks[3], (E, DIM, INTER), dtype=jnp.float32) * s_hid, 'w3': jax.random.normal(ks[4], (E, INTER, DIM), dtype=jnp.float32) * s_in, 'ws1': jax.random.normal(ks[5], (N_SHARED * INTER, DIM), dtype=jnp.float32) * s_in, 'ws2': jax.random.normal(ks[6], (DIM, N_SHARED * INTER), dtype=jnp.float32) * s_hid, 'ws3': jax.random.normal(ks[7], (N_SHARED * INTER, DIM), dtype=jnp.float32) * s_in}
    _L0_ffn_all = _L0_ffn_setup()
    _L0_ffn_in = {k: v for k, v in _L0_ffn_all.items() if k in ('gate_w', 'w1', 'w2', 'w3', 'ws1', 'ws2', 'ws3')}
    del _L0_ffn_all

    def _L1_xattn_setup():
        import jax, jax.numpy as jnp
        import numpy as np
        FP8_MAX = 448.0
        EPS = 1e-05

        def _fp8_roundtrip(x):
            return x.astype(jnp.float8_e4m3fn).astype(jnp.float32)

        def _div_clamp_fp8(x, scale):
            y = jnp.clip(x.astype(jnp.float32) / scale, -FP8_MAX, FP8_MAX)
            y = y.astype(jnp.bfloat16).astype(jnp.float32)
            return _fp8_roundtrip(y)

        def _ln(x, w, b):
            mu = jnp.mean(x, axis=-1, keepdims=True)
            var = jnp.mean(jnp.square(x - mu), axis=-1, keepdims=True)
            return (x - mu) * jax.lax.rsqrt(var + EPS) * w + b

        def _fp8_linear_pertensor(x, wq, w_scale, in_scale):
            xq = _div_clamp_fp8(x, in_scale)
            return jnp.einsum('bsi,oi->bso', xq * in_scale, wq) * w_scale

        def _gqa(q, k, v):
            scale = 1.0 / np.sqrt(q.shape[-1])
            scores = jnp.einsum('bsghd,btgd->bghst', q, k) * scale
            p = jax.nn.softmax(scores, axis=-1)
            return jnp.einsum('bghst,btgd->bsghd', p, v)
        key = jax.random.key(seed)
        ks = jax.random.split(key, 8)
        B, S, SC, H, NH, G, D = (2, 256, 64, 256, 16, 8, 128)

        def qw(k, out_f, in_f):
            w = jax.random.normal(k, (out_f, in_f), jnp.float32) * 0.02
            sc = jnp.max(jnp.abs(w)) / FP8_MAX
            return (_fp8_roundtrip(w / sc), sc.astype(jnp.float32))
        wq, wq_s = qw(ks[0], NH * D, H)
        wqx, wqx_s = qw(ks[1], NH * D, H)
        wk, wk_s = qw(ks[2], G * D, H)
        wv, wv_s = qw(ks[3], G * D, H)
        wproj, wp_s = qw(ks[4], H, 2 * NH * D)
        return {'hidden_states': jax.random.normal(ks[5], (B, S, H), jnp.float32), 'cond': jax.random.normal(ks[6], (B, SC, H), jnp.float32), 'ln_w': jnp.ones((H,), jnp.float32), 'ln_b': jnp.zeros((H,), jnp.float32), 'wq': wq, 'wq_scale': wq_s, 'q_in_scale': jnp.full((H,), 0.05, jnp.float32), 'wqx': wqx, 'wqx_scale': wqx_s, 'qx_in_scale': jnp.full((H,), 0.05, jnp.float32), 'wk': wk, 'wk_scale': wk_s, 'k_in_scale': jnp.full((H,), 0.05, jnp.float32), 'wv': wv, 'wv_scale': wv_s, 'v_in_scale': jnp.full((H,), 0.05, jnp.float32), 'w_kv_x': jax.random.normal(ks[7], (2 * G * D, H), jnp.float32) * 0.02, 'qln_w': jnp.ones((D,), jnp.float32), 'qln_b': jnp.zeros((D,), jnp.float32), 'kln_w': jnp.ones((D,), jnp.float32), 'kln_b': jnp.zeros((D,), jnp.float32), 'qxln_w': jnp.ones((D,), jnp.float32), 'qxln_b': jnp.zeros((D,), jnp.float32), 'kxln_w': jnp.ones((D,), jnp.float32), 'kxln_b': jnp.zeros((D,), jnp.float32), 'wproj': wproj, 'proj_w_scale': wp_s, 'proj_in_scale': jnp.asarray(0.05, jnp.float32), 'proj_smooth': jnp.full((2 * NH * D,), 0.05, jnp.float32)}
    _L1_xattn_all = _L1_xattn_setup()
    _L1_xattn_in = {k: v for k, v in _L1_xattn_all.items() if k in ('ln_w', 'ln_b', 'wq', 'wq_scale', 'q_in_scale', 'wqx', 'wqx_scale', 'qx_in_scale', 'wk', 'wk_scale', 'k_in_scale', 'wv', 'wv_scale', 'v_in_scale', 'w_kv_x', 'qln_w', 'qln_b', 'kln_w', 'kln_b', 'qxln_w', 'qxln_b', 'kxln_w', 'kxln_b', 'wproj', 'proj_w_scale', 'proj_in_scale', 'proj_smooth')}
    del _L1_xattn_all

    def _L1_attn_setup():
        import jax, jax.numpy as jnp
        import numpy as np
        EMBED_DIM = 256
        NUM_HEADS = 16
        HEAD_DIM = EMBED_DIM // NUM_HEADS // 2
        DEPTH = 12
        LAMBDA_INIT = 0.8 - 0.6 * np.exp(-0.3 * DEPTH)
        EPS = 1e-05

        def _attn(q, k, v):
            scale = HEAD_DIM ** (-0.5)
            scores = jnp.einsum('bthd,bshd->bhts', q, k) * scale
            probs = jax.nn.softmax(scores, axis=-1)
            return jnp.einsum('bhts,bshe->bthe', probs, v)
        key = jax.random.key(seed)
        ks = jax.random.split(key, 9)
        B, T = (1, 256)
        scale = 1.0 / np.sqrt(EMBED_DIM)
        return {'x': jax.random.normal(ks[0], (B, T, EMBED_DIM), jnp.float32), 'wq': jax.random.normal(ks[1], (EMBED_DIM, EMBED_DIM), jnp.float32) * scale, 'wk': jax.random.normal(ks[2], (EMBED_DIM, EMBED_DIM), jnp.float32) * scale, 'wv': jax.random.normal(ks[3], (EMBED_DIM, EMBED_DIM), jnp.float32) * scale, 'wo': jax.random.normal(ks[4], (EMBED_DIM, EMBED_DIM), jnp.float32) * scale, 'lambda_q1': jax.random.normal(ks[5], (HEAD_DIM,), jnp.float32) * 0.1, 'lambda_k1': jax.random.normal(ks[6], (HEAD_DIM,), jnp.float32) * 0.1, 'lambda_q2': jax.random.normal(ks[7], (HEAD_DIM,), jnp.float32) * 0.1, 'lambda_k2': jax.random.normal(ks[8], (HEAD_DIM,), jnp.float32) * 0.1, 'subln_w': jnp.ones((2 * HEAD_DIM,), jnp.float32)}
    _L1_attn_all = _L1_attn_setup()
    _L1_attn_in = {k: v for k, v in _L1_attn_all.items() if k in ('wq', 'wk', 'wv', 'wo', 'lambda_q1', 'lambda_k1', 'lambda_q2', 'lambda_k2', 'subln_w')}
    del _L1_attn_all

    def _L1_ffn_setup():
        import jax, jax.numpy as jnp
        import numpy as np
        HIDDEN = 256
        INTER = 1024
        SCALE = 64.0

        def fwht(x):
            orig_shape = x.shape
            n = orig_shape[-1]
            x = x.reshape(-1, n)
            h = 1
            while h < n:
                x = x.reshape(-1, n // (2 * h), 2, h)
                a, b = (x[:, :, 0, :], x[:, :, 1, :])
                x = jnp.stack([a + b, a - b], axis=2).reshape(-1, n)
                h *= 2
            return (x / jnp.sqrt(jnp.asarray(n, x.dtype))).reshape(orig_shape)
        key = jax.random.key(seed)
        ks = jax.random.split(key, 8)
        inp = jax.random.normal(ks[0], (4, 256, HIDDEN), dtype=jnp.float32)
        SU_ug = jnp.where(jax.random.bernoulli(ks[1], 0.5, (HIDDEN,)), 1.0, -1.0).astype(jnp.float32)
        SU_dp = jnp.where(jax.random.bernoulli(ks[2], 0.5, (INTER,)), 1.0, -1.0).astype(jnp.float32)
        Wscale_ug = jax.random.uniform(ks[3], (2 * INTER,), jnp.float32, 0.5, 1.5)
        Wscale_dp = jax.random.uniform(ks[4], (HIDDEN,), jnp.float32, 0.5, 1.5)
        W_up = jax.random.normal(ks[5], (INTER, HIDDEN), dtype=jnp.float32) * 0.02
        W_gate = jax.random.normal(ks[6], (INTER, HIDDEN), dtype=jnp.float32) * 0.02
        W_down = jax.random.normal(ks[7], (HIDDEN, INTER), dtype=jnp.float32) * 0.02
        return {'input': inp, 'SU_ug': SU_ug, 'SU_dp': SU_dp, 'Wscale_ug': Wscale_ug, 'Wscale_dp': Wscale_dp, 'W_up': W_up, 'W_gate': W_gate, 'W_down': W_down}
    _L1_ffn_all = _L1_ffn_setup()
    _L1_ffn_in = {k: v for k, v in _L1_ffn_all.items() if k in ('SU_ug', 'SU_dp', 'Wscale_ug', 'Wscale_dp', 'W_up', 'W_gate', 'W_down')}
    del _L1_ffn_all
    return {'x': x, 'ctx_2048': ctx_2048, 'mask_1xSxS2_ff0': mask_1xSxS2_ff0, 'L0_xattn_Wq': _L0_xattn_in['Wq'], 'L0_xattn_bq': _L0_xattn_in['bq'], 'L0_xattn_Wk': _L0_xattn_in['Wk'], 'L0_xattn_bk': _L0_xattn_in['bk'], 'L0_xattn_Wv': _L0_xattn_in['Wv'], 'L0_xattn_bv': _L0_xattn_in['bv'], 'L0_xattn_Wo': _L0_xattn_in['Wo'], 'L0_xattn_qn_w': _L0_xattn_in['qn_w'], 'L0_xattn_kn_w': _L0_xattn_in['kn_w'], 'L0_attn_Wq': _L0_attn_in['Wq'], 'L0_attn_k_weight': _L0_attn_in['k_weight'], 'L0_attn_v_weight': _L0_attn_in['v_weight'], 'L0_attn_Wg': _L0_attn_in['Wg'], 'L0_attn_Wout': _L0_attn_in['Wout'], 'L0_ffn_gate_w': _L0_ffn_in['gate_w'], 'L0_ffn_w1': _L0_ffn_in['w1'], 'L0_ffn_w2': _L0_ffn_in['w2'], 'L0_ffn_w3': _L0_ffn_in['w3'], 'L0_ffn_ws1': _L0_ffn_in['ws1'], 'L0_ffn_ws2': _L0_ffn_in['ws2'], 'L0_ffn_ws3': _L0_ffn_in['ws3'], 'L1_xattn_ln_w': _L1_xattn_in['ln_w'], 'L1_xattn_ln_b': _L1_xattn_in['ln_b'], 'L1_xattn_wq': _L1_xattn_in['wq'], 'L1_xattn_wq_scale': _L1_xattn_in['wq_scale'], 'L1_xattn_q_in_scale': _L1_xattn_in['q_in_scale'], 'L1_xattn_wqx': _L1_xattn_in['wqx'], 'L1_xattn_wqx_scale': _L1_xattn_in['wqx_scale'], 'L1_xattn_qx_in_scale': _L1_xattn_in['qx_in_scale'], 'L1_xattn_wk': _L1_xattn_in['wk'], 'L1_xattn_wk_scale': _L1_xattn_in['wk_scale'], 'L1_xattn_k_in_scale': _L1_xattn_in['k_in_scale'], 'L1_xattn_wv': _L1_xattn_in['wv'], 'L1_xattn_wv_scale': _L1_xattn_in['wv_scale'], 'L1_xattn_v_in_scale': _L1_xattn_in['v_in_scale'], 'L1_xattn_w_kv_x': _L1_xattn_in['w_kv_x'], 'L1_xattn_qln_w': _L1_xattn_in['qln_w'], 'L1_xattn_qln_b': _L1_xattn_in['qln_b'], 'L1_xattn_kln_w': _L1_xattn_in['kln_w'], 'L1_xattn_kln_b': _L1_xattn_in['kln_b'], 'L1_xattn_qxln_w': _L1_xattn_in['qxln_w'], 'L1_xattn_qxln_b': _L1_xattn_in['qxln_b'], 'L1_xattn_kxln_w': _L1_xattn_in['kxln_w'], 'L1_xattn_kxln_b': _L1_xattn_in['kxln_b'], 'L1_xattn_wproj': _L1_xattn_in['wproj'], 'L1_xattn_proj_w_scale': _L1_xattn_in['proj_w_scale'], 'L1_xattn_proj_in_scale': _L1_xattn_in['proj_in_scale'], 'L1_xattn_proj_smooth': _L1_xattn_in['proj_smooth'], 'L1_attn_wq': _L1_attn_in['wq'], 'L1_attn_wk': _L1_attn_in['wk'], 'L1_attn_wv': _L1_attn_in['wv'], 'L1_attn_wo': _L1_attn_in['wo'], 'L1_attn_lambda_q1': _L1_attn_in['lambda_q1'], 'L1_attn_lambda_k1': _L1_attn_in['lambda_k1'], 'L1_attn_lambda_q2': _L1_attn_in['lambda_q2'], 'L1_attn_lambda_k2': _L1_attn_in['lambda_k2'], 'L1_attn_subln_w': _L1_attn_in['subln_w'], 'L1_ffn_SU_ug': _L1_ffn_in['SU_ug'], 'L1_ffn_SU_dp': _L1_ffn_in['SU_dp'], 'L1_ffn_Wscale_ug': _L1_ffn_in['Wscale_ug'], 'L1_ffn_Wscale_dp': _L1_ffn_in['Wscale_dp'], 'L1_ffn_W_up': _L1_ffn_in['W_up'], 'L1_ffn_W_gate': _L1_ffn_in['W_gate'], 'L1_ffn_W_down': _L1_ffn_in['W_down']}

def reference(x, ctx_2048, mask_1xSxS2_ff0, L0_xattn_Wq, L0_xattn_bq, L0_xattn_Wk, L0_xattn_bk, L0_xattn_Wv, L0_xattn_bv, L0_xattn_Wo, L0_xattn_qn_w, L0_xattn_kn_w, L0_attn_Wq, L0_attn_k_weight, L0_attn_v_weight, L0_attn_Wg, L0_attn_Wout, L0_ffn_gate_w, L0_ffn_w1, L0_ffn_w2, L0_ffn_w3, L0_ffn_ws1, L0_ffn_ws2, L0_ffn_ws3, L1_xattn_ln_w, L1_xattn_ln_b, L1_xattn_wq, L1_xattn_wq_scale, L1_xattn_q_in_scale, L1_xattn_wqx, L1_xattn_wqx_scale, L1_xattn_qx_in_scale, L1_xattn_wk, L1_xattn_wk_scale, L1_xattn_k_in_scale, L1_xattn_wv, L1_xattn_wv_scale, L1_xattn_v_in_scale, L1_xattn_w_kv_x, L1_xattn_qln_w, L1_xattn_qln_b, L1_xattn_kln_w, L1_xattn_kln_b, L1_xattn_qxln_w, L1_xattn_qxln_b, L1_xattn_kxln_w, L1_xattn_kxln_b, L1_xattn_wproj, L1_xattn_proj_w_scale, L1_xattn_proj_in_scale, L1_xattn_proj_smooth, L1_attn_wq, L1_attn_wk, L1_attn_wv, L1_attn_wo, L1_attn_lambda_q1, L1_attn_lambda_k1, L1_attn_lambda_q2, L1_attn_lambda_k2, L1_attn_subln_w, L1_ffn_SU_ug, L1_ffn_SU_dp, L1_ffn_Wscale_ug, L1_ffn_Wscale_dp, L1_ffn_W_up, L1_ffn_W_gate, L1_ffn_W_down):
    import jax
    import jax.numpy as jnp

    def _L0_xattn_ref(hidden_states, encoder_hidden_states, attention_mask, Wq, bq, Wk, bk, Wv, bv, Wo, qn_w, kn_w):
        import jax, jax.numpy as jnp
        import numpy as np
        H = 256
        NH = 16
        NKV = 4
        HD = 128
        GROUPS = NH // NKV
        EPS = 1e-06
        B, S, SE = (1, 256, 512)

        def _rmsnorm(x, w, eps=EPS):
            xf = x.astype(jnp.float32)
            var = jnp.mean(xf * xf, axis=-1, keepdims=True)
            return (xf * jax.lax.rsqrt(var + eps)).astype(x.dtype) * w
        b, s, _ = hidden_states.shape
        se = encoder_hidden_states.shape[1]
        q = (hidden_states @ Wq + bq).reshape(b, s, NH, HD).transpose(0, 2, 1, 3)
        k = (encoder_hidden_states @ Wk + bk).reshape(b, se, NKV, HD).transpose(0, 2, 1, 3)
        v = (encoder_hidden_states @ Wv + bv).reshape(b, se, NKV, HD).transpose(0, 2, 1, 3)
        k = jnp.repeat(k, GROUPS, axis=1)
        v = jnp.repeat(v, GROUPS, axis=1)
        q = _rmsnorm(q, qn_w)
        k = _rmsnorm(k, kn_w)
        scale = 1.0 / np.sqrt(HD).astype(np.float32)
        scores = jnp.einsum('bhsd,bhed->bhse', q, k) * scale
        scores = scores + attention_mask[:, None, :, :]
        probs = jax.nn.softmax(scores.astype(jnp.float32), axis=-1).astype(q.dtype)
        out = jnp.einsum('bhse,bhed->bhsd', probs, v)
        out = out.transpose(0, 2, 1, 3).reshape(b, s, NH * HD)
        return out @ Wo

    def _L0_attn_ref(x, Wq, k_weight, v_weight, Wg, Wout):
        import jax, jax.numpy as jnp
        import numpy as np
        NUM_HEADS = 16
        H = NUM_HEADS
        B, N, E = x.shape
        M = k_weight.shape[0]
        q = jnp.einsum('bne,fe->bnf', x, Wq)
        dk = q.shape[-1] // H
        q = q.reshape(B, N, H, dk).transpose(0, 2, 1, 3)
        k = k_weight.reshape(M, H, dk).transpose(1, 0, 2)
        dv = v_weight.shape[1] // H
        v = v_weight.reshape(M, H, dv).transpose(1, 0, 2)
        scale = jnp.asarray(dk, x.dtype) ** 0.5
        k = k * scale
        v = v * scale
        energy = jax.nn.silu(jnp.einsum('bhnd,hmd->bhnm', q, k))
        out = jnp.einsum('bhnm,hmd->bhnd', energy, v)
        out = out.transpose(0, 2, 1, 3).reshape(B, N, H * dv)
        gate = jax.nn.silu(jnp.einsum('bne,ve->bnv', x, Wg))
        out = out * gate
        return jnp.einsum('bnv,ev->bne', out, Wout)

    def _L0_ffn_ref(x, gate_w, w1, w2, w3, ws1, ws2, ws3):
        import jax, jax.numpy as jnp
        import numpy as np
        B, S, DIM = (2, 256, 256)
        INTER = 128
        E = 8
        K = 2
        N_SHARED = 1
        ROUTE_SCALE = 1.0
        shape = x.shape
        xf = x.reshape(-1, DIM)
        scores = jax.nn.softmax(xf @ gate_w.T, axis=-1)
        weights, idx = jax.lax.top_k(scores, K)
        weights = weights * ROUTE_SCALE
        h = jnp.einsum('td,eid->eti', xf, w1)
        g = jax.nn.silu(h) * jnp.einsum('td,eid->eti', xf, w3)
        eo = jnp.einsum('eti,edi->etd', g, w2)
        comb = jnp.einsum('tke,tk->te', jax.nn.one_hot(idx, E, dtype=xf.dtype), weights)
        y = jnp.einsum('etd,te->td', eo, comb)
        z = jax.nn.silu(xf @ ws1.T) * (xf @ ws3.T) @ ws2.T
        return (y + z).reshape(shape)

    def _L1_xattn_ref(hidden_states, cond, ln_w, ln_b, wq, wq_scale, q_in_scale, wqx, wqx_scale, qx_in_scale, wk, wk_scale, k_in_scale, wv, wv_scale, v_in_scale, w_kv_x, qln_w, qln_b, kln_w, kln_b, qxln_w, qxln_b, kxln_w, kxln_b, wproj, proj_w_scale, proj_in_scale, proj_smooth):
        import jax, jax.numpy as jnp
        import numpy as np
        FP8_MAX = 448.0
        EPS = 1e-05

        def _fp8_roundtrip(x):
            return x.astype(jnp.float8_e4m3fn).astype(jnp.float32)

        def _div_clamp_fp8(x, scale):
            y = jnp.clip(x.astype(jnp.float32) / scale, -FP8_MAX, FP8_MAX)
            y = y.astype(jnp.bfloat16).astype(jnp.float32)
            return _fp8_roundtrip(y)

        def _ln(x, w, b):
            mu = jnp.mean(x, axis=-1, keepdims=True)
            var = jnp.mean(jnp.square(x - mu), axis=-1, keepdims=True)
            return (x - mu) * jax.lax.rsqrt(var + EPS) * w + b

        def _fp8_linear_pertensor(x, wq, w_scale, in_scale):
            xq = _div_clamp_fp8(x, in_scale)
            return jnp.einsum('bsi,oi->bso', xq * in_scale, wq) * w_scale

        def _gqa(q, k, v):
            scale = 1.0 / np.sqrt(q.shape[-1])
            scores = jnp.einsum('bsghd,btgd->bghst', q, k) * scale
            p = jax.nn.softmax(scores, axis=-1)
            return jnp.einsum('bghst,btgd->bsghd', p, v)
        b, s, _ = hidden_states.shape
        sc = cond.shape[1]
        d = qln_w.shape[0]
        nh = wq.shape[0] // d
        g = wk.shape[0] // d
        hpg = nh // g
        ln_out = _ln(hidden_states, ln_w, ln_b)
        q = _fp8_linear_pertensor(ln_out, wq, wq_scale, q_in_scale).reshape(b, s, g, hpg, d)
        q = _ln(q, qln_w, qln_b)
        k = _fp8_linear_pertensor(ln_out, wk, wk_scale, k_in_scale).reshape(b, s, g, d)
        k = _ln(k, kln_w, kln_b)
        v = _fp8_linear_pertensor(ln_out, wv, wv_scale, v_in_scale).reshape(b, s, g, d)
        core = _gqa(q, k, v).reshape(b, s, nh * d)
        qx = _fp8_linear_pertensor(ln_out, wqx, wqx_scale, qx_in_scale).reshape(b, s, g, hpg, d)
        qx = _ln(qx, qxln_w, qxln_b)
        kvx = jnp.einsum('bsi,oi->bso', cond, w_kv_x)
        kx, vx = jnp.split(kvx, 2, axis=-1)
        kx = _ln(kx.reshape(b, sc, g, d), kxln_w, kxln_b)
        vx = vx.reshape(b, sc, g, d)
        xout = _gqa(qx, kx, vx).reshape(b, s, nh * d)
        cat = jnp.concatenate([core, xout], axis=-1)
        catq = _div_clamp_fp8(cat, proj_smooth)
        return jnp.einsum('bsi,oi->bso', catq, wproj) * (proj_in_scale * proj_w_scale)

    def _L1_attn_ref(x, wq, wk, wv, wo, lambda_q1, lambda_k1, lambda_q2, lambda_k2, subln_w):
        import jax, jax.numpy as jnp
        import numpy as np
        EMBED_DIM = 256
        NUM_HEADS = 16
        HEAD_DIM = EMBED_DIM // NUM_HEADS // 2
        DEPTH = 12
        LAMBDA_INIT = 0.8 - 0.6 * np.exp(-0.3 * DEPTH)
        EPS = 1e-05

        def _attn(q, k, v):
            scale = HEAD_DIM ** (-0.5)
            scores = jnp.einsum('bthd,bshd->bhts', q, k) * scale
            probs = jax.nn.softmax(scores, axis=-1)
            return jnp.einsum('bhts,bshe->bthe', probs, v)
        b, t, _ = x.shape
        q = (x @ wq.T).reshape(b, t, NUM_HEADS, 2, HEAD_DIM)
        k = (x @ wk.T).reshape(b, t, NUM_HEADS, 2, HEAD_DIM)
        v = (x @ wv.T).reshape(b, t, NUM_HEADS, 2 * HEAD_DIM)
        q1, q2 = (q[:, :, :, 0], q[:, :, :, 1])
        k1, k2 = (k[:, :, :, 0], k[:, :, :, 1])
        attn1 = _attn(q1, k1, v)
        attn2 = _attn(q2, k2, v)
        lam1 = jnp.exp(jnp.sum(lambda_q1 * lambda_k1))
        lam2 = jnp.exp(jnp.sum(lambda_q2 * lambda_k2))
        lambda_full = lam1 - lam2 + LAMBDA_INIT
        attn = attn1 - lambda_full * attn2
        rms = jax.lax.rsqrt(jnp.mean(attn * attn, axis=-1, keepdims=True) + EPS)
        attn = attn * rms * subln_w
        attn = attn * (1.0 - LAMBDA_INIT)
        attn = attn.reshape(b, t, NUM_HEADS * 2 * HEAD_DIM)
        return attn @ wo.T

    def _L1_ffn_ref(input, SU_ug, SU_dp, Wscale_ug, Wscale_dp, W_up, W_gate, W_down):
        import jax, jax.numpy as jnp
        import numpy as np
        HIDDEN = 256
        INTER = 1024
        SCALE = 64.0

        def fwht(x):
            orig_shape = x.shape
            n = orig_shape[-1]
            x = x.reshape(-1, n)
            h = 1
            while h < n:
                x = x.reshape(-1, n // (2 * h), 2, h)
                a, b = (x[:, :, 0, :], x[:, :, 1, :])
                x = jnp.stack([a + b, a - b], axis=2).reshape(-1, n)
                h *= 2
            return (x / jnp.sqrt(jnp.asarray(n, x.dtype))).reshape(orig_shape)
        n = SU_ug.shape[0]
        x = input.reshape(-1, n)
        x = fwht(x * SU_ug) / SCALE
        x_up = x @ W_up.T * (Wscale_ug[:INTER] * SCALE)
        x_gate = x @ W_gate.T * (Wscale_ug[INTER:] * SCALE)
        x = jax.nn.silu(x_gate) * x_up
        x = fwht(x * SU_dp) / SCALE
        x = x @ W_down.T * (Wscale_dp * SCALE)
        return x.reshape(input.shape)
    x = x + _L0_xattn_ref(_layernorm(x, axis=-1), ctx_2048, mask_1xSxS2_ff0, L0_xattn_Wq, L0_xattn_bq, L0_xattn_Wk, L0_xattn_bk, L0_xattn_Wv, L0_xattn_bv, L0_xattn_Wo, L0_xattn_qn_w, L0_xattn_kn_w)
    x = x + _L0_attn_ref(_layernorm(x, axis=-1), L0_attn_Wq, L0_attn_k_weight, L0_attn_v_weight, L0_attn_Wg, L0_attn_Wout)
    x = x + _L0_ffn_ref(_layernorm(x, axis=-1), L0_ffn_gate_w, L0_ffn_w1, L0_ffn_w2, L0_ffn_w3, L0_ffn_ws1, L0_ffn_ws2, L0_ffn_ws3)
    x = x + _L1_xattn_ref(_layernorm(x, axis=-1), ctx_2048, L1_xattn_ln_w, L1_xattn_ln_b, L1_xattn_wq, L1_xattn_wq_scale, L1_xattn_q_in_scale, L1_xattn_wqx, L1_xattn_wqx_scale, L1_xattn_qx_in_scale, L1_xattn_wk, L1_xattn_wk_scale, L1_xattn_k_in_scale, L1_xattn_wv, L1_xattn_wv_scale, L1_xattn_v_in_scale, L1_xattn_w_kv_x, L1_xattn_qln_w, L1_xattn_qln_b, L1_xattn_kln_w, L1_xattn_kln_b, L1_xattn_qxln_w, L1_xattn_qxln_b, L1_xattn_kxln_w, L1_xattn_kxln_b, L1_xattn_wproj, L1_xattn_proj_w_scale, L1_xattn_proj_in_scale, L1_xattn_proj_smooth)
    x = x + _L1_attn_ref(_layernorm(x, axis=-1), L1_attn_wq, L1_attn_wk, L1_attn_wv, L1_attn_wo, L1_attn_lambda_q1, L1_attn_lambda_k1, L1_attn_lambda_q2, L1_attn_lambda_k2, L1_attn_subln_w)
    x = x + _L1_ffn_ref(_layernorm(x, axis=-1), L1_ffn_SU_ug, L1_ffn_SU_dp, L1_ffn_Wscale_ug, L1_ffn_Wscale_dp, L1_ffn_W_up, L1_ffn_W_gate, L1_ffn_W_down)
    return x

_drawn_inputs = setup_inputs


def setup_inputs(seed=0):
    import zlib

    import numpy as np

    out = dict(_drawn_inputs(seed))
    spreads = {'L0_xattn_qn_w': (1.0, 0.6),
     'L0_xattn_kn_w': (1.0, 0.6),
     'L1_xattn_ln_w': (1.0, 0.595),
     'L1_xattn_ln_b': (0.0, 0.294),
     'L1_xattn_q_in_scale': (0.05000000074505806, 0.6),
     'L1_xattn_qx_in_scale': (0.05000000074505806, 0.6),
     'L1_xattn_k_in_scale': (0.05000000074505806, 0.6),
     'L1_xattn_v_in_scale': (0.05000000074505806, 0.6),
     'L1_xattn_qln_w': (1.0, 0.6),
     'L1_xattn_qln_b': (0.0, 0.8),
     'L1_xattn_kln_w': (1.0, 0.6),
     'L1_xattn_kln_b': (0.0, 2.0),
     'L1_xattn_qxln_w': (1.0, 0.6),
     'L1_xattn_qxln_b': (0.0, 0.8),
     'L1_xattn_kxln_w': (1.0, 0.6),
     'L1_xattn_kxln_b': (0.0, 2.0),
     'L1_xattn_proj_smooth': (0.05000000074505806, 0.2),
     'L1_attn_subln_w': (1.0, 0.584)}
    factors = {'L0_xattn_bq': 6.291,
     'L0_xattn_bk': 8.0,
     'L1_attn_lambda_q1': 8.0,
     'L1_attn_lambda_k1': 8.0,
     'L1_attn_lambda_q2': 38.412,
     'L1_attn_lambda_k2': 26.497,
     'L1_ffn_Wscale_ug': 4.916,
     'L1_ffn_Wscale_dp': 6.8}
    for name, (base, spread) in spreads.items():
        noise = np.random.default_rng([zlib.crc32(name.encode()), seed]).standard_normal(out[name].shape)
        drawn = base * np.exp(spread * noise) if base else spread * noise
        out[name] = jnp.asarray(drawn.astype(out[name].dtype))
    for name, factor in factors.items():
        out[name] = (out[name] * factor).astype(out[name].dtype)
    return out
```

```python
import math
from contextlib import ExitStack

import concourse.bass as bass
from concourse import mybir

F32 = mybir.dt.float32
BF16 = mybir.dt.bfloat16
U16 = mybir.dt.uint16
U32 = mybir.dt.uint32
I32 = mybir.dt.int32
ALU = mybir.AluOpType
ACT = mybir.ActivationFunctionType
AX = mybir.AxisListType

P = 128
H = 256
HC = H // P
S = 32
SE = 257
BT = P // S
HD = 128
NH = 16
UNITS = NH // 4
EXPLN = "natural_log_exp_and_others"
FP8_MAX = 448.0
FP8_SMALLEST = 2.0 ** -6
FP8_ROUND = 1.5 * 2.0 ** 20


class Part(ExitStack):

    def __init__(self, nc):
        super().__init__()
        self.nc, self.sems = nc, []

    def semaphore(self, name):
        self.sems.append(self.enter_context(self.nc.semaphore(name)))
        return self.sems[-1]

    def open_block(self):
        self.callback(self.clear)
        return self.enter_context(self.nc.Block())

    def clear(self):
        with self.nc.Block() as block:
            @block.gpsimd
            def _(pool):
                for s in self.sems:
                    pool.sem_clear(s)


class Signal:

    def __init__(self, ctx, nc, name, per, unit=1):
        self.sem = ctx.semaphore(name)
        self.per, self.unit, self.name = per, unit, name

    def prime(self, eng):
        eng.sem_inc(self.sem, self.per * self.unit)

    def now(self, i, k):
        assert 1 <= k <= self.per, (self.name, k, self.per)
        return i * (self.per * self.unit) + (self.per + k) * self.unit

    def before(self, i, k):
        assert 1 <= k <= self.per, (self.name, k, self.per)
        return i * (self.per * self.unit) + k * self.unit

    def after(self, i, k):
        return self.now(i, k) if k >= 1 else self.before(i, k + self.per)


class Chain(Signal):

    k = 0

    def next(self, i):
        self.k += 1
        return self.now(i, self.k)

    def done(self):
        assert self.k == self.per, (self.name, self.k)


def cross_attention(nc, d, X, Yc, ident, layer, tiles):
    L1 = layer == 1
    G = 8 if L1 else 4
    GU = G // UNITS
    SUBS = UNITS * BT * GU
    NU = UNITS * BT
    KW = SE + 1 if L1 else SE
    MG = P // GU
    SCALE = HD ** -0.5
    EPS = 1e-5 if L1 else 1e-6
    CW = [P, P, SE - 2 * P]
    n = f"x{layer}_"

    with Part(nc) as ctx:
        def sb(name, shape, dt=F32):
            return ctx.enter_context(nc.sbuf_tensor(n + name, shape, dt))

        def bank(name):
            return ctx.enter_context(nc.psum_tensor(n + name, [P, 512], F32))

        def sig(name, per, unit=1):
            return Signal(ctx, nc, n + name, per, unit)

        wq = sb("wq", [P, HC, NH * HD])
        wk = sb("wk", [P, HC, G * HD])
        wv = sb("wv", [P, HC, G * HD])
        wo = sb("wo", [P, NH, H])
        ones = sb("ones", [P, P])
        eps_ln = sb("eps_ln", [P, 1])
        eps_h = sb("eps_h", [P, 1])
        qscale = sb("qscale", [P, 1])
        if L1:
            vecs = sb("vecs", [P, 24])
            inv_in = sb("inv_in", [P, HC])
            smooth = sb("smooth", [P, NH])
            inv_sm = sb("inv_sm", [P, NH])
            qbias = sb("qbias", [P, 1])
            wmean = sb("wmean", [P, HC, NH])
            yscale = sb("yscale", [P, 1])
            lnT = sb("lnT", [P, HC, P])
        else:
            bq = sb("bq", [P, NH * HD])
            bkv = sb("bkv", [P, 2, G])
            nw = sb("nw", [P, 2])
            mask = sb("mask", [P, SE])
        stats = sb("stats", [P, 6])
        mv = sb("mv", [P, 2])
        lr = sb("lr", [P, 1])
        xn = sb("xn", [P, H])
        xnT = sb("xnT", [P, HC, P])
        qn = sb("qn", [P, NH, HD])
        qsq = sb("qsq", [P, 4, HD])
        qss = sb("qss", [P, NH])
        qr = sb("qr", [P, NH])
        qTn = sb("qTn", [P, BT, NH, S])
        qT = sb("qT", [P, BT, NH, S])
        cn = sb("cn", [P, BT, 3, H])
        cT = sb("cT", [P, 2, HC, SE])
        sq = sb("sq", [P, 2 * GU, SE])
        rs = sb("rs", [P, 2 * GU, SE])
        kT = sb("kT", [P, 4, GU, KW])
        pr = sb("pr", [P, 4, SE])
        top = sb("top", [P, NU])
        ntop = sb("ntop", [P, NU])
        ps = sb("ps", [P, NU])
        rps = sb("rps", [P, NU])
        pT = sb("pT", [P, 2, 3, UNITS * P])
        pcT = sb("pcT", [P, HC, UNITS * P])
        oT = sb("oT", [P, NH, P])
        if L1:
            qa = sb("qa", [P, NH * S])
            qb = sb("qb", [P, NH * S], BF16)
            qe = sb("qe", [P, NH * S], BF16)
            qm = sb("qm", [P, NH * S])
            ysum = sb("ysum", [P, H])
        else:
            sm = sb("sm", [P, 2, SE])

        Kb = [bank("Kb0"), bank("Kb1")]
        SSb = bank("SSb")
        Sb = bank("Sb")
        PTb = bank("PTb")
        Lb = bank("Lb")
        PC = [bank("PC0"), bank("PC1")]
        QB = [PC[1], PC[0], PC[1], PC[0]]
        TB = [PC[1], PC[1], PC[0], PC[1]]

        weights = ctx.semaphore(n + "weights")
        ready = ctx.semaphore(n + "constants_ready")
        setup = ctx.semaphore(n + "setup_steps")
        gate = ctx.semaphore(n + "gate")
        ctx_in = [sig(f"context_loaded{b}", 1, 16 * 2) for b in range(BT)]
        NLN = 2 if L1 else 1
        ln_sum = sig("ln_stats", NLN)
        ln_agg = sig("ln_aggregated", NLN)
        ln_log = sig("ln_log", NLN)
        ln_rs = sig("ln_rsqrt", NLN)
        x_mid = sig("x_normed_once", 1)
        xn_done = sig("xn_done", 1)
        xt_done = sig("xt_transposed", 1)
        xt_copied = sig("xt_copied", 1)
        xq_steps = sig("x_quantise_steps", 7)
        xq_done = sig("xq_done", 1)
        q_done = sig("q_projected", 4)
        q_in = sig("q_copied", 4)
        q_sq = sig("q_squared", 4)
        q_sum = sig("q_summed", 4)
        q_log = sig("q_log", 4)
        q_rs = sig("q_rsqrt", 4)
        qn_done = sig("q_normed", 4)
        qt_done = sig("q_transposed", 4)
        qt_copied = sig("qTn_copied", 4)
        qT_ready = sig("qT_ready", BT)
        ct_done = sig("ctx_transposed", BT)
        ct_copied = sig("ctxT_copied", BT)
        k_done = sig("k_projected", SUBS)
        k_sq = sig("k_squared", SUBS)
        k_raw = sig("k_copied", SUBS)
        ss_done = sig("k_summed", SUBS)
        k_log = sig("k_log", SUBS)
        k_rs = sig("k_rsqrt", SUBS)
        kt_done = sig("kT_normed", SUBS)
        s_done = sig("scores_done", NU)
        top_found = sig("max_found", NU)
        top_done = sig("max_negated", NU)
        e_done = sig("exp_done", NU)
        r_done = sig("sum_inverted", NU)
        pn_done = sig("probs_normed", NU)
        pt_done = sig("probs_transposed", NU)
        pt_copied = sig("pT_copied", NU)
        pl_copied = sig("pT_last_copied", BT)
        pc_done = sig("pc_done", BT * HC)
        pc_copied = sig("pcT_copied", BT * HC)
        o_done = sig("out_heads_done", BT)
        o_read = sig("out_heads_read", BT)
        oq_steps = sig("out_quantise_steps", 4 * BT)
        o_copied = sig("oT_copied", BT)
        y_done = sig("y_done", 1)
        y_summed = sig("y_summed", 1)
        x_added = sig("x_added", 1)

        def lagging(i, u, lag, cur, prev):
            if u >= lag:
                return [(i, u - lag)] if cur and u - lag < NU else []
            return [(i - 1, u - lag + NU)] if prev else []

        def batch_at(i, u, lag, cur, prev):
            if u % UNITS != lag % UNITS:
                return []
            if u >= lag:
                return [(i, (u - lag) // UNITS)] if cur else []
            return [(i - 1, (u - lag) // UNITS + BT)] if prev else []

        def run(eng, tile):
            tile(0, True, False, True)
            with eng.Fori(1, tiles - 1) as i:
                tile(i, True, True, True)
            tile(tiles - 1, True, True, False)
            tile(tiles, False, True, False)

        def steps(cur):
            return range(NU if cur else 8)

        block = ctx.open_block()

        @block.sync
        def _(sp):
            loads = [(wq, d["wq"].rearrange("(c p) n -> p c n", p=P)),
                     (wk, d["wk"].rearrange("(c p) n -> p c n", p=P)),
                     (wv, d["wv"].rearrange("(c p) n -> p c n", p=P)),
                     (wo, d["wo"].rearrange("(h p) n -> p h n", p=P))]
            if L1:
                loads += [(vecs, d["vecs"]), (smooth, d["smooth"])]
            else:
                loads += [(bq, d["bq"]), (bkv, d["bkv"]), (nw, d["nw"]), (mask, d["mask"])]
            for dst, src in loads:
                sp.dma_start(dst[:], src).then_inc(weights, 16)
            for s in ctx_in:
                s.prime(sp)
            with sp.Fori(0, tiles) as i:
                for b in range(BT):
                    sp.wait_ge(pc_done.sem, pc_done.before(i, HC * (b + 1)))
                    src = d["ctx"][i * BT + b]
                    sp.dma_start(cn[:, b, 0:2, :], src[0:2 * P, :].rearrange("(c p) n -> p c n", p=P)
                                 ).then_inc(ctx_in[b].sem, 16)
                    sp.dma_start(cn[0:1, b, 2, :], src[2 * P:SE, :]).then_inc(ctx_in[b].sem, 16)

        NLOADS = 6 if L1 else 8

        @block.tensor
        def _(pe):
            for s in (xt_done, q_done, qt_done, ct_done, k_done, ss_done, s_done, pt_done, pc_done, o_done, y_done):
                s.prime(pe)
            pe.wait_ge(weights, 16 * NLOADS)
            pe.wait_ge(ready, 1)

            def transpose_tokens(t):
                pe.wait_ge(xn_done.sem, xn_done.now(t, 1))
                for c in range(HC):
                    m = pe.transpose(PC[1][:, c * P:(c + 1) * P], xn[:, c * P:(c + 1) * P], ident[:])
                m.then_inc(xt_done.sem, 1)

            def project_query(t, k):
                if k == 0:
                    x_ready = xq_done if L1 else xt_copied
                    pe.wait_ge(x_ready.sem, x_ready.now(t, 1))
                if k >= 2:
                    pe.wait_ge(q_in.sem, q_in.now(t, k - 1))
                for c in range(HC):
                    m = pe.matmul(QB[k][:, :], xnT[:, c, :], wq[:, c, k * 512:(k + 1) * 512],
                                  start=c == 0, stop=c == HC - 1)
                m.then_inc(q_done.sem, 1)

            def transpose_query(t, k):
                pe.wait_ge(qn_done.sem, qn_done.now(t, k + 1))
                pe.wait_ge(q_in.sem, q_in.now(t, 3 if k < 2 else 4))
                if k in (1, 3):
                    pe.wait_ge(qt_copied.sem, qt_copied.now(t, k // 2 + 1))
                for h in range(4):
                    m = pe.transpose(TB[k][:, h * P:(h + 1) * P], qn[:, 4 * k + h, :], ident[:])
                m.then_inc(qt_done.sem, 1)

            def transpose_context(t, b):
                pe.wait_ge(ctx_in[b].sem, ctx_in[b].now(t, 1))
                for h in range(HC):
                    for c in range(3):
                        m = pe.transpose(PC[h][:, c * P:c * P + CW[c]], cn[0:CW[c], b, c, h * P:(h + 1) * P],
                                         ident[0:CW[c], 0:CW[c]])
                m.then_inc(ct_done.sem, 1)

            def project_key(t, j):
                b, g = j // G, j % G
                if g == 0:
                    pe.wait_ge(ct_copied.sem, ct_copied.now(t, b + 1))
                pe.wait_ge(k_sq.sem, k_sq.after(t, j - 1))
                for c in range(HC):
                    m = pe.matmul(Kb[j % 2][:, 0:SE], wk[:, c, g * HD:(g + 1) * HD], cT[:, b % 2, c, :],
                                  start=c == 0, stop=c == HC - 1)
                m.then_inc(k_done.sem, 1)

            def sum_squares(t, j):
                pe.wait_ge(k_sq.sem, k_sq.now(t, j + 1))
                pe.wait_ge(k_log.sem, k_log.after(t, j))
                pe.matmul(SSb[:, 0:SE], ones[:], sq[:, j % (2 * GU), :], start=True, stop=True
                          ).then_inc(ss_done.sem, 1)

            def scores(t, u):
                b, h = u // UNITS, 4 * (u % UNITS)
                if u % UNITS == 0:
                    pe.wait_ge(qT_ready.sem, qT_ready.now(t, b + 1))
                s_read = e_done if L1 else top_done
                pe.wait_ge(s_read.sem, s_read.after(t, u))
                pe.wait_ge(kt_done.sem, kt_done.now(t, GU * (u + 1)))
                for g in range(GU):
                    q = qT[:, b, h + g * 4 // GU:h + (g + 1) * 4 // GU, :].rearrange("p h q -> p (h q)")
                    m = pe.matmul(Sb[g * MG:(g + 1) * MG, 0:KW], q, kT[:, u % 4, g, :], start=True, stop=True)
                m.then_inc(s_done.sem, 1)

            def transpose_probs(t, u):
                b, v = u // UNITS, u % UNITS
                pe.wait_ge(pn_done.sem, pn_done.now(t, u + 1))
                pe.wait_ge(pt_copied.sem, pt_copied.after(t, u))
                if v == 0:
                    pe.wait_ge(pl_copied.sem, pl_copied.after(t, b))
                for c in range(2):
                    pe.transpose(PTb[:, c * P:(c + 1) * P], pr[:, u % 4, c * P:(c + 1) * P], ident[:])
                pe.transpose(Lb[0:CW[2], v * P:(v + 1) * P], pr[:, u % 4, 2 * P:SE], ident[:]
                             ).then_inc(pt_done.sem, 1)

            def weigh_context(t, b):
                pe.wait_ge(pt_copied.sem, pt_copied.now(t, UNITS * (b + 1)))
                pe.wait_ge(pl_copied.sem, pl_copied.now(t, b + 1))
                pe.wait_ge(o_copied.sem, o_copied.after(t, b))
                for h in range(HC):
                    for c in range(3):
                        m = pe.matmul(PC[h][:, :], cn[0:CW[c], b, c, h * P:(h + 1) * P],
                                      pT[0:CW[c], b % 2, c, :], start=c == 0, stop=c == 2)
                    m.then_inc(pc_done.sem, 1)

            def project_values(t, b):
                pe.wait_ge(pc_copied.sem, pc_copied.now(t, HC * (b + 1)))
                for g in range(G):
                    w = UNITS * P // G
                    for c in range(HC):
                        m = pe.matmul(PC[0][:, g * w:(g + 1) * w], wv[:, c, g * HD:(g + 1) * HD],
                                      pcT[:, c, g * w:(g + 1) * w], start=c == 0, stop=c == HC - 1)
                m.then_inc(o_done.sem, 1)

            def project_out(t):
                pe.wait_ge(o_copied.sem, o_copied.now(t, BT))
                for h in range(NH):
                    m = pe.matmul(PC[1][:, 0:H], oT[:, h, :], wo[:, h, :], start=h == 0, stop=h == NH - 1)
                m.then_inc(y_done.sem, 1)

            def tile(i, cur, prev, nxt):
                for u in steps(cur):
                    for g in range(GU):
                        if cur:
                            project_key(i, GU * u + g)
                        for t, v in lagging(i, u, 1, cur, prev):
                            sum_squares(t, GU * v + g)
                    for t, v in lagging(i, u, 2, cur, prev):
                        scores(t, v)
                    for t, v in lagging(i, u, 4, cur, prev):
                        transpose_probs(t, v)
                    for t, b in batch_at(i, u, 8, cur, prev):
                        weigh_context(t, b)
                    for t, b in batch_at(i, u, 9, cur, prev):
                        project_values(t, b)
                    if u == 1 and nxt:
                        transpose_tokens(i + 1)
                    if u == 3 and cur:
                        if prev:
                            pe.wait_ge(o_copied.sem, o_copied.now(i - 1, 3))
                        if nxt:
                            pe.wait_ge(xt_copied.sem, xt_copied.now(i + 1, 1))
                        transpose_context(i, 1)
                    if u == 5 and nxt:
                        project_query(i + 1, 0)
                    if u == 6 and nxt:
                        if prev:
                            pe.wait_ge(o_copied.sem, o_copied.now(i - 1, 4))
                        project_query(i + 1, 1)
                    if u == 6 and prev:
                        if nxt:
                            pe.wait_ge(q_in.sem, q_in.now(i + 1, 1))
                        project_out(i - 1)
                    if u == 7 and cur:
                        if nxt:
                            pe.wait_ge(q_in.sem, q_in.now(i + 1, 2))
                        if prev:
                            pe.wait_ge(x_added.sem, x_added.now(i - 1, 1))
                        transpose_context(i, 2)
                    if u == 9 and nxt:
                        project_query(i + 1, 2)
                    if u == 10 and nxt:
                        pe.wait_ge(o_copied.sem, o_copied.now(i, 1))
                        project_query(i + 1, 3)
                        transpose_query(i + 1, 0)
                    if u == 11 and cur:
                        if nxt:
                            pe.wait_ge(q_in.sem, q_in.now(i + 1, 4))
                            pe.wait_ge(qt_copied.sem, qt_copied.now(i + 1, 1))
                        pe.wait_ge(o_copied.sem, o_copied.now(i, 1))
                        transpose_context(i, 3)
                    if u == 13 and nxt:
                        transpose_query(i + 1, 1)
                    if u == 14 and nxt:
                        pe.wait_ge(o_copied.sem, o_copied.now(i, 2))
                        transpose_query(i + 1, 2)
                        transpose_query(i + 1, 3)
                    if u == 15 and nxt:
                        pe.wait_ge(qt_copied.sem, qt_copied.now(i + 1, 4))
                        transpose_context(i + 1, 0)

            transpose_tokens(0)
            for k in range(4):
                project_query(0, k)
            for k in range(4):
                transpose_query(0, k)
            pe.wait_ge(qt_copied.sem, qt_copied.now(0, 4))
            transpose_context(0, 0)
            run(pe, tile)

        @block.scalar
        def _(act):
            for s in (xt_copied, q_sq, q_log, q_rs, qt_copied, ct_copied, k_sq, k_log, k_rs, e_done, ln_log, ln_rs):
                s.prime(act)
            act.preload_act_table_set(EXPLN)
            act.wait_ge(ready, 1)

            def rsqrt_tokens(t, k):
                act.wait_ge(ln_agg.sem, ln_agg.now(t, k + 1))
                act.activation(lr[:], mv[:, 1:2], ACT.Ln, bias=eps_ln[:]).then_inc(ln_log.sem, 1)
                act.wait_ge(ln_log.sem, ln_log.now(t, k + 1))
                act.activation(lr[:], lr[:], ACT.Exp, scale=-0.5).then_inc(ln_rs.sem, 1)

            def copy_tokens(t):
                act.wait_ge(xt_done.sem, xt_done.now(t, 1))
                if L1:
                    act.wait_ge(xq_done.sem, xq_done.before(t, 1))
                else:
                    act.wait_ge(q_done.sem, q_done.before(t, 4))
                act.activation((lnT if L1 else xnT)[:], PC[1][:, 0:H].rearrange("p (c t) -> p c t", c=HC), ACT.Copy
                               ).then_inc(xt_copied.sem, 1)

            def square_query(t, k):
                act.wait_ge(q_in.sem, q_in.now(t, k + 1))
                act.wait_ge(q_sum.sem, q_sum.after(t, k))
                act.activation(qsq[:], qn[:, 4 * k:4 * k + 4, :], ACT.Square).then_inc(q_sq.sem, 1)

            def rsqrt_query(t, k):
                hs = slice(4 * k, 4 * k + 4)
                act.wait_ge(q_sum.sem, q_sum.now(t, k + 1))
                act.activation(qr[:, hs], qss[:, hs], ACT.Ln, bias=eps_h[:], scale=1.0 / HD).then_inc(q_log.sem, 1)
                act.wait_ge(q_log.sem, q_log.now(t, k + 1))
                act.activation(qr[:, hs], qr[:, hs], ACT.Exp, scale=-0.5).then_inc(q_rs.sem, 1)

            def copy_query(t, k):
                act.wait_ge(qt_done.sem, qt_done.now(t, k + 1))
                act.wait_ge(qT_ready.sem, qT_ready.before(t, BT))
                src = TB[k][:, :].rearrange("p (h b q) -> p h b q", h=4, b=BT)
                dst = qTn[:, :, 4 * k:4 * k + 4, :].rearrange("p b h q -> p h b q")
                if L1:
                    act.activation(dst, src, ACT.Identity, scale=qscale[:], bias=qbias[:]).then_inc(qt_copied.sem, 1)
                else:
                    act.activation(dst, src, ACT.Copy, scale=qscale[:]).then_inc(qt_copied.sem, 1)

            def copy_context(t, b):
                act.wait_ge(ct_done.sem, ct_done.now(t, b + 1))
                act.wait_ge(k_done.sem, k_done.after(t, G * (b - 1)))
                act.activation(cT[:, b % 2, 0, :], PC[0][:, 0:SE], ACT.Copy)
                act.activation(cT[:, b % 2, 1, :], PC[1][:, 0:SE], ACT.Copy).then_inc(ct_copied.sem, 1)

            def square_key(t, j):
                act.wait_ge(k_raw.sem, k_raw.now(t, j + 1))
                act.wait_ge(ss_done.sem, ss_done.after(t, j + 1 - 2 * GU))
                dst = sq[:, j % (2 * GU), :]
                if L1:
                    act.activation(dst, Kb[j % 2][:, 0:SE], ACT.Square).then_inc(k_sq.sem, 1)
                else:
                    act.activation(dst, Kb[j % 2][:, 0:SE], ACT.Square, bias=bkv[:, 0, j % G:j % G + 1]
                                   ).then_inc(k_sq.sem, 1)

            def rsqrt_key(t, j):
                r = rs[:, j % (2 * GU), :]
                act.wait_ge(ss_done.sem, ss_done.now(t, j + 1))
                act.wait_ge(kt_done.sem, kt_done.after(t, j + 1 - 2 * GU))
                act.activation(r, SSb[:, 0:SE], ACT.Ln, bias=eps_h[:]).then_inc(k_log.sem, 1)
                act.wait_ge(k_log.sem, k_log.now(t, j + 1))
                act.activation(r, r, ACT.Exp, scale=-0.5).then_inc(k_rs.sem, 1)

            def exp_scores(t, u):
                act.wait_ge(top_done.sem, top_done.now(t, u + 1))
                act.wait_ge(pt_done.sem, pt_done.after(t, u - 3))
                src = Sb[:, 0:SE] if L1 else sm[:, u % 2, :]
                act.activation(pr[:, u % 4, :], src, ACT.Exp, bias=ntop[:, u:u + 1],
                               accum_out=ps[:, u:u + 1]).then_inc(e_done.sem, 1)

            def tile(i, cur, prev, nxt):
                for u in steps(cur):
                    if u == 1 and nxt and L1:
                        rsqrt_tokens(i + 1, 1)
                    for g in range(GU):
                        if cur:
                            square_key(i, GU * u + g)
                        for t, v in lagging(i, u, 1, cur, prev):
                            rsqrt_key(t, GU * v + g)
                    for t, v in lagging(i, u, 2, cur, prev):
                        exp_scores(t, v)
                    if u == 0 and nxt:
                        rsqrt_tokens(i + 1, 0)
                    if u == 1 and nxt:
                        copy_tokens(i + 1)
                    if u in (3, 7, 11) and cur:
                        copy_context(i, u // 4 + 1)
                    if u in (5, 6, 9, 10) and nxt:
                        square_query(i + 1, {5: 0, 6: 1, 9: 2, 10: 3}[u])
                    if u in (6, 7, 10, 11) and nxt:
                        rsqrt_query(i + 1, {6: 0, 7: 1, 10: 2, 11: 3}[u])
                    if u == 10 and nxt:
                        copy_query(i + 1, 0)
                    if u == 13 and nxt:
                        copy_query(i + 1, 1)
                    if u == 14 and nxt:
                        copy_query(i + 1, 2)
                        copy_query(i + 1, 3)
                    if u == 15 and nxt:
                        copy_context(i + 1, 0)

            for k in range(NLN):
                rsqrt_tokens(0, k)
            copy_tokens(0)
            for k in range(4):
                square_query(0, k)
                rsqrt_query(0, k)
            for k in range(4):
                copy_query(0, k)
            copy_context(0, 0)
            run(act, tile)

        @block.gpsimd
        def _(pool):
            for s in (kt_done, qT_ready):
                s.prime(pool)
            pool.wait_ge(ready, 1)

            def norm_key(t, j):
                k = kT[:, j // GU % 4, j % GU, 0:SE]
                pool.wait_ge(k_raw.sem, k_raw.now(t, j + 1))
                pool.wait_ge(k_rs.sem, k_rs.now(t, j + 1))
                pool.tensor_tensor(k, k, rs[:, j % (2 * GU), :], ALU.mult).then_inc(kt_done.sem, 1)

            def queries_of_batch(t, b):
                pool.wait_ge(qt_copied.sem, qt_copied.now(t, 4))
                pool.wait_ge(s_done.sem, s_done.before(t, UNITS * (b + 1)))
                pool.sem_inc(gate, 1)
                pool.tensor_copy(qT[:, b, :, :], qTn[:, b, :, :]).then_inc(qT_ready.sem, 1)

            def tile(i, cur, prev, nxt):
                for u in steps(cur):
                    for t, v in lagging(i, u, 1, cur, prev):
                        for g in range(GU):
                            norm_key(t, GU * v + g)
                    if u == 2 and cur:
                        queries_of_batch(i, 3)
                    if u == 15 and nxt:
                        for b in range(3):
                            queries_of_batch(i + 1, b)

            for b in range(3):
                queries_of_batch(0, b)
            run(pool, tile)

        @block.vector
        def _(dve):
            for s in (xn_done, xq_done, q_in, q_sum, qn_done, k_raw, top_found, top_done, r_done, pn_done, pt_copied,
                      pl_copied, pc_copied, o_read, oq_steps, o_copied, y_summed, x_added, ln_sum, ln_agg, x_mid,
                      xq_steps):
                s.prime(dve)
            dve.memset(ones[:], 1.0 / HD)
            dve.memset(eps_ln[:], 1e-5)
            dve.memset(eps_h[:], EPS)
            dve.wait_ge(weights, 16 * NLOADS)
            step = [0]

            def then(ins):
                step[0] += 1
                ins.then_inc(setup, 1)
                dve.wait_ge(setup, step[0])

            if L1:
                for w, nh in ((wq, NH), (wk, G)):
                    wr = w[:].rearrange("p c (h e) -> p (c h) e", e=HD)
                    mean = wmean[:].rearrange("p c h -> p (c h)")[:, 0:HC * nh]
                    then(dve.tensor_reduce(mean, wr, AX.X, ALU.add))
                    then(dve.tensor_scalar(mean, mean, 1.0 / HD, None, ALU.mult))
                    then(dve.tensor_tensor(wr, wr, mean.unsqueeze(2).to_broadcast([P, HC * nh, HD]), ALU.subtract))
                then(dve.reciprocal(inv_in[:], vecs[:, 4:6]))
                then(dve.reciprocal(inv_sm[:], smooth[:]))
                then(dve.tensor_scalar(qscale[:], vecs[:, 6:7], SCALE, None, ALU.mult))
                then(dve.tensor_scalar(qbias[:], vecs[:, 7:8], SCALE, None, ALU.mult))
                then(dve.tensor_tensor(yscale[:], vecs[:, 11:12], vecs[:, 12:13], ALU.mult))
                for r in range(4 * GU):
                    then(dve.tensor_copy(kT[:, r // GU, r % GU, SE:KW], vecs[:, 9:10]))
            else:
                then(dve.scalar_tensor_tensor(qscale[:], nw[:, 0:1], SCALE, nw[:, 1:2], ALU.mult, ALU.mult))
            dve.sem_inc(ready, 1)

            def token_stats(t, k):
                dve.bn_stats(stats[:], xn[:] if k else X[:, t, :]).then_inc(ln_sum.sem, 1)
                dve.wait_ge(ln_sum.sem, ln_sum.now(t, k + 1))
                dve.sem_inc(gate, 1)
                dve.bn_aggr(mv[:], stats[:]).then_inc(ln_agg.sem, 1)

            def norm_tokens(t, k):
                dve.wait_ge(ln_rs.sem, ln_rs.now(t, k + 1))
                if k == 0:
                    dve.wait_ge(xt_done.sem, xt_done.before(t, 1))
                src = xn[:] if k else X[:, t, :]
                norm = dve.tensor_scalar(xn[:], src, mv[:, 0:1], lr[:], ALU.subtract, ALU.mult)
                if k == NLN - 1:
                    norm.then_inc(xn_done.sem, 1)
                else:
                    norm.then_inc(x_mid.sem, 1)
                    dve.wait_ge(x_mid.sem, x_mid.now(t, 1))

            def quantise_tokens(t):
                dve.wait_ge(xt_copied.sem, xt_copied.now(t, 1))
                a, b, e, m = qa[:, 0:H], qb[:, 0:H], qe[:, 0:H], qm[:, 0:H]
                wide = lambda x: x.rearrange("p (c t) -> p c t", c=HC)
                for c in range(HC):
                    w = dve.tensor_scalar(lnT[:, c, :], lnT[:, c, :], vecs[:, c:c + 1], vecs[:, 2 + c:3 + c],
                                          ALU.mult, ALU.add)
                w.then_inc(xq_steps.sem, 1)
                dve.wait_ge(xq_steps.sem, xq_steps.now(t, 1))
                dve.tensor_tensor(wide(a), lnT[:], inv_in[:].unsqueeze(2).to_broadcast([P, HC, P]), ALU.mult
                                  ).then_inc(xq_steps.sem, 1)
                dve.wait_ge(xq_steps.sem, xq_steps.now(t, 2))
                dve.tensor_scalar(b, a, FP8_MAX, -FP8_MAX, ALU.min, ALU.max).then_inc(xq_steps.sem, 1)
                dve.wait_ge(xq_steps.sem, xq_steps.now(t, 3))
                dve.tensor_scalar(e.bitcast(U16), b.bitcast(U16), 0x7F80, None, ALU.bitwise_and
                                  ).then_inc(xq_steps.sem, 1)
                dve.wait_ge(xq_steps.sem, xq_steps.now(t, 4))
                dve.tensor_scalar(m, e, FP8_SMALLEST, FP8_ROUND, ALU.max, ALU.mult).then_inc(xq_steps.sem, 1)
                dve.wait_ge(xq_steps.sem, xq_steps.now(t, 5))
                dve.tensor_tensor(a, b, m, ALU.add).then_inc(xq_steps.sem, 1)
                dve.wait_ge(xq_steps.sem, xq_steps.now(t, 6))
                dve.tensor_tensor(a, a, m, ALU.subtract).then_inc(xq_steps.sem, 1)
                dve.wait_ge(xq_steps.sem, xq_steps.now(t, 7))
                dve.wait_ge(q_done.sem, q_done.before(t, 4))
                dve.tensor_tensor(xnT[:], wide(a), vecs[:, 4:6].unsqueeze(2).to_broadcast([P, HC, P]), ALU.mult
                                  ).then_inc(xq_done.sem, 1)

            def copy_queries(t, k):
                dst = qn[:, 4 * k:4 * k + 4, :].rearrange("p h e -> p (h e)")
                dve.wait_ge(q_done.sem, q_done.now(t, k + 1))
                dve.wait_ge(qt_done.sem, qt_done.before(t, k + 1))
                if L1:
                    dve.tensor_scalar(dst, QB[k][:, :], vecs[:, 10:11], None, ALU.mult).then_inc(q_in.sem, 1)
                else:
                    dve.tensor_tensor(dst, QB[k][:, :], bq[:, k * 512:(k + 1) * 512], ALU.add).then_inc(q_in.sem, 1)

            def sum_queries(t, k):
                dve.wait_ge(q_sq.sem, q_sq.now(t, k + 1))
                dve.tensor_reduce(qss[:, 4 * k:4 * k + 4], qsq[:], AX.X, ALU.add).then_inc(q_sum.sem, 1)

            def norm_queries(t, k):
                q = qn[:, 4 * k:4 * k + 4, :]
                dve.wait_ge(q_rs.sem, q_rs.now(t, k + 1))
                dve.tensor_tensor(q, q, qr[:, 4 * k:4 * k + 4].unsqueeze(2).to_broadcast([P, 4, HD]), ALU.mult
                                  ).then_inc(qn_done.sem, 1)

            def copy_key(t, j):
                u, g = j // GU, j % GU
                dve.wait_ge(k_done.sem, k_done.now(t, j + 1))
                dve.wait_ge(s_done.sem, s_done.after(t, u - 3))
                if L1:
                    dve.tensor_scalar(kT[:, u % 4, g, 0:SE], Kb[j % 2][:, 0:SE], vecs[:, 8:9], None, ALU.mult
                                      ).then_inc(k_raw.sem, 1)
                else:
                    dve.tensor_scalar(kT[:, u % 4, g, 0:SE], Kb[j % 2][:, 0:SE], bkv[:, 0, j % G:j % G + 1], None,
                                      ALU.add).then_inc(k_raw.sem, 1)

            def max_scores(t, u):
                dve.wait_ge(s_done.sem, s_done.now(t, u + 1))
                if L1:
                    dve.tensor_reduce(top[:, u:u + 1], Sb[:, 0:SE], AX.X, ALU.max, negate=True
                                      ).then_inc(top_found.sem, 1)
                    dve.wait_ge(top_found.sem, top_found.now(t, u + 1))
                    qkb = Sb[:, SE:KW]
                    dve.tensor_scalar(ntop[:, u:u + 1], top[:, u:u + 1], qkb, qkb, ALU.subtract, ALU.add
                                      ).then_inc(top_done.sem, 1)
                else:
                    dve.wait_ge(e_done.sem, e_done.after(t, u - 1))
                    dve.sem_inc(gate, 1)
                    dve.tensor_tensor_reduce(sm[:, u % 2, :], Sb[:, 0:SE], mask[:], 1.0, -3.0e38, ALU.add, ALU.max,
                                             top[:, u:u + 1]).then_inc(top_found.sem, 1)
                    dve.wait_ge(top_found.sem, top_found.now(t, u + 1))
                    dve.tensor_scalar(ntop[:, u:u + 1], top[:, u:u + 1], -1.0, None, ALU.mult
                                      ).then_inc(top_done.sem, 1)

            def norm_probs(t, u):
                dve.wait_ge(e_done.sem, e_done.now(t, u + 1))
                dve.reciprocal(rps[:, u:u + 1], ps[:, u:u + 1]).then_inc(r_done.sem, 1)
                dve.wait_ge(r_done.sem, r_done.now(t, u + 1))
                dve.tensor_scalar(pr[:, u % 4, :], pr[:, u % 4, :], rps[:, u:u + 1], None, ALU.mult
                                  ).then_inc(pn_done.sem, 1)

            def copy_probs(t, u):
                b, v = u // UNITS, u % UNITS
                dve.wait_ge(pt_done.sem, pt_done.now(t, u + 1))
                if v == 0:
                    dve.wait_ge(pc_done.sem, pc_done.after(t, HC * (b - 1)))
                dve.tensor_copy(pT[:, b % 2, 0:2, v * P:(v + 1) * P],
                                PTb[:, 0:2 * P].rearrange("p (c r) -> p c r", c=2)).then_inc(pt_copied.sem, 1)
                if v == UNITS - 1:
                    dve.tensor_copy(pT[0:CW[2], b % 2, 2, :], Lb[0:CW[2], :]).then_inc(pl_copied.sem, 1)

            def copy_weighed(t, b):
                dve.wait_ge(o_done.sem, o_done.after(t, b))
                for h in range(HC):
                    dve.wait_ge(pc_done.sem, pc_done.now(t, HC * b + h + 1))
                    dve.tensor_copy(pcT[:, h, :], PC[h][:, :]).then_inc(pc_copied.sem, 1)

            def copy_heads(t, b):
                dve.wait_ge(o_done.sem, o_done.now(t, b + 1))
                if b == 0:
                    dve.wait_ge(y_done.sem, y_done.before(t, 1))
                src = PC[0][:, :].rearrange("p (h q) -> p h q", h=NH)
                dst = oT[:, :, b * S:(b + 1) * S]
                if not L1:
                    for g in range(G):
                        a = dve.tensor_scalar(dst[:, 4 * g:4 * g + 4, :], src[:, 4 * g:4 * g + 4, :],
                                              bkv[:, 1, g:g + 1], None, ALU.add)
                    a.then_inc(o_copied.sem, 1)
                    return
                wide = lambda x: x[:].rearrange("p (h q) -> p h q", h=NH)
                dve.tensor_tensor(wide(qa), src, inv_sm[:].unsqueeze(2).to_broadcast([P, NH, S]), ALU.mult
                                  ).then_inc(o_read.sem, 1)
                dve.wait_ge(o_read.sem, o_read.now(t, b + 1))
                dve.tensor_scalar(qb[:], qa[:], FP8_MAX, -FP8_MAX, ALU.min, ALU.max).then_inc(oq_steps.sem, 1)
                dve.wait_ge(oq_steps.sem, oq_steps.now(t, 4 * b + 1))
                dve.tensor_scalar(qe[:].bitcast(U16), qb[:].bitcast(U16), 0x7F80, None, ALU.bitwise_and
                                  ).then_inc(oq_steps.sem, 1)
                dve.wait_ge(oq_steps.sem, oq_steps.now(t, 4 * b + 2))
                dve.tensor_scalar(qm[:], qe[:], FP8_SMALLEST, FP8_ROUND, ALU.max, ALU.mult).then_inc(oq_steps.sem, 1)
                dve.wait_ge(oq_steps.sem, oq_steps.now(t, 4 * b + 3))
                dve.tensor_tensor(qa[:], qb[:], qm[:], ALU.add).then_inc(oq_steps.sem, 1)
                dve.wait_ge(oq_steps.sem, oq_steps.now(t, 4 * b + 4))
                dve.tensor_tensor(dst, wide(qa), wide(qm), ALU.subtract).then_inc(o_copied.sem, 1)

            def add_output(t):
                dve.wait_ge(y_done.sem, y_done.now(t, 1))
                if L1:
                    dve.scalar_tensor_tensor(ysum[:], PC[1][:, 0:H], yscale[:], Yc[:, t, :], ALU.mult, ALU.add
                                             ).then_inc(y_summed.sem, 1)
                    dve.wait_ge(y_summed.sem, y_summed.now(t, 1))
                    dve.tensor_tensor(X[:, t, :], X[:, t, :], ysum[:], ALU.add).then_inc(x_added.sem, 1)
                else:
                    dve.tensor_tensor(X[:, t, :], X[:, t, :], PC[1][:, 0:H], ALU.add).then_inc(x_added.sem, 1)

            def tile(i, cur, prev, nxt):
                for u in steps(cur):
                    if cur:
                        for g in range(GU):
                            copy_key(i, GU * u + g)
                    if u == 0 and nxt:
                        token_stats(i + 1, 0)
                    if u == 1 and nxt:
                        norm_tokens(i + 1, NLN - 1)
                    for t, v in lagging(i, u, 3, cur, prev):
                        norm_probs(t, v)
                    for t, v in lagging(i, u, 2, cur, prev):
                        max_scores(t, v)
                    if u == 0 and nxt and L1:
                        norm_tokens(i + 1, 0)
                        token_stats(i + 1, 1)
                    if u == 2 and nxt and L1:
                        quantise_tokens(i + 1)
                    if u in (6, 7, 10, 11) and nxt:
                        sum_queries(i + 1, {6: 0, 7: 1, 10: 2, 11: 3}[u])
                    if u in (7, 8, 11, 12) and nxt:
                        norm_queries(i + 1, {7: 0, 8: 1, 11: 2, 12: 3}[u])
                    if u == 7 and prev:
                        add_output(i - 1)
                    for t, v in lagging(i, u, 4, cur, prev):
                        copy_probs(t, v)
                    for t, b in batch_at(i, u, 8, cur, prev):
                        copy_weighed(t, b)
                    for t, b in batch_at(i, u, 9, cur, prev):
                        copy_heads(t, b)
                    if u in (5, 6, 9, 10) and nxt:
                        copy_queries(i + 1, {5: 0, 6: 1, 9: 2, 10: 3}[u])

            token_stats(0, 0)
            norm_tokens(0, 0)
            if L1:
                token_stats(0, 1)
                norm_tokens(0, 1)
                quantise_tokens(0)
            for k in range(4):
                copy_queries(0, k)
                sum_queries(0, k)
                norm_queries(0, k)
            run(dve, tile)


PT = 4


class TokenNorm:

    def __init__(self, ctx, nc, n, X, ident, pt=PT):
        def sb(name, shape):
            return ctx.enter_context(nc.sbuf_tensor(n + name, shape, F32))

        self.X, self.ident, self.pt = X, ident, pt
        self.stats = sb("ln_stats", [P, pt, 6])
        self.mv = sb("ln_mv", [P, pt, 2])
        self.lr = sb("ln_r", [P, pt])
        self.eps = sb("ln_eps", [P, 1])
        self.xn = sb("xn", [P, pt, H])
        self.xnT = sb("xnT", [P, HC, pt * P])
        self.gate = ctx.semaphore(n + "ln_gate")
        self.eps_set = ctx.semaphore(n + "ln_eps_set")
        self.summed = Signal(ctx, nc, n + "ln_summed", 1)
        self.aggregated = Signal(ctx, nc, n + "ln_aggregated", 1)
        self.logged = Signal(ctx, nc, n + "ln_logged", 1)
        self.scaled = Signal(ctx, nc, n + "ln_rsqrt", 1)
        self.normed = Signal(ctx, nc, n + "ln_normed", 1)
        self.turned = Signal(ctx, nc, n + "ln_transposed", HC)
        self.copied = Signal(ctx, nc, n + "ln_copied", HC)

    def vector_setup(self, dve):
        for s in (self.summed, self.aggregated, self.normed):
            s.prime(dve)
        dve.memset(self.eps[:], 1e-5).then_inc(self.eps_set, 1)

    def scalar_setup(self, act):
        for s in (self.logged, self.scaled, self.copied):
            s.prime(act)
        act.wait_ge(self.eps_set, 1)

    def vector(self, dve, i):
        for t in range(self.pt):
            a = dve.bn_stats(self.stats[:, t, :], self.X[:, i * self.pt + t, :])
        a.then_inc(self.summed.sem, 1)
        dve.wait_ge(self.summed.sem, self.summed.now(i, 1))
        dve.sem_inc(self.gate, 1)
        for t in range(self.pt):
            a = dve.bn_aggr(self.mv[:, t, :], self.stats[:, t, :])
        a.then_inc(self.aggregated.sem, 1)
        dve.wait_ge(self.scaled.sem, self.scaled.now(i, 1))
        dve.wait_ge(self.turned.sem, self.turned.before(i, HC))
        for t in range(self.pt):
            a = dve.tensor_scalar(self.xn[:, t, :], self.X[:, i * self.pt + t, :], self.mv[:, t, 0:1],
                                  self.lr[:, t:t + 1], ALU.subtract, ALU.mult)
        a.then_inc(self.normed.sem, 1)

    def scalar_rsqrt(self, act, i):
        act.wait_ge(self.aggregated.sem, self.aggregated.now(i, 1))
        act.activation(self.lr[:], self.mv[:, :, 1], ACT.Ln, bias=self.eps[:]).then_inc(self.logged.sem, 1)
        act.wait_ge(self.logged.sem, self.logged.now(i, 1))
        act.activation(self.lr[:], self.lr[:], ACT.Exp, scale=-0.5).then_inc(self.scaled.sem, 1)

    def tensor(self, pe, i, banks):
        pe.wait_ge(self.normed.sem, self.normed.now(i, 1))
        for c in range(HC):
            for t in range(self.pt):
                m = pe.transpose(banks[c][:, t * P:(t + 1) * P], self.xn[:, t, c * P:(c + 1) * P], self.ident[:])
            m.then_inc(self.turned.sem, 1)

    def scalar_copy(self, act, i, banks):
        for c in range(HC):
            act.wait_ge(self.turned.sem, self.turned.now(i, c + 1))
            act.activation(self.xnT[:, c, :], banks[c][:, 0:self.pt * P], ACT.Copy).then_inc(self.copied.sem, 1)


def product_attention(nc, d, X, ident, tiles):
    n = "a0_"
    M = 512
    MC = M // P
    NHQ = 4
    DK = 16
    SLOT = 32
    KSCALE = float(DK) ** 0.5
    STEPS = NHQ * MC * 4
    passes = tiles // PT
    N = PT * P
    with Part(nc) as ctx:
        def sb(name, shape, dt=F32):
            return ctx.enter_context(nc.sbuf_tensor(n + name, shape, dt))

        def bank(name):
            return ctx.enter_context(nc.psum_tensor(n + name, [P, 512], F32))

        def sig(name, per, unit=1):
            return Signal(ctx, nc, n + name, per, unit)

        wq = sb("wq", [P, HC, NHQ * P])
        kT = sb("kT", [P, NHQ, M])
        vw = sb("vw", [P, MC, 512])
        wg = sb("wg", [P, HC, 512])
        wo = sb("wo", [P, NHQ, H])
        qT = sb("qT", [P, NHQ, N])
        eT = sb("eT", [P, 4, N])
        gT = sb("gT", [P, 2, N])
        og = sb("og", [P, NHQ, N])
        Eb = [bank(f"E{k}") for k in range(4)]
        Ob = [bank("O0"), bank("O1")]
        Tb = [bank("T0"), bank("T1")]
        ln = TokenNorm(ctx, nc, n, X, ident)
        weights = ctx.semaphore(n + "weights")
        q_done = sig("q_done", NHQ)
        q_copied = sig("q_copied", NHQ)
        g_done = sig("gate_done", NHQ)
        g_copied = sig("gate_silu", NHQ)
        e_done = sig("energy_done", STEPS)
        e_silu = sig("energy_silu", STEPS)
        pv_done = sig("pv_done", STEPS)
        og_done = sig("gated", NHQ)
        y_done = sig("y_done", 2)
        x_added = sig("x_added", 2)
        block = ctx.open_block()

        @block.sync
        def _(sp):
            for dst, src in ((wq, d["wq"].rearrange("(c p) n -> p c n", p=P)),
                             (kT, d["kT"].rearrange("j p m -> p j m")),
                             (vw, d["vw"].rearrange("(c p) n -> p c n", p=P)),
                             (wg, d["wg"].rearrange("(c p) n -> p c n", p=P)),
                             (wo, d["wo"].rearrange("(c p) n -> p c n", p=P))):
                sp.dma_start(dst[:], src).then_inc(weights, 16)

        @block.tensor
        def _(pe):
            for s in (ln.turned, q_done, g_done, e_done, pv_done, y_done):
                s.prime(pe)
            pe.wait_ge(weights, 16 * 5)

            def energy(i, s):
                hq, c, r = s // 16, s // 4 % 4, s % 4
                at = slice(SLOT * r, SLOT * r + DK)
                pe.matmul(Eb[r][:, :], kT[at, hq, c * P:(c + 1) * P], qT[at, hq, :], start=True, stop=True
                          ).then_inc(e_done.sem, 1)

            def weigh(i, s):
                hq, c, r = s // 16, s // 4 % 4, s % 4
                pe.wait_ge(e_silu.sem, e_silu.now(i, s + 1))
                if s % 16 == 0:
                    pe.wait_ge(og_done.sem, og_done.after(i, hq - 1))
                h = 4 * hq + r
                pe.matmul(Ob[hq % 2][32 * r:32 * r + 32, :], vw[:, c, 32 * h:32 * h + 32], eT[:, r, :],
                          start=c == 0, stop=c == MC - 1).then_inc(pv_done.sem, 1)

            with pe.Fori(0, passes) as i:
                pe.wait_ge(x_added.sem, x_added.before(i, 2))
                ln.tensor(pe, i, Tb)
                pe.wait_ge(ln.copied.sem, ln.copied.now(i, HC))
                for j in range(NHQ):
                    for c in range(HC):
                        m = pe.matmul(Eb[j][:, :], wq[:, c, j * P:(j + 1) * P], ln.xnT[:, c, :],
                                      start=c == 0, stop=c == HC - 1)
                    m.then_inc(q_done.sem, 1)
                for s in range(STEPS + 2):
                    if s < STEPS and s % 16 == 0:
                        j = s // 16
                        if j >= 2:
                            pe.wait_ge(g_copied.sem, g_copied.now(i, j - 1))
                        for c in range(HC):
                            m = pe.matmul(Tb[j % 2][:, :], wg[:, c, j * P:(j + 1) * P], ln.xnT[:, c, :],
                                          start=c == 0, stop=c == HC - 1)
                        m.then_inc(g_done.sem, 1)
                        if j == 0:
                            pe.wait_ge(q_copied.sem, q_copied.now(i, NHQ))
                    if s < STEPS:
                        energy(i, s)
                    if s >= 2:
                        weigh(i, s - 2)
                pe.wait_ge(og_done.sem, og_done.now(i, NHQ))
                pe.wait_ge(g_copied.sem, g_copied.now(i, NHQ))
                for k in range(2):
                    for t in (2 * k, 2 * k + 1):
                        for j in range(NHQ):
                            m = pe.matmul(Tb[k][:, t % 2 * H:t % 2 * H + H], og[:, j, t * P:(t + 1) * P], wo[:, j, :],
                                          start=j == 0, stop=j == NHQ - 1)
                    m.then_inc(y_done.sem, 1)

        @block.scalar
        def _(act):
            ln.scalar_setup(act)
            for s in (q_copied, g_copied, e_silu):
                s.prime(act)
            with act.Fori(0, passes) as i:
                ln.scalar_rsqrt(act, i)
                act.wait_ge(g_done.sem, g_done.before(i, NHQ))
                ln.scalar_copy(act, i, Tb)
                act.wait_ge(e_done.sem, e_done.before(i, STEPS))
                for j in range(NHQ):
                    act.wait_ge(q_done.sem, q_done.now(i, j + 1))
                    act.activation(qT[:, j, :], Eb[j][:, :], ACT.Copy).then_inc(q_copied.sem, 1)
                for s in range(STEPS):
                    if s % 16 == 0:
                        j = s // 16
                        act.wait_ge(g_done.sem, g_done.now(i, j + 1))
                        act.wait_ge(og_done.sem, og_done.after(i, j - 1))
                        act.activation(gT[:, j % 2, :], Tb[j % 2][:, :], ACT.Silu).then_inc(g_copied.sem, 1)
                    act.wait_ge(e_done.sem, e_done.now(i, s + 1))
                    act.wait_ge(pv_done.sem, pv_done.after(i, s - 3))
                    act.activation(eT[:, s % 4, :], Eb[s % 4][:, :], ACT.Silu, scale=KSCALE
                                   ).then_inc(e_silu.sem, 1)

        @block.vector
        def _(dve):
            ln.vector_setup(dve)
            for s in (og_done, x_added):
                s.prime(dve)
            with dve.Fori(0, passes) as i:
                ln.vector(dve, i)
                for j in range(NHQ):
                    dve.wait_ge(g_copied.sem, g_copied.now(i, j + 1))
                    dve.wait_ge(pv_done.sem, pv_done.now(i, 16 * (j + 1)))
                    if j == 0:
                        dve.wait_ge(y_done.sem, y_done.before(i, 2))
                    dve.scalar_tensor_tensor(og[:, j, :], Ob[j % 2][:, :], KSCALE, gT[:, j % 2, :],
                                             ALU.mult, ALU.mult).then_inc(og_done.sem, 1)
                for k in range(2):
                    dve.wait_ge(y_done.sem, y_done.now(i, k + 1))
                    for t in (2 * k, 2 * k + 1):
                        Xt = X[:, i * PT + t, :]
                        a = dve.tensor_tensor(Xt, Xt, Tb[k][:, t % 2 * H:t % 2 * H + H], ALU.add)
                    a.then_inc(x_added.sem, 1)


def experts(nc, d, X, ident, tiles):
    n = "e0_"
    E = 8
    ALL = E + 1
    passes = tiles // PT
    N = PT * P
    with Part(nc) as ctx:
        def sb(name, shape, dt=F32):
            return ctx.enter_context(nc.sbuf_tensor(n + name, shape, dt))

        def bank(name):
            return ctx.enter_context(nc.psum_tensor(n + name, [P, 512], F32))

        def sig(name, per, unit=1):
            return Signal(ctx, nc, n + name, per, unit)

        w1 = sb("w1", [P, HC, ALL * P])
        w3 = sb("w3", [P, HC, ALL * P])
        w2 = sb("w2", [P, ALL, H])
        wr = sb("wr", [P, HC, E])
        places = sb("places", [P, E])
        lg = sb("lg", [P, PT, E])
        pe_ = sb("probs", [P, PT, E])
        m1 = sb("m1", [P, PT])
        sums = sb("sums", [P, PT])
        rsum = sb("rsum", [P, PT])
        best = sb("best", [P, PT, 8])
        at = sb("at", [P, PT, 8], U32)
        atf = sb("atf", [P, PT, 8])
        chosen = sb("chosen", [P, PT, E])
        comb = sb("comb", [P, PT, E])
        g1 = sb("g1", [P, 2, N])
        gT = sb("gT", [P, 2, N])
        Ab = [bank("A0"), bank("A1")]
        Bb = [bank("B0"), bank("B1")]
        Yb = [[bank("Y0"), bank("Y1")], [bank("T0"), bank("T1")]]
        Tb = Yb[1]
        ln = TokenNorm(ctx, nc, n, X, ident)
        weights = ctx.semaphore(n + "weights")
        r_done = sig("router_done", 1)
        r_shift = sig("router_shifted", 1)
        r_exp = sig("router_exp", 1)
        h_done = sig("hidden_done", 2 * ALL)
        h_silu = sig("hidden_silu", ALL)
        g_done = sig("gated", ALL)
        y_done = sig("y_done", ALL)
        x_added = sig("x_added", ALL)
        dchain = Chain(ctx, nc, n + "dve_chain", 8 + 2 * PT)
        block = ctx.open_block()

        @block.sync
        def _(sp):
            for dst, src in ((w1, d["w1"].rearrange("(c p) n -> p c n", p=P)),
                             (w3, d["w3"].rearrange("(c p) n -> p c n", p=P)),
                             (w2, d["w2"].rearrange("(e p) n -> p e n", p=P)),
                             (wr, d["wr"].rearrange("(c p) n -> p c n", p=P)),
                             (places, d["places"])):
                sp.dma_start(dst[:], src).then_inc(weights, 16)

        @block.tensor
        def _(pe):
            for s in (ln.turned, r_done, h_done, y_done):
                s.prime(pe)
            pe.wait_ge(weights, 16 * 5)
            with pe.Fori(0, passes) as i:
                pe.wait_ge(x_added.sem, x_added.before(i, ALL - 1))
                ln.tensor(pe, i, Tb)
                pe.wait_ge(ln.copied.sem, ln.copied.now(i, HC))
                for t in range(PT):
                    for c in range(HC):
                        m = pe.matmul(Tb[0][:, t * E:(t + 1) * E], ln.xnT[:, c, t * P:(t + 1) * P], wr[:, c, :],
                                      start=c == 0, stop=c == HC - 1)
                m.then_inc(r_done.sem, 1)
                for e in range(ALL + 1):
                    if e < ALL:
                        pe.wait_ge(g_done.sem, g_done.after(i, e - 1))
                        for w, b in ((w1, Ab), (w3, Bb)):
                            for c in range(HC):
                                m = pe.matmul(b[e % 2][:, :], w[:, c, e * P:(e + 1) * P], ln.xnT[:, c, :],
                                              start=c == 0, stop=c == HC - 1)
                            m.then_inc(h_done.sem, 1)
                    if e:
                        f = e - 1
                        pe.wait_ge(g_done.sem, g_done.now(i, e))
                        pe.wait_ge(x_added.sem, x_added.after(i, f - 1))
                        if f == 1:
                            pe.wait_ge(r_shift.sem, r_shift.now(i, 1))
                        for t in range(PT):
                            m = pe.matmul(Yb[f % 2][t // 2][:, t % 2 * H:t % 2 * H + H],
                                          gT[:, f % 2, t * P:(t + 1) * P], w2[:, f, :], start=True, stop=True)
                        m.then_inc(y_done.sem, 1)

        @block.scalar
        def _(act):
            ln.scalar_setup(act)
            for s in (r_exp, h_silu):
                s.prime(act)
            with act.Fori(0, passes) as i:
                ln.scalar_rsqrt(act, i)
                act.wait_ge(h_done.sem, h_done.before(i, 2 * ALL))
                ln.scalar_copy(act, i, Tb)
                act.wait_ge(r_shift.sem, r_shift.now(i, 1))
                act.activation(pe_[:], lg[:], ACT.Exp).then_inc(r_exp.sem, 1)
                for e in range(ALL):
                    act.wait_ge(h_done.sem, h_done.now(i, 2 * e + 1))
                    act.wait_ge(g_done.sem, g_done.after(i, e - 1))
                    act.activation(g1[:, e % 2, :], Ab[e % 2][:, :], ACT.Silu).then_inc(h_silu.sem, 1)

        @block.vector
        def _(dve):
            ln.vector_setup(dve)
            for s in (r_shift, g_done, x_added, dchain):
                s.prime(dve)
            dve.wait_ge(weights, 16 * 5)

            def link(i, ins):
                ins.then_inc(dchain.sem, 1)
                dve.wait_ge(dchain.sem, dchain.next(i))

            def add_expert(i, e):
                dve.wait_ge(y_done.sem, y_done.now(i, e + 1))
                if e:
                    dve.wait_ge(x_added.sem, x_added.now(i, e))
                for t in range(PT):
                    Xt = X[:, i * PT + t, :]
                    y = Yb[e % 2][t // 2][:, t % 2 * H:t % 2 * H + H]
                    if e < E:
                        a = dve.scalar_tensor_tensor(Xt, y, comb[:, t, e:e + 1], Xt, ALU.mult, ALU.add)
                    else:
                        a = dve.tensor_tensor(Xt, Xt, y, ALU.add)
                a.then_inc(x_added.sem, 1)

            with dve.Fori(0, passes) as i:
                dchain.k = 0
                ln.vector(dve, i)
                dve.wait_ge(r_done.sem, r_done.now(i, 1))
                scores = Tb[0][:, 0:PT * E].rearrange("p (t e) -> p t e", t=PT)
                link(i, dve.tensor_reduce(m1[:], scores, AX.X, ALU.max))
                dve.tensor_tensor(lg[:], scores, m1[:].unsqueeze(2).to_broadcast([P, PT, E]), ALU.subtract
                                  ).then_inc(r_shift.sem, 1)
                dve.wait_ge(r_exp.sem, r_exp.now(i, 1))
                link(i, dve.tensor_reduce(sums[:], pe_[:], AX.X, ALU.add))
                link(i, dve.reciprocal(rsum[:], sums[:]))
                link(i, dve.tensor_tensor(pe_[:], pe_[:], rsum[:].unsqueeze(2).to_broadcast([P, PT, E]), ALU.mult))
                dve.sem_inc(ln.gate, 1)
                for t in range(PT):
                    a = dve.max(best[:, t, :], pe_[:, t, :])
                link(i, a)
                dve.sem_inc(ln.gate, 1)
                for t in range(PT):
                    a = dve.max_index(at[:, t, :], best[:, t, :], pe_[:, t, :])
                link(i, a)
                link(i, dve.tensor_copy(atf[:], at[:]))
                for t in range(PT):
                    link(i, dve.tensor_scalar(chosen[:, t, :], places[:], atf[:, t, 0:1], None, ALU.is_equal))
                    link(i, dve.scalar_tensor_tensor(chosen[:, t, :], places[:], atf[:, t, 1:2], chosen[:, t, :],
                                                     ALU.is_equal, ALU.add))
                link(i, dve.tensor_tensor(comb[:], pe_[:], chosen[:], ALU.mult))
                for e in range(ALL + 1):
                    if e < ALL:
                        dve.wait_ge(h_silu.sem, h_silu.now(i, e + 1))
                        dve.wait_ge(h_done.sem, h_done.now(i, 2 * e + 2))
                        dve.wait_ge(y_done.sem, y_done.after(i, e - 1))
                        dve.tensor_tensor(gT[:, e % 2, :], g1[:, e % 2, :], Bb[e % 2][:, :], ALU.mult
                                          ).then_inc(g_done.sem, 1)
                    if e:
                        add_expert(i, e - 1)
                dchain.done()


def core_attention(nc, d, X, Yc, ident, tiles):
    n = "c1_"
    G = 8
    NK = NH + G
    KINDS = 3
    SCALE = HD ** -0.5
    with Part(nc) as ctx:
        def sb(name, shape, dt=F32):
            return ctx.enter_context(nc.sbuf_tensor(n + name, shape, dt))

        def sig(name, per, unit=1):
            return Signal(ctx, nc, n + name, per, unit)

        wqk = sb("wqk", [P, HC, NK * HD])
        wv = sb("wv", [P, HC, G * HD])
        wo = sb("wo", [P, NH, H])
        vecs = sb("vecs", [P, 20])
        smooth = sb("smooth", [P, NH])
        inv_in = sb("inv_in", [P, KINDS * HC])
        inv_sm = sb("inv_sm", [P, NH])
        qw = sb("qw", [P, 2])
        yscale = sb("yscale", [P, 1])
        wmean = sb("wmean", [P, HC * NK])
        eps = sb("eps", [P, 1])
        qa = sb("qa", [P, NH * P])
        qb = sb("qb", [P, NH * P], BF16)
        qe = sb("qe", [P, NH * P], BF16)
        qm = sb("qm", [P, NH * P])
        xa = sb("xa", [P, KINDS * HC * P])
        xb = sb("xb", [P, KINDS * HC * P], BF16)
        xe = sb("xe", [P, KINDS * HC * P], BF16)
        xm = sb("xm", [P, KINDS * HC * P])
        lnT = sb("lnT", [P, HC, P])
        xq = sb("xq", [P, KINDS * HC, P])
        qk = sb("qk", [P, NK, HD])
        qksq = sb("qksq", [P, NK, HD])
        ss = sb("ss", [P, NK])
        rs = sb("rs", [P, NK])
        vn = sb("vn", [P, G, HD])
        qkT = sb("qkT", [P, NK, P])
        ntop = sb("ntop", [P, NH])
        sums = sb("sums", [P, NH])
        rsum = sb("rsum", [P, NH])
        sc = sb("sc", [P, NH, S])
        pr = sb("pr", [P, NH, S])
        prT = sb("prT", [P, NH, S])
        oT = sb("oT", [P, NH, P])
        banks = [ctx.enter_context(nc.psum_tensor(f"{n}B{k}", [P, 512], F32)) for k in range(8)]
        ln = TokenNorm(ctx, nc, n, X, ident, pt=1)
        weights = ctx.semaphore(n + "weights")
        ready = ctx.semaphore(n + "constants_ready")
        setup = ctx.semaphore(n + "setup_steps")
        lstats = sig("ln2_stats", 1)
        lr_done = sig("ln2_rsqrt", 1)
        xn_done = sig("xn_done", 1)
        xt_done = sig("x_transposed", 1)
        xt_copied = sig("xT_copied", 1)
        xq_done = sig("x_quantised", 1)
        p_done = sig("projected", 8)
        p_copied = sig("qk_copied", 6)
        v_copied = sig("v_copied", 2)
        sq_done = sig("squared", 1)
        ss_done = sig("squares_summed", 1)
        rs_done = sig("heads_rsqrt", 1)
        qn_done = sig("heads_normed", 1)
        t_done = sig("heads_transposed", 6)
        t_copied = sig("heads_copied", 6)
        s_done = sig("scores_done", 1)
        sub_done = sig("scores_shifted", 1)
        e_done = sig("exp_done", 1)
        pT_done = sig("probs_transposed", 1)
        o_done = sig("heads_out", 1)
        o_copied = sig("heads_quantised", 1)
        y_done = sig("y_done", 1)
        y_copied = sig("y_copied", 1)
        x_log = sig("ln2_log", 1)
        h_log = sig("heads_log", 1)
        x_steps = sig("x_quantise_steps", 8)
        sm_steps = sig("softmax_steps", 4)
        oq_steps = sig("out_quantise_steps", 4)
        oq_sum = sig("out_rounded_up", 1)
        gate = ctx.semaphore(n + "gate")

        block = ctx.open_block()

        @block.sync
        def _(sp):
            for dst, src in ((wqk, d["wqk"].rearrange("(c p) n -> p c n", p=P)),
                             (wv, d["wv"].rearrange("(c p) n -> p c n", p=P)),
                             (wo, d["wo"].rearrange("(h p) n -> p h n", p=P)),
                             (vecs, d["vecs"]), (smooth, d["smooth"])):
                sp.dma_start(dst[:], src).then_inc(weights, 16)

        PB = [0, 1, 2, 0, 1, 2, 3, 0]
        TB = [1, 2, 0, 1, 2, 0]
        XB, YB, SB = banks[3], banks[1], banks[4]
        OB = banks[4:8]

        @block.tensor
        def _(pe):
            for s in (xt_done, p_done, t_done, s_done, o_done, y_done):
                s.prime(pe)
            pe.wait_ge(ready, 1)

            def transpose_tokens(t):
                pe.wait_ge(xn_done.sem, xn_done.now(t, 1))
                pe.wait_ge(v_copied.sem, v_copied.before(t, 1))
                for c in range(HC):
                    m = pe.transpose(XB[:, c * P:(c + 1) * P], ln.xn[:, 0, c * P:(c + 1) * P], ident[:])
                m.then_inc(xt_done.sem, 1)

            def project(t, k, last=None):
                kind = (0, 0, 0, 0, 1, 1, 2, 2)[k]
                w = wqk[:, :, k * 512:(k + 1) * 512] if k < 6 else wv[:, :, (k - 6) * 512:(k - 5) * 512]
                if k == 0:
                    pe.wait_ge(xq_done.sem, xq_done.now(t, 1))
                if k == 1 and last is not None:
                    pe.wait_ge(y_copied.sem, y_copied.before(last, 1))
                if k in (3, 4, 5, 7):
                    pe.wait_ge(p_copied.sem, p_copied.now(t, {3: 1, 4: 2, 5: 3, 7: 4}[k]))
                for c in range(HC):
                    m = pe.matmul(banks[PB[k]][:, :], xq[:, kind * HC + c, :], w[:, c, :], start=c == 0,
                                  stop=c == HC - 1)
                m.then_inc(p_done.sem, 1)

            def transpose_heads(t, k):
                if k == 0:
                    pe.wait_ge(qn_done.sem, qn_done.now(t, 1))
                    pe.wait_ge(v_copied.sem, v_copied.now(t, 2))
                if k >= 3:
                    pe.wait_ge(t_copied.sem, t_copied.now(t, k - 2))
                for h in range(4):
                    m = pe.transpose(banks[TB[k]][:, h * P:(h + 1) * P], qk[:, 4 * k + h, :], ident[:])
                m.then_inc(t_done.sem, 1)

            def scores(t):
                pe.wait_ge(t_copied.sem, t_copied.now(t, 6))
                pe.wait_ge(oq_steps.sem, oq_steps.before(t, 1))
                for h in range(NH):
                    for b in range(BT):
                        at = slice(b * S, (b + 1) * S)
                        m = pe.matmul(SB[at, h * S:(h + 1) * S], qkT[:, h, at], qkT[:, NH + h // 2, at],
                                      start=True, stop=True)
                m.then_inc(s_done.sem, 1)

            def weigh_values(t):
                pe.wait_ge(pT_done.sem, pT_done.now(t, 1))
                pe.wait_ge(v_copied.sem, v_copied.now(t, 2))
                for g in range(G):
                    for b in range(BT):
                        at = slice(b * S, (b + 1) * S)
                        m = pe.matmul(OB[b][:, g * 2 * S:(g + 1) * 2 * S], vn[at, g, :],
                                      prT[at, 2 * g:2 * g + 2, :].rearrange("p h q -> p (h q)"),
                                      start=True, stop=True)
                m.then_inc(o_done.sem, 1)

            def project_out(t):
                pe.wait_ge(o_copied.sem, o_copied.now(t, 1))
                for h in range(NH):
                    m = pe.matmul(YB[:, 0:H], oT[:, h, :], wo[:, h, :], start=h == 0, stop=h == NH - 1)
                m.then_inc(y_done.sem, 1)

            def tile(i, one, two):
                scores(i)
                for k in range(8 if one else 0):
                    project(i + 1, k, last=i)
                weigh_values(i)
                for k in range(6 if one else 0):
                    transpose_heads(i + 1, k)
                if two:
                    transpose_tokens(i + 2)
                if one:
                    pe.wait_ge(t_copied.sem, t_copied.now(i + 1, 4))
                project_out(i)

            transpose_tokens(0)
            for k in range(8):
                project(0, k)
            for k in range(6):
                transpose_heads(0, k)
            transpose_tokens(1)
            with pe.Fori(0, tiles - 2) as i:
                tile(i, True, True)
            tile(tiles - 2, True, False)
            tile(tiles - 1, False, False)

        @block.scalar
        def _(act):
            for s in (ln.logged, ln.scaled, x_log, lr_done, xt_copied, sq_done, h_log, rs_done, t_copied, e_done,
                      v_copied):
                s.prime(act)
            act.preload_act_table_set(EXPLN)
            act.wait_ge(ready, 1)

            def tokens(t):
                ln.scalar_rsqrt(act, t)
                act.wait_ge(lstats.sem, lstats.now(t, 1))
                act.activation(ln.lr[:], ln.mv[:, :, 1], ACT.Ln, bias=eps[:]).then_inc(x_log.sem, 1)
                act.wait_ge(x_log.sem, x_log.now(t, 1))
                act.activation(ln.lr[:], ln.lr[:], ACT.Exp, scale=-0.5).then_inc(lr_done.sem, 1)
                act.wait_ge(xt_done.sem, xt_done.now(t, 1))
                act.wait_ge(xq_done.sem, xq_done.before(t, 1))
                act.activation(lnT[:], XB[:, 0:H].rearrange("p (c t) -> p c t", c=HC), ACT.Copy
                               ).then_inc(xt_copied.sem, 1)

            def values(t):
                act.wait_ge(o_done.sem, o_done.before(t, 1))
                for k in range(2):
                    act.wait_ge(p_done.sem, p_done.now(t, 7 + k))
                    act.activation(vn[:, 4 * k:4 * k + 4, :].rearrange("p g e -> p (g e)"), banks[PB[6 + k]][:, :],
                                   ACT.Copy, scale=vecs[:, 16:17]).then_inc(v_copied.sem, 1)

            def heads_rsqrt(t):
                act.wait_ge(p_copied.sem, p_copied.now(t, 6))
                act.activation(qksq[:], qk[:], ACT.Square).then_inc(sq_done.sem, 1)
                act.wait_ge(ss_done.sem, ss_done.now(t, 1))
                act.activation(rs[:], ss[:], ACT.Ln, bias=eps[:], scale=1.0 / HD).then_inc(h_log.sem, 1)
                act.wait_ge(h_log.sem, h_log.now(t, 1))
                act.activation(rs[:], rs[:], ACT.Exp, scale=-0.5).then_inc(rs_done.sem, 1)

            def heads_copy(t):
                act.wait_ge(s_done.sem, s_done.before(t, 1))
                for k in range(6):
                    act.wait_ge(t_done.sem, t_done.now(t, k + 1))
                    w, b = (qw[:, 0:1], qw[:, 1:2]) if k < 4 else (vecs[:, 12:13], vecs[:, 13:14])
                    act.activation(qkT[:, 4 * k:4 * k + 4, :].rearrange("p h t -> p (h t)"), banks[TB[k]][:, :],
                                   ACT.Identity, scale=w, bias=b).then_inc(t_copied.sem, 1)

            def tile(i, one, two):
                act.wait_ge(sub_done.sem, sub_done.now(i, 1))
                act.activation(pr[:], sc[:], ACT.Exp).then_inc(e_done.sem, 1)
                if one:
                    heads_rsqrt(i + 1)
                    values(i + 1)
                    heads_copy(i + 1)
                if two:
                    tokens(i + 2)

            tokens(0)
            heads_rsqrt(0)
            values(0)
            heads_copy(0)
            tokens(1)
            with act.Fori(0, tiles - 2) as i:
                tile(i, True, True)
            tile(tiles - 2, True, False)
            tile(tiles - 1, False, False)

        @block.gpsimd
        def _(pool):
            for s in (oq_sum, o_copied):
                s.prime(pool)

            def tile(i):
                pool.wait_ge(oq_steps.sem, oq_steps.now(i, 4))
                pool.tensor_tensor(qa[:], qb[:], qm[:], ALU.add).then_inc(oq_sum.sem, 1)
                pool.wait_ge(oq_sum.sem, oq_sum.now(i, 1))
                pool.wait_ge(y_done.sem, y_done.before(i, 1))
                pool.tensor_tensor(oT[:].rearrange("p h t -> p (h t)"), qa[:], qm[:], ALU.subtract
                                   ).then_inc(o_copied.sem, 1)

            with pool.Fori(0, tiles) as i:
                tile(i)

        @block.vector
        def _(dve):
            ln.vector_setup(dve)
            for s in (lstats, xn_done, xq_done, p_copied, ss_done, qn_done, sub_done, pT_done, y_copied,
                      x_steps, sm_steps, oq_steps):
                s.prime(dve)
            dve.memset(eps[:], 1e-5)
            dve.wait_ge(weights, 16 * 5)
            step = [0]

            def then(ins):
                step[0] += 1
                ins.then_inc(setup, 1)
                dve.wait_ge(setup, step[0])

            wr = wqk[:].rearrange("p c (h e) -> p (c h) e", e=HD)
            then(dve.tensor_reduce(wmean[:], wr, AX.X, ALU.add))
            then(dve.tensor_scalar(wmean[:], wmean[:], 1.0 / HD, None, ALU.mult))
            then(dve.tensor_tensor(wr, wr, wmean[:].unsqueeze(2).to_broadcast([P, HC * NK, HD]), ALU.subtract))
            then(dve.reciprocal(inv_in[:], vecs[:, 4:10]))
            then(dve.reciprocal(inv_sm[:], smooth[:]))
            then(dve.tensor_scalar(qw[:], vecs[:, 10:12], SCALE, None, ALU.mult))
            then(dve.tensor_tensor(yscale[:], vecs[:, 17:18], vecs[:, 18:19], ALU.mult))
            dve.sem_inc(ready, 2)

            def tokens(t):
                Xt = X[:, t, :]
                dve.bn_stats(ln.stats[:, 0, :], Xt).then_inc(ln.summed.sem, 1)
                dve.wait_ge(ln.summed.sem, ln.summed.now(t, 1))
                dve.sem_inc(gate, 1)
                dve.bn_aggr(ln.mv[:, 0, :], ln.stats[:, 0, :]).then_inc(ln.aggregated.sem, 1)
                dve.wait_ge(ln.scaled.sem, ln.scaled.now(t, 1))
                dve.wait_ge(xt_done.sem, xt_done.before(t, 1))
                dve.tensor_scalar(ln.xn[:, 0, :], Xt, ln.mv[:, 0, 0:1], ln.lr[:], ALU.subtract, ALU.mult
                                  ).then_inc(ln.normed.sem, 1)
                dve.wait_ge(ln.normed.sem, ln.normed.now(t, 1))
                dve.bn_stats(ln.stats[:, 0, :], ln.xn[:, 0, :]).then_inc(x_steps.sem, 1)
                dve.wait_ge(x_steps.sem, x_steps.now(t, 1))
                dve.sem_inc(gate, 1)
                dve.bn_aggr(ln.mv[:, 0, :], ln.stats[:, 0, :]).then_inc(lstats.sem, 1)
                dve.wait_ge(lr_done.sem, lr_done.now(t, 1))
                dve.tensor_scalar(ln.xn[:, 0, :], ln.xn[:, 0, :], ln.mv[:, 0, 0:1], ln.lr[:], ALU.subtract, ALU.mult
                                  ).then_inc(xn_done.sem, 1)
                dve.wait_ge(xt_copied.sem, xt_copied.now(t, 1))
                for c in range(HC):
                    w = dve.tensor_scalar(lnT[:, c, :], lnT[:, c, :], vecs[:, c:c + 1], vecs[:, 2 + c:3 + c],
                                          ALU.mult, ALU.add)
                w.then_inc(x_steps.sem, 1)
                dve.wait_ge(x_steps.sem, x_steps.now(t, 2))
                N = KINDS * HC * P
                a, b, e, m = xa[:, 0:N], xb[:, 0:N], xe[:, 0:N], xm[:, 0:N]
                for k in range(KINDS * HC):
                    w = dve.tensor_scalar(xa[:, k * P:(k + 1) * P], lnT[:, k % HC, :], inv_in[:, k:k + 1], None,
                                          ALU.mult)
                w.then_inc(x_steps.sem, 1)
                dve.wait_ge(x_steps.sem, x_steps.now(t, 3))
                dve.tensor_scalar(b, a, FP8_MAX, -FP8_MAX, ALU.min, ALU.max).then_inc(x_steps.sem, 1)
                dve.wait_ge(x_steps.sem, x_steps.now(t, 4))
                dve.tensor_scalar(e.bitcast(U16), b.bitcast(U16), 0x7F80, None, ALU.bitwise_and
                                  ).then_inc(x_steps.sem, 1)
                dve.wait_ge(x_steps.sem, x_steps.now(t, 5))
                dve.tensor_scalar(m, e, FP8_SMALLEST, FP8_ROUND, ALU.max, ALU.mult).then_inc(x_steps.sem, 1)
                dve.wait_ge(x_steps.sem, x_steps.now(t, 6))
                dve.tensor_tensor(a, b, m, ALU.add).then_inc(x_steps.sem, 1)
                dve.wait_ge(x_steps.sem, x_steps.now(t, 7))
                dve.tensor_tensor(a, a, m, ALU.subtract).then_inc(x_steps.sem, 1)
                dve.wait_ge(x_steps.sem, x_steps.now(t, 8))
                dve.wait_ge(p_done.sem, p_done.before(t, 8))
                dve.tensor_tensor(xq[:], a.rearrange("p (k t) -> p k t", t=P),
                                  vecs[:, 4:10].unsqueeze(2).to_broadcast([P, KINDS * HC, P]), ALU.mult
                                  ).then_inc(xq_done.sem, 1)

            def copy_heads(t, k):
                if k == 0:
                    dve.wait_ge(t_done.sem, t_done.before(t, 6))
                dve.wait_ge(p_done.sem, p_done.now(t, k + 1))
                w = vecs[:, 14:15] if k < 4 else vecs[:, 15:16]
                dve.tensor_scalar(qk[:, 4 * k:4 * k + 4, :].rearrange("p h e -> p (h e)"), banks[PB[k]][:, :], w,
                                  None, ALU.mult).then_inc(p_copied.sem, 1)

            def sum_heads(t):
                dve.wait_ge(sq_done.sem, sq_done.now(t, 1))
                dve.tensor_reduce(ss[:], qksq[:], AX.X, ALU.add).then_inc(ss_done.sem, 1)

            def norm_heads(t):
                dve.wait_ge(rs_done.sem, rs_done.now(t, 1))
                dve.tensor_tensor(qk[:], qk[:], rs[:].unsqueeze(2).to_broadcast([P, NK, HD]), ALU.mult
                                  ).then_inc(qn_done.sem, 1)

            def shift_scores(t):
                sview = SB[:, :].rearrange("p (h k) -> p h k", h=NH)
                dve.wait_ge(s_done.sem, s_done.now(t, 1))
                dve.tensor_reduce(ntop[:], sview, AX.X, ALU.max, negate=True).then_inc(sm_steps.sem, 1)
                dve.wait_ge(sm_steps.sem, sm_steps.now(t, 1))
                dve.tensor_tensor(sc[:], sview, ntop[:].unsqueeze(2).to_broadcast([P, NH, S]), ALU.add
                                  ).then_inc(sub_done.sem, 1)

            def norm_probs(t):
                dve.wait_ge(e_done.sem, e_done.now(t, 1))
                dve.tensor_reduce(sums[:], pr[:], AX.X, ALU.add).then_inc(sm_steps.sem, 1)
                dve.wait_ge(sm_steps.sem, sm_steps.now(t, 2))
                dve.reciprocal(rsum[:], sums[:]).then_inc(sm_steps.sem, 1)
                dve.wait_ge(sm_steps.sem, sm_steps.now(t, 3))
                dve.tensor_tensor(pr[:], pr[:], rsum[:].unsqueeze(2).to_broadcast([P, NH, S]), ALU.mult
                                  ).then_inc(sm_steps.sem, 1)
                dve.wait_ge(sm_steps.sem, sm_steps.now(t, 4))
                dve.wait_ge(o_done.sem, o_done.before(t, 1))
                dve.transpose(prT[:].rearrange("p h k -> p (h k)"), pr[:].rearrange("p h k -> p (h k)")
                              ).then_inc(pT_done.sem, 1)

            def quantise_heads(t):
                wide = qa[:].rearrange("p (h t) -> p h t", h=NH)
                dve.wait_ge(o_done.sem, o_done.now(t, 1))
                dve.wait_ge(o_copied.sem, o_copied.before(t, 1))
                for b in range(BT):
                    w = dve.tensor_tensor(wide[:, :, b * S:(b + 1) * S], OB[b][:, :].rearrange("p (h q) -> p h q", h=NH),
                                          inv_sm[:].unsqueeze(2).to_broadcast([P, NH, S]), ALU.mult)
                w.then_inc(oq_steps.sem, 1)
                dve.wait_ge(oq_steps.sem, oq_steps.now(t, 1))
                dve.tensor_scalar(qb[:], qa[:], FP8_MAX, -FP8_MAX, ALU.min, ALU.max).then_inc(oq_steps.sem, 1)
                dve.wait_ge(oq_steps.sem, oq_steps.now(t, 2))
                dve.tensor_scalar(qe[:].bitcast(U16), qb[:].bitcast(U16), 0x7F80, None, ALU.bitwise_and
                                  ).then_inc(oq_steps.sem, 1)
                dve.wait_ge(oq_steps.sem, oq_steps.now(t, 3))
                dve.tensor_scalar(qm[:], qe[:], FP8_SMALLEST, FP8_ROUND, ALU.max, ALU.mult).then_inc(oq_steps.sem, 1)

            def copy_output(t):
                dve.wait_ge(y_done.sem, y_done.now(t, 1))
                dve.tensor_scalar(Yc[:, t, :], YB[:, 0:H], yscale[:], None, ALU.mult).then_inc(y_copied.sem, 1)

            def tile(i, one, two):
                shift_scores(i)
                if one:
                    copy_heads(i + 1, 0)
                norm_probs(i)
                if one:
                    for k in range(1, 6):
                        copy_heads(i + 1, k)
                    sum_heads(i + 1)
                    norm_heads(i + 1)
                quantise_heads(i)
                if two:
                    tokens(i + 2)
                copy_output(i)

            tokens(0)
            for k in range(6):
                copy_heads(0, k)
            sum_heads(0)
            norm_heads(0)
            tokens(1)
            with dve.Fori(0, tiles - 2) as i:
                tile(i, True, True)
            tile(tiles - 2, True, False)
            tile(tiles - 1, False, False)


def difference_attention(nc, d, X, ident, tiles):
    n = "a1_"
    NHA = 16
    HALVES = 2 * NHA
    DH = 8
    DV = 2 * DH
    NJ = HALVES // 4
    LAMBDA_INIT = 0.8 - 0.6 * math.exp(-0.3 * 12)
    with Part(nc) as ctx:
        def sb(name, shape, dt=F32):
            return ctx.enter_context(nc.sbuf_tensor(n + name, shape, dt))

        def sig(name, per, unit=1):
            return Signal(ctx, nc, n + name, per, unit)

        wqk = sb("wqk", [P, HC, 2 * NJ * P])
        wv = sb("wv", [P, HC, H])
        wo = sb("wo", [P, HC, H])
        lam = sb("lam", [P, 4, DH])
        lamp = sb("lamp", [P, 2, DH])
        lams = sb("lams", [P, 2])
        lame = sb("lame", [P, 2])
        nlam = sb("nlam", [P, 1])
        subw = sb("subw", [P, DV])
        qkT = sb("qkT", [P, 2 * NJ, P])
        vn = sb("vn", [P, H])
        ntop = sb("ntop", [P, 4, NJ])
        sc = sb("sc", [P, 4, NJ, S])
        pr = sb("pr", [P, 4, NJ, S])
        sums = sb("sums", [P, 4, NJ])
        rsum = sb("rsum", [P, 4, NJ])
        df = sb("df", [P, 2, NJ, S])
        dfT = sb("dfT", [P, 2, NJ, S])
        at = sb("at", [P, H])
        asq = sb("asq", [P, H])
        ass = sb("ass", [P, NHA])
        ars = sb("ars", [P, NHA])
        aT = sb("aT", [P, HC, P])
        eps = sb("eps", [P, 1])
        banks = [ctx.enter_context(nc.psum_tensor(f"{n}B{k}", [P, 512], F32)) for k in range(8)]
        ln = TokenNorm(ctx, nc, n, X, ident, pt=1)
        weights = ctx.semaphore(n + "weights")
        setup = ctx.semaphore(n + "setup_steps")
        lam_exp = ctx.semaphore(n + "lambda_exp")
        gate = ctx.semaphore(n + "gate")
        p_done = sig("projected", 5)
        p_copied = sig("projected_copied", 5)
        s_done = sig("scores_done", 1)
        sub_done = sig("scores_shifted", 1)
        e_done = sig("exp_done", 1)
        dT_done = sig("difference_transposed", 1)
        o_done = sig("heads_out", 1)
        a_sum = sig("squares_summed", 1)
        a_log = sig("squares_log", 1)
        a_rs = sig("heads_rsqrt", 1)
        a_done = sig("heads_normed", 1)
        aT_done = sig("heads_transposed", 1)
        aT_copied = sig("heads_copied", 1)
        y_done = sig("y_done", 1)
        x_added = sig("x_added", 1)
        dchain = Chain(ctx, nc, n + "dve_chain", 1 + 1 + 3 + 1 + 2 + 1)
        block = ctx.open_block()

        @block.sync
        def _(sp):
            for dst, src in ((wqk, d["wqk"].rearrange("(c p) n -> p c n", p=P)),
                             (wv, d["wv"].rearrange("(c p) n -> p c n", p=P)),
                             (wo, d["wo"].rearrange("(c p) n -> p c n", p=P)),
                             (lam, d["lam"]), (subw, d["subw"])):
                sp.dma_start(dst[:], src).then_inc(weights, 16)

        @block.tensor
        def _(pe):
            for s in (ln.turned, p_done, s_done, o_done, aT_done, y_done):
                s.prime(pe)
            pe.wait_ge(weights, 16 * 5)
            with pe.Fori(0, tiles) as i:
                pe.wait_ge(aT_copied.sem, aT_copied.before(i, 1))
                ln.tensor(pe, i, banks[5:7])
                pe.wait_ge(ln.copied.sem, ln.copied.now(i, HC))
                for k in range(4):
                    for j in range(4 * k, 4 * k + 4):
                        for c in range(HC):
                            m = pe.matmul(banks[k][:, j % 4 * P:(j % 4 + 1) * P], wqk[:, c, j * P:(j + 1) * P],
                                          ln.xnT[:, c, :], start=c == 0, stop=c == HC - 1)
                    m.then_inc(p_done.sem, 1)
                for c in range(HC):
                    m = pe.matmul(banks[4][:, 0:H], ln.xnT[:, c, :], wv[:, c, :], start=c == 0, stop=c == HC - 1)
                m.then_inc(p_done.sem, 1)
                pe.wait_ge(p_copied.sem, p_copied.now(i, 5))
                pe.sem_inc(gate, 1)
                for j in range(NJ):
                    for r in range(4):
                        for b in range(BT):
                            rows, tok = slice(32 * r, 32 * r + DH), slice(b * S, (b + 1) * S)
                            m = pe.matmul(banks[r][tok, j * S:(j + 1) * S], qkT[rows, j, tok], qkT[rows, NJ + j, tok],
                                          start=True, stop=True)
                m.then_inc(s_done.sem, 1)
                pe.wait_ge(dT_done.sem, dT_done.now(i, 1))
                pe.sem_inc(gate, 1)
                for h in range(NHA):
                    for b in range(BT):
                        tok = slice(b * S, (b + 1) * S)
                        m = pe.matmul(banks[b][tok, h * DV:(h + 1) * DV], dfT[tok, h % 2, h // 2, :],
                                      vn[tok, h * DV:(h + 1) * DV], start=True, stop=True)
                m.then_inc(o_done.sem, 1)
                pe.wait_ge(a_done.sem, a_done.now(i, 1))
                for c in range(HC):
                    m = pe.transpose(banks[5][:, c * P:(c + 1) * P], at[:, c * P:(c + 1) * P], ident[:])
                m.then_inc(aT_done.sem, 1)
                pe.wait_ge(aT_copied.sem, aT_copied.now(i, 1))
                pe.wait_ge(x_added.sem, x_added.before(i, 1))
                for c in range(HC):
                    m = pe.matmul(banks[7][:, 0:H], aT[:, c, :], wo[:, c, :], start=c == 0, stop=c == HC - 1)
                m.then_inc(y_done.sem, 1)

        @block.scalar
        def _(act):
            ln.scalar_setup(act)
            for s in (p_copied, e_done, a_log, a_rs, aT_copied):
                s.prime(act)
            act.preload_act_table_set(EXPLN)
            act.wait_ge(setup, 2)
            act.activation(lame[:], lams[:], ACT.Exp).then_inc(lam_exp, 1)
            with act.Fori(0, tiles) as i:
                ln.scalar_rsqrt(act, i)
                act.wait_ge(p_done.sem, p_done.before(i, 5))
                ln.scalar_copy(act, i, banks[5:7])
                act.wait_ge(s_done.sem, s_done.before(i, 1))
                for k in range(4):
                    act.wait_ge(p_done.sem, p_done.now(i, k + 1))
                    act.activation(qkT[:, 4 * k:4 * k + 4, :].rearrange("p j t -> p (j t)"), banks[k][:, :], ACT.Copy
                                   ).then_inc(p_copied.sem, 1)
                act.wait_ge(p_done.sem, p_done.now(i, 5))
                act.wait_ge(o_done.sem, o_done.before(i, 1))
                act.activation(vn[:], banks[4][:, 0:H], ACT.Copy).then_inc(p_copied.sem, 1)
                act.wait_ge(sub_done.sem, sub_done.now(i, 1))
                act.activation(pr[:], sc[:], ACT.Exp, scale=DH ** -0.5).then_inc(e_done.sem, 1)
                act.wait_ge(a_sum.sem, a_sum.now(i, 1))
                act.activation(ars[:], ass[:], ACT.Ln, bias=eps[:], scale=1.0 / DV).then_inc(a_log.sem, 1)
                act.wait_ge(a_log.sem, a_log.now(i, 1))
                act.activation(ars[:], ars[:], ACT.Exp, scale=-0.5).then_inc(a_rs.sem, 1)
                act.wait_ge(aT_done.sem, aT_done.now(i, 1))
                act.wait_ge(y_done.sem, y_done.before(i, 1))
                act.activation(aT[:].rearrange("p c t -> p (c t)"), banks[5][:, 0:H], ACT.Copy
                               ).then_inc(aT_copied.sem, 1)

        @block.vector
        def _(dve):
            ln.vector_setup(dve)
            for s in (sub_done, dT_done, a_sum, a_done, x_added, dchain):
                s.prime(dve)
            dve.memset(eps[:], 1e-5)
            dve.wait_ge(weights, 16 * 5)
            step = [0]

            def then(ins):
                step[0] += 1
                ins.then_inc(setup, 1)
                dve.wait_ge(setup, step[0])

            then(dve.tensor_tensor(lamp[:], lam[:, 0:4:2, :], lam[:, 1:4:2, :], ALU.mult))
            then(dve.tensor_reduce(lams[:], lamp[:], AX.X, ALU.add))
            dve.wait_ge(lam_exp, 1)
            then(dve.tensor_tensor(nlam[:], lame[:, 1:2], lame[:, 0:1], ALU.subtract))
            then(dve.tensor_scalar(nlam[:], nlam[:], LAMBDA_INIT, None, ALU.subtract))
            then(dve.tensor_scalar(subw[:], subw[:], 1.0 - LAMBDA_INIT, None, ALU.mult))

            def link(i, ins):
                ins.then_inc(dchain.sem, 1)
                dve.wait_ge(dchain.sem, dchain.next(i))

            with dve.Fori(0, tiles) as i:
                dchain.k = 0
                ln.vector(dve, i)
                dve.wait_ge(s_done.sem, s_done.now(i, 1))
                for r in range(4):
                    view = banks[r][:, 0:NJ * S].rearrange("p (j k) -> p j k", j=NJ)
                    a = dve.tensor_reduce(ntop[:, r, :], view, AX.X, ALU.max, negate=True)
                link(i, a)
                for r in range(4):
                    view = banks[r][:, 0:NJ * S].rearrange("p (j k) -> p j k", j=NJ)
                    a = dve.tensor_tensor(sc[:, r, :, :], view, ntop[:, r, :].unsqueeze(2).to_broadcast([P, NJ, S]),
                                          ALU.add)
                a.then_inc(sub_done.sem, 1)
                dve.wait_ge(e_done.sem, e_done.now(i, 1))
                rows = lambda t: t[:].rearrange("p r j -> p (r j)")
                wide = pr[:].rearrange("p r j k -> p (r j) k")
                link(i, dve.tensor_reduce(rows(sums), wide, AX.X, ALU.add))
                link(i, dve.reciprocal(rows(rsum), rows(sums)))
                link(i, dve.tensor_scalar(rsum[:, 1:4:2, :], rsum[:, 1:4:2, :], nlam[:], None, ALU.mult))
                link(i, dve.tensor_tensor(wide, wide, rows(rsum).unsqueeze(2).to_broadcast([P, 4 * NJ, S]), ALU.mult))
                for e in range(2):
                    a = dve.tensor_tensor(df[:, e, :, :], pr[:, 2 * e, :, :], pr[:, 2 * e + 1, :, :], ALU.add)
                link(i, a)
                dve.wait_ge(o_done.sem, o_done.before(i, 1))
                dve.transpose(dfT[:].rearrange("p e j k -> p (e j k)"), df[:].rearrange("p e j k -> p (e j k)")
                              ).then_inc(dT_done.sem, 1)
                dve.wait_ge(o_done.sem, o_done.now(i, 1))
                dve.wait_ge(aT_done.sem, aT_done.before(i, 1))
                for b in range(BT):
                    tok = slice(b * S, (b + 1) * S)
                    a = dve.tensor_copy(at[tok, :], banks[b][tok, 0:H])
                link(i, a)
                link(i, dve.tensor_tensor(asq[:], at[:], at[:], ALU.mult))
                heads = lambda t: t[:].rearrange("p (h e) -> p h e", h=NHA)
                dve.tensor_reduce(ass[:], heads(asq), AX.X, ALU.add).then_inc(a_sum.sem, 1)
                dve.wait_ge(a_rs.sem, a_rs.now(i, 1))
                link(i, dve.tensor_tensor(heads(at), heads(at), ars[:].unsqueeze(2).to_broadcast([P, NHA, DV]), ALU.mult))
                dve.tensor_tensor(heads(at), heads(at), subw[:].unsqueeze(1).to_broadcast([P, NHA, DV]), ALU.mult
                                  ).then_inc(a_done.sem, 1)
                dve.wait_ge(y_done.sem, y_done.now(i, 1))
                dve.tensor_tensor(X[:, i, :], X[:, i, :], banks[7][:, 0:H], ALU.add).then_inc(x_added.sem, 1)
                dchain.done()


def hadamard_ffn(nc, d, X, ident, tiles):
    n = "f1_"
    F = 1024
    FC = F // P
    GUARD = 64.0
    passes = tiles // PT
    N = PT * P
    with Part(nc) as ctx:
        def sb(name, shape, dt=F32):
            return ctx.enter_context(nc.sbuf_tensor(n + name, shape, dt))

        def bank(name):
            return ctx.enter_context(nc.psum_tensor(n + name, [P, 512], F32))

        def sig(name, per, unit=1):
            return Signal(ctx, nc, n + name, per, unit)

        raw = sb("raw", [P, HC, 2 * F])
        rawd = sb("rawd", [P, FC, H])
        wug = sb("wug", [P, HC, 2 * F])
        wd = sb("wd", [P, FC, H])
        had = sb("had", [P, 2, P])
        cols = sb("cols", [P, HC + FC + 2 * FC])
        wsd = sb("wsd", [P, H])
        su = sb("su", [P, HC])
        sd = sb("sd", [P, FC])
        su64 = sb("su64", [P, 2 * FC])
        g1 = sb("g1", [P, 2, N])
        gT = sb("gT", [P, FC, N])
        Ab = [bank("A0"), bank("A1")]
        Bb = [bank("B0"), bank("B1")]
        Yb = [bank("Y0"), bank("Y1")]
        Tb = [bank("T0"), bank("T1")]
        ln = TokenNorm(ctx, nc, n, X, ident)
        weights = ctx.semaphore(n + "weights")
        folded = ctx.semaphore(n + "folded")
        fold_read = ctx.semaphore(n + "fold_read")
        scales = ctx.semaphore(n + "scales")
        h_done = sig("hidden_done", 2 * FC)
        h_silu = sig("hidden_silu", FC)
        g_done = sig("gated", FC)
        y_done = sig("y_done", 2)
        x_added = sig("x_added", 2)
        FOLDS = HC * 4 + FC
        block = ctx.open_block()

        @block.sync
        def _(sp):
            for dst, src in ((had, d["had"]), (raw, d["raw"].rearrange("(c p) n -> p c n", p=P)),
                             (rawd, d["rawd"].rearrange("(c p) n -> p c n", p=P)),
                             (cols, d["cols"]), (wsd, d["wsd"])):
                sp.dma_start(dst[:], src).then_inc(weights, 16)

        @block.tensor
        def _(pe):
            for s in (ln.turned, h_done, y_done):
                s.prime(pe)
            pe.wait_ge(weights, 16 * 5)
            for f in range(FOLDS):
                if f >= 2:
                    pe.wait_ge(fold_read, f - 1)
                if f < HC * 4:
                    a, k = f // 4, f % 4
                    for c in range(HC):
                        m = pe.matmul(Ab[f % 2][:, :], had[:, a & c, :], raw[:, c, k * 512:(k + 1) * 512],
                                      start=c == 0, stop=c == HC - 1)
                else:
                    a = f - HC * 4
                    for c in range(FC):
                        m = pe.matmul(Ab[f % 2][:, 0:H], had[:, bin(a & c).count("1") % 2, :], rawd[:, c, :],
                                      start=c == 0, stop=c == FC - 1)
                m.then_inc(folded, 1)
            pe.wait_ge(fold_read, FOLDS)
            with pe.Fori(0, passes) as i:
                ln.tensor(pe, i, Tb)
                pe.wait_ge(ln.copied.sem, ln.copied.now(i, HC))
                for k in range(FC):
                    pe.wait_ge(g_done.sem, g_done.after(i, k - 1))
                    for w, b in ((F, Ab), (0, Bb)):
                        for c in range(HC):
                            m = pe.matmul(b[k % 2][:, :], wug[:, c, w + k * P:w + (k + 1) * P], ln.xnT[:, c, :],
                                          start=c == 0, stop=c == HC - 1)
                        m.then_inc(h_done.sem, 1)
                pe.wait_ge(g_done.sem, g_done.now(i, FC))
                for y in range(2):
                    pe.wait_ge(x_added.sem, x_added.before(i, y + 1))
                    for t in (2 * y, 2 * y + 1):
                        for k in range(FC):
                            m = pe.matmul(Yb[y][:, t % 2 * H:t % 2 * H + H], gT[:, k, t * P:(t + 1) * P], wd[:, k, :],
                                          start=k == 0, stop=k == FC - 1)
                    m.then_inc(y_done.sem, 1)

        @block.scalar
        def _(act):
            ln.scalar_setup(act)
            h_silu.prime(act)
            act.wait_ge(scales, 4)
            with act.Fori(0, passes) as i:
                ln.scalar_rsqrt(act, i)
                act.wait_ge(h_done.sem, h_done.before(i, 2 * FC))
                ln.scalar_copy(act, i, Tb)
                for k in range(FC):
                    act.wait_ge(h_done.sem, h_done.now(i, 2 * k + 1))
                    act.wait_ge(g_done.sem, g_done.after(i, k - 1))
                    act.activation(g1[:, k % 2, :], Ab[k % 2][:, :], ACT.Silu, scale=su64[:, FC + k:FC + k + 1]
                                   ).then_inc(h_silu.sem, 1)

        @block.vector
        def _(dve):
            ln.vector_setup(dve)
            for s in (g_done, x_added):
                s.prime(dve)
            dve.wait_ge(weights, 16 * 5)
            dve.tensor_scalar(su[:], cols[:, 0:HC], 1.0 / (H ** 0.5 * GUARD), None, ALU.mult).then_inc(scales, 1)
            dve.tensor_scalar(sd[:], cols[:, HC:HC + FC], 1.0 / (F ** 0.5 * GUARD), None, ALU.mult
                              ).then_inc(scales, 1)
            dve.tensor_scalar(su64[:], cols[:, HC + FC:], GUARD, None, ALU.mult).then_inc(scales, 1)
            dve.tensor_scalar(wsd[:], wsd[:], GUARD, None, ALU.mult).then_inc(scales, 1)
            dve.wait_ge(scales, 4)
            for f in range(FOLDS):
                dve.wait_ge(folded, f + 1)
                if f < HC * 4:
                    a, k = f // 4, f % 4
                    m = dve.tensor_scalar(wug[:, a, k * 512:(k + 1) * 512], Ab[f % 2][:, :], su[:, a:a + 1], None,
                                          ALU.mult)
                else:
                    a = f - HC * 4
                    m = dve.scalar_tensor_tensor(wd[:, a, :], Ab[f % 2][:, 0:H], sd[:, a:a + 1], wsd[:],
                                                 ALU.mult, ALU.mult)
                m.then_inc(fold_read, 1)
            with dve.Fori(0, passes) as i:
                ln.vector(dve, i)
                for k in range(FC):
                    dve.wait_ge(h_silu.sem, h_silu.now(i, k + 1))
                    dve.wait_ge(h_done.sem, h_done.now(i, 2 * k + 2))
                    if k == 0:
                        dve.wait_ge(y_done.sem, y_done.before(i, 2))
                    dve.scalar_tensor_tensor(gT[:, k, :], Bb[k % 2][:, :], su64[:, k:k + 1], g1[:, k % 2, :],
                                             ALU.mult, ALU.mult).then_inc(g_done.sem, 1)
                for y in range(2):
                    dve.wait_ge(y_done.sem, y_done.now(i, y + 1))
                    for t in (2 * y, 2 * y + 1):
                        Xt = X[:, i * PT + t, :]
                        a = dve.tensor_tensor(Xt, Xt, Yb[y][:, t % 2 * H:t % 2 * H + H], ALU.add)
                    a.then_inc(x_added.sem, 1)


def build(nc, d, out, n_batches):
    tiles = n_batches // BT
    with ExitStack() as ctx:
        X = ctx.enter_context(nc.sbuf_tensor("X", [P, tiles, H], F32))
        Yc = ctx.enter_context(nc.sbuf_tensor("Yc", [P, tiles, H], F32))
        ident = ctx.enter_context(nc.sbuf_tensor("ident", [P, P], F32))
        loaded = ctx.enter_context(nc.semaphore("loaded"))
        stored = ctx.enter_context(nc.semaphore("stored"))
        x_rows = d["x"].rearrange("(t b) s c -> (b s) t c", b=BT)
        out_rows = out.rearrange("(t b) s c -> (b s) t c", b=BT)
        with nc.Block() as block:
            @block.sync
            def _(sp):
                sp.dma_start(X[:], x_rows).then_inc(loaded, 16)
                sp.dma_start(ident[:], d["ident"]).then_inc(loaded, 16)
                sp.wait_ge(loaded, 32)
        cross_attention(nc, sub(d, "x0_"), X, Yc, ident, 0, tiles)
        product_attention(nc, sub(d, "a0_"), X, ident, tiles)
        experts(nc, sub(d, "e0_"), X, ident, tiles)
        core_attention(nc, sub(d, "c1_"), X, Yc, ident, tiles)
        cross_attention(nc, sub(d, "x1_"), X, Yc, ident, 1, tiles)
        difference_attention(nc, sub(d, "a1_"), X, ident, tiles)
        hadamard_ffn(nc, sub(d, "f1_"), X, ident, tiles)
        with nc.Block() as block:
            @block.sync
            def _(sp):
                sp.dma_start(out_rows, X[:]).then_inc(stored, 16)
                sp.wait_ge(stored, 16)


def sub(d, prefix):
    got = {k[len(prefix):]: v for k, v in d.items() if k.startswith(prefix)}
    got["ctx"] = d["ctx"]
    return got


def lay_out(inputs):
    import numpy as np
    g = {k: np.asarray(v) for k, v in inputs.items()}
    T = lambda a: np.ascontiguousarray(a.T)
    rows = lambda a, n=128: np.ascontiguousarray(np.broadcast_to(a, (n,) + a.shape))
    col = lambda a: np.ascontiguousarray(a.reshape(-1, 128).T)
    one = lambda a: np.ascontiguousarray(np.broadcast_to(a.reshape(1, 1), (128, 1)))
    a = {"x": g["x"], "ctx": g["ctx_2048"], "ident": np.eye(128, dtype=np.float32)}
    a["x0_wq"], a["x0_wk"], a["x0_wv"], a["x0_wo"] = (g["L0_xattn_" + w] for w in ("Wq", "Wk", "Wv", "Wo"))
    a["x0_bq"] = rows(g["L0_xattn_bq"])
    a["x0_bkv"] = np.stack([col(g["L0_xattn_bk"]), col(g["L0_xattn_bv"])], 1)
    a["x0_nw"] = np.stack([g["L0_xattn_qn_w"], g["L0_xattn_kn_w"]], 1)
    a["x0_mask"] = np.tile(g["mask_1xSxS2_ff0"][0], (4, 1))
    wkv = g["L1_xattn_w_kv_x"]
    a["x1_wq"], a["x1_wk"], a["x1_wv"] = T(g["L1_xattn_wqx"]), T(wkv[0:1024]), T(wkv[1024:2048])
    a["x1_wo"] = T(g["L1_xattn_wproj"][:, 2048:4096])
    a["x1_smooth"] = col(g["L1_xattn_proj_smooth"][2048:4096])
    a["x1_vecs"] = np.concatenate(
        [col(g["L1_xattn_ln_w"]), col(g["L1_xattn_ln_b"]), col(g["L1_xattn_qx_in_scale"]),
         col(g["L1_xattn_qxln_w"]), col(g["L1_xattn_qxln_b"]), col(g["L1_xattn_kxln_w"]), col(g["L1_xattn_kxln_b"]),
         one(g["L1_xattn_wqx_scale"]), one(g["L1_xattn_proj_in_scale"]), one(g["L1_xattn_proj_w_scale"]),
         np.zeros((128, 11), np.float32)], 1)
    def slots(w):
        out = np.zeros((16, 32, w.shape[1]), np.float32)
        out[:, 0:16] = w.reshape(16, 16, -1)
        return out.reshape(512, -1)
    a["a0_wq"], a["a0_kT"] = T(slots(g["L0_attn_Wq"])), slots(T(g["L0_attn_k_weight"])).reshape(4, 128, 512)
    a["a0_vw"], a["a0_wg"] = T(slots(T(g["L0_attn_v_weight"]))), T(slots(g["L0_attn_Wg"]))
    a["a0_wo"] = slots(T(g["L0_attn_Wout"]))
    for w in ("w1", "w3"):
        a["e0_" + w] = T(np.concatenate([g["L0_ffn_" + w].reshape(1024, 256), g["L0_ffn_ws" + w[1]]]))
    a["e0_w2"] = np.concatenate([g["L0_ffn_w2"].transpose(0, 2, 1).reshape(1024, 256), g["L0_ffn_ws2"].T])
    a["e0_wr"] = T(g["L0_ffn_gate_w"])
    a["e0_places"] = rows(np.arange(8, dtype=np.float32))
    a["c1_wqk"] = T(np.concatenate([g["L1_xattn_wq"], g["L1_xattn_wk"]]))
    a["c1_wv"], a["c1_wo"] = T(g["L1_xattn_wv"]), T(g["L1_xattn_wproj"][:, 0:2048])
    a["c1_smooth"] = col(g["L1_xattn_proj_smooth"][0:2048])
    a["c1_vecs"] = np.concatenate(
        [col(g["L1_xattn_" + k]) for k in ("ln_w", "ln_b", "q_in_scale", "k_in_scale", "v_in_scale",
                                           "qln_w", "qln_b", "kln_w", "kln_b")]
        + [one(g["L1_xattn_" + k]) for k in ("wq_scale", "wk_scale", "wv_scale", "proj_in_scale", "proj_w_scale")]
        + [np.zeros((128, 1), np.float32)], 1)
    def half_slots(w):
        out = np.zeros((32, 32, 256), np.float32)
        out[:, 0:8] = w.reshape(32, 8, 256)
        return T(out.reshape(1024, 256))
    a["a1_wqk"] = np.concatenate([half_slots(g["L1_attn_wq"]), half_slots(g["L1_attn_wk"])], 1)
    a["a1_wv"], a["a1_wo"] = T(g["L1_attn_wv"]), T(g["L1_attn_wo"])
    a["a1_lam"] = rows(np.stack([g["L1_attn_lambda_" + k] for k in ("q1", "k1", "q2", "k2")]))
    a["a1_subw"] = rows(g["L1_attn_subln_w"])
    had = np.ones((1, 1), np.float32)
    while len(had) < 128:
        had = np.block([[had, had], [had, -had]])
    a["f1_had"] = np.stack([had, -had], 1)
    a["f1_raw"] = np.concatenate([T(g["L1_ffn_W_up"]), T(g["L1_ffn_W_gate"])], 1)
    a["f1_rawd"] = T(g["L1_ffn_W_down"])
    a["f1_cols"] = np.concatenate([col(g["L1_ffn_SU_ug"]), col(g["L1_ffn_SU_dp"]), col(g["L1_ffn_Wscale_ug"])], 1)
    a["f1_wsd"] = rows(g["L1_ffn_Wscale_dp"])
    return {k: np.ascontiguousarray(v) for k, v in a.items()}


def kernel(**inputs):
    import concourse.bacc as bacc
    from concourse.bass_utils import run_bass_kernel_spmd as run

    arrays = lay_out(inputs)
    nc = bacc.Bacc("TRN2", target_bir_lowering=False, num_devices=1)
    d = {k: nc.dram_tensor("in_" + k, v.shape, mybir.dt.from_np(v.dtype), kind="ExternalInput").ap()
         for k, v in arrays.items()}
    shape = inputs["x"].shape
    out = nc.dram_tensor("out_x", tuple(shape), F32, kind="ExternalOutput").ap()
    build(nc, d, out, shape[0])
    r = run(nc, [{"in_" + k: v for k, v in arrays.items()}], core_ids=[0])
    return r.results[0]["out_x"]
```

```python
import math
from contextlib import ExitStack

import concourse.bass as bass
from concourse import mybir

F32 = mybir.dt.float32
BF16 = mybir.dt.bfloat16
U16 = mybir.dt.uint16
U32 = mybir.dt.uint32
I32 = mybir.dt.int32
ALU = mybir.AluOpType
ACT = mybir.ActivationFunctionType
AX = mybir.AxisListType

P = 128
H = 256
HC = H // P
S = 32
SE = 257
BT = P // S
HD = 128
NH = 16
UNITS = NH // 4
EXPLN = "natural_log_exp_and_others"
FP8_MAX = 448.0
FP8_SMALLEST = 2.0 ** -6
FP8_ROUND = 1.5 * 2.0 ** 20


class Part(ExitStack):

    def __init__(self, nc):
        super().__init__()
        self.nc, self.sems = nc, []

    def semaphore(self, name):
        self.sems.append(self.enter_context(self.nc.semaphore(name)))
        return self.sems[-1]

    def open_block(self):
        self.callback(self.clear)
        return self.enter_context(self.nc.Block())

    def clear(self):
        with self.nc.Block() as block:
            @block.gpsimd
            def _(pool):
                for s in self.sems:
                    pool.sem_clear(s)


class Signal:

    def __init__(self, ctx, nc, name, per, unit=1):
        self.sem = ctx.semaphore(name)
        self.per, self.unit, self.name = per, unit, name

    def prime(self, eng):
        eng.sem_inc(self.sem, self.per * self.unit)

    def now(self, i, k):
        assert 1 <= k <= self.per, (self.name, k, self.per)
        return i * (self.per * self.unit) + (self.per + k) * self.unit

    def before(self, i, k):
        assert 1 <= k <= self.per, (self.name, k, self.per)
        return i * (self.per * self.unit) + k * self.unit

    def after(self, i, k):
        return self.now(i, k) if k >= 1 else self.before(i, k + self.per)


class Chain(Signal):

    k = 0

    def next(self, i):
        self.k += 1
        return self.now(i, self.k)

    def done(self):
        assert self.k == self.per, (self.name, self.k)


def cross_attention(nc, d, X, Yc, ident, layer, tiles):
    L1 = layer == 1
    G = 8 if L1 else 4
    GU = G // UNITS
    SUBS = UNITS * BT * GU
    NU = UNITS * BT
    KW = SE + 1 if L1 else SE
    MG = P // GU
    SCALE = HD ** -0.5
    EPS = 1e-5 if L1 else 1e-6
    CW = [P, P, SE - 2 * P]
    n = f"x{layer}_"

    with Part(nc) as ctx:
        def sb(name, shape, dt=F32):
            return ctx.enter_context(nc.sbuf_tensor(n + name, shape, dt))

        def bank(name):
            return ctx.enter_context(nc.psum_tensor(n + name, [P, 512], F32))

        def sig(name, per, unit=1):
            return Signal(ctx, nc, n + name, per, unit)

        wq = sb("wq", [P, HC, NH * HD])
        wk = sb("wk", [P, HC, G * HD])
        wv = sb("wv", [P, HC, G * HD])
        wo = sb("wo", [P, NH, H])
        ones = sb("ones", [P, P])
        eps_ln = sb("eps_ln", [P, 1])
        eps_h = sb("eps_h", [P, 1])
        qscale = sb("qscale", [P, 1])
        if L1:
            vecs = sb("vecs", [P, 24])
            inv_in = sb("inv_in", [P, HC])
            smooth = sb("smooth", [P, NH])
            inv_sm = sb("inv_sm", [P, NH])
            qbias = sb("qbias", [P, 1])
            wmean = sb("wmean", [P, HC, NH])
            yscale = sb("yscale", [P, 1])
            lnT = sb("lnT", [P, HC, P])
        else:
            bq = sb("bq", [P, NH * HD])
            bkv = sb("bkv", [P, 2, G])
            nw = sb("nw", [P, 2])
            mask = sb("mask", [P, SE])
        stats = sb("stats", [P, 6])
        mv = sb("mv", [P, 2])
        lr = sb("lr", [P, 1])
        xn = sb("xn", [P, H])
        xnT = sb("xnT", [P, HC, P])
        qn = sb("qn", [P, NH, HD])
        qsq = sb("qsq", [P, 4, HD])
        qss = sb("qss", [P, NH])
        qr = sb("qr", [P, NH])
        qTn = sb("qTn", [P, BT, NH, S])
        qT = sb("qT", [P, BT, NH, S])
        cn = sb("cn", [P, BT, 3, H])
        cT = sb("cT", [P, 2, HC, SE])
        sq = sb("sq", [P, 2 * GU, SE])
        rs = sb("rs", [P, 2 * GU, SE])
        kT = sb("kT", [P, 4, GU, KW])
        pr = sb("pr", [P, 4, SE])
        top = sb("top", [P, NU])
        ntop = sb("ntop", [P, NU])
        ps = sb("ps", [P, NU])
        rps = sb("rps", [P, NU])
        pT = sb("pT", [P, 2, 3, UNITS * P])
        pcT = sb("pcT", [P, HC, UNITS * P])
        oT = sb("oT", [P, NH, P])
        if L1:
            qa = sb("qa", [P, NH * S])
            qb = sb("qb", [P, NH * S], BF16)
            qe = sb("qe", [P, NH * S], BF16)
            qm = sb("qm", [P, NH * S])
            ysum = sb("ysum", [P, H])
        else:
            sm = sb("sm", [P, 2, SE])

        Kb = [bank("Kb0"), bank("Kb1")]
        SSb = bank("SSb")
        Sb = bank("Sb")
        PTb = bank("PTb")
        Lb = bank("Lb")
        PC = [bank("PC0"), bank("PC1")]
        QB = [PC[1], PC[0], PC[1], PC[0]]
        TB = [PC[1], PC[1], PC[0], PC[1]]

        weights = ctx.semaphore(n + "weights")
        key_weights = ctx.semaphore(n + "key_weights")
        late_weights = ctx.semaphore(n + "late_weights")
        ready = ctx.semaphore(n + "constants_ready")
        setup = ctx.semaphore(n + "setup_steps")
        gate = ctx.semaphore(n + "gate")
        ctx_in = [sig(f"context_loaded{b}", 1, 16 * 2) for b in range(BT)]
        NLN = 2 if L1 else 1
        ln_sum = sig("ln_stats", NLN)
        ln_agg = sig("ln_aggregated", NLN)
        ln_log = sig("ln_log", NLN)
        ln_rs = sig("ln_rsqrt", NLN)
        x_mid = sig("x_normed_once", 1)
        xn_done = sig("xn_done", 1)
        xt_done = sig("xt_transposed", 1)
        xt_copied = sig("xt_copied", 1)
        xq_steps = sig("x_quantise_steps", 7)
        xq_done = sig("xq_done", 1)
        q_done = sig("q_projected", 4)
        q_in = sig("q_copied", 4)
        q_sq = sig("q_squared", 4)
        q_sum = sig("q_summed", 4)
        q_log = sig("q_log", 4)
        q_rs = sig("q_rsqrt", 4)
        qn_done = sig("q_normed", 4)
        qt_done = sig("q_transposed", 4)
        qt_copied = sig("qTn_copied", 4)
        qT_ready = sig("qT_ready", BT)
        ct_done = sig("ctx_transposed", BT)
        ct_copied = sig("ctxT_copied", BT)
        k_done = sig("k_projected", SUBS)
        k_sq = sig("k_squared", SUBS)
        k_raw = sig("k_copied", SUBS)
        ss_done = sig("k_summed", SUBS)
        k_log = sig("k_log", SUBS)
        k_rs = sig("k_rsqrt", SUBS)
        kt_done = sig("kT_normed", SUBS)
        s_done = sig("scores_done", NU)
        top_found = sig("max_found", NU)
        top_done = sig("max_negated", NU)
        e_done = sig("exp_done", NU)
        r_done = sig("sum_inverted", NU)
        pn_done = sig("probs_normed", NU)
        pt_done = sig("probs_transposed", NU)
        pt_copied = sig("pT_copied", NU)
        pl_copied = sig("pT_last_copied", BT)
        pc_done = sig("pc_done", BT * HC)
        pc_copied = sig("pcT_copied", BT * HC)
        o_done = sig("out_heads_done", BT)
        o_read = sig("out_heads_read", BT)
        oq_steps = sig("out_quantise_steps", 4 * BT)
        o_copied = sig("oT_copied", BT)
        pc0_read = o_read if L1 else o_copied
        y_done = sig("y_done", 1)
        y_summed = sig("y_summed", 1)
        x_added = sig("x_added", 1)

        def lagging(i, u, lag, cur, prev):
            if u >= lag:
                return [(i, u - lag)] if cur and u - lag < NU else []
            return [(i - 1, u - lag + NU)] if prev else []

        def batch_at(i, u, lag, cur, prev):
            if u % UNITS != lag % UNITS:
                return []
            if u >= lag:
                return [(i, (u - lag) // UNITS)] if cur else []
            return [(i - 1, (u - lag) // UNITS + BT)] if prev else []

        def run(eng, tile):
            tile(0, True, False, True)
            with eng.Fori(1, tiles - 1) as i:
                tile(i, True, True, True)
            tile(tiles - 1, True, True, False)
            tile(tiles, False, True, False)

        def steps(cur):
            return range(NU if cur else 8)

        block = ctx.open_block()

        @block.sync
        def _(sp):
            sp.dma_start(wq[:], d["wq"].rearrange("(c p) n -> p c n", p=P)).then_inc(weights, 16)
            if L1:
                loads = [(vecs, d["vecs"]), (smooth, d["smooth"])]
            else:
                loads = [(bkv, d["bkv"]), (nw, d["nw"]), (bq, d["bq"]), (mask, d["mask"])]
                sp.dma_start(wk[:], d["wk"].rearrange("(c p) n -> p c n", p=P)).then_inc(key_weights, 16)
            for dst, src in loads:
                sp.dma_start(dst[:], src).then_inc(weights, 16)
            if L1:
                sp.dma_start(wk[:], d["wk"].rearrange("(c p) n -> p c n", p=P)).then_inc(key_weights, 16)
            sp.dma_start(wv[:], d["wv"].rearrange("(c p) n -> p c n", p=P)).then_inc(late_weights, 16)
            sp.dma_start(wo[:], d["wo"].rearrange("(h p) n -> p h n", p=P)).then_inc(late_weights, 16)
            for s in ctx_in:
                s.prime(sp)
            with sp.Fori(0, tiles) as i:
                for b in range(BT):
                    sp.wait_ge(pc_done.sem, pc_done.before(i, HC * (b + 1)))
                    src = d["ctx"][i * BT + b]
                    sp.dma_start(cn[:, b, 0:2, :], src[0:2 * P, :].rearrange("(c p) n -> p c n", p=P)
                                 ).then_inc(ctx_in[b].sem, 16)
                    sp.dma_start(cn[0:1, b, 2, :], src[2 * P:SE, :]).then_inc(ctx_in[b].sem, 16)

        NLOADS = 3 if L1 else 5

        @block.tensor
        def _(pe):
            for s in (xt_done, q_done, qt_done, ct_done, k_done, ss_done, s_done, pt_done, pc_done, o_done, y_done):
                s.prime(pe)
            pe.wait_ge(weights, 16 * NLOADS)
            pe.wait_ge(ready, 1)

            def transpose_tokens(t):
                pe.wait_ge(xn_done.sem, xn_done.now(t, 1))
                for c in range(HC):
                    m = pe.transpose(PC[1][:, c * P:(c + 1) * P], xn[:, c * P:(c + 1) * P], ident[:])
                m.then_inc(xt_done.sem, 1)

            def project_query(t, k):
                if k == 0:
                    x_ready = xq_done if L1 else xt_copied
                    pe.wait_ge(x_ready.sem, x_ready.now(t, 1))
                if k >= 2:
                    pe.wait_ge(q_in.sem, q_in.now(t, k - 1))
                for c in range(HC):
                    m = pe.matmul(QB[k][:, :], xnT[:, c, :], wq[:, c, k * 512:(k + 1) * 512],
                                  start=c == 0, stop=c == HC - 1)
                m.then_inc(q_done.sem, 1)

            def transpose_query(t, k):
                pe.wait_ge(qn_done.sem, qn_done.now(t, k + 1))
                pe.wait_ge(q_in.sem, q_in.now(t, 3 if k < 2 else 4))
                if k in (1, 3):
                    pe.wait_ge(qt_copied.sem, qt_copied.now(t, k // 2 + 1))
                for h in range(4):
                    m = pe.transpose(TB[k][:, h * P:(h + 1) * P], qn[:, 4 * k + h, :], ident[:])
                m.then_inc(qt_done.sem, 1)

            def transpose_context(t, b):
                pe.wait_ge(ctx_in[b].sem, ctx_in[b].now(t, 1))
                for h in range(HC):
                    for c in range(3):
                        m = pe.transpose(PC[h][:, c * P:c * P + CW[c]], cn[0:CW[c], b, c, h * P:(h + 1) * P],
                                         ident[0:CW[c], 0:CW[c]])
                m.then_inc(ct_done.sem, 1)

            def project_key(t, j):
                b, g = j // G, j % G
                if g == 0:
                    pe.wait_ge(ct_copied.sem, ct_copied.now(t, b + 1))
                pe.wait_ge(k_sq.sem, k_sq.after(t, j - 1))
                for c in range(HC):
                    m = pe.matmul(Kb[j % 2][:, 0:SE], wk[:, c, g * HD:(g + 1) * HD], cT[:, b % 2, c, :],
                                  start=c == 0, stop=c == HC - 1)
                m.then_inc(k_done.sem, 1)

            def sum_squares(t, j):
                pe.wait_ge(k_sq.sem, k_sq.now(t, j + 1))
                pe.wait_ge(k_log.sem, k_log.after(t, j))
                pe.matmul(SSb[:, 0:SE], ones[:], sq[:, j % (2 * GU), :], start=True, stop=True
                          ).then_inc(ss_done.sem, 1)

            def scores(t, u):
                b, h = u // UNITS, 4 * (u % UNITS)
                if u % UNITS == 0:
                    pe.wait_ge(qT_ready.sem, qT_ready.now(t, b + 1))
                s_read = e_done if L1 else top_done
                pe.wait_ge(s_read.sem, s_read.after(t, u))
                pe.wait_ge(kt_done.sem, kt_done.now(t, GU * (u + 1)))
                for g in range(GU):
                    q = qT[:, b, h + g * 4 // GU:h + (g + 1) * 4 // GU, :].rearrange("p h q -> p (h q)")
                    m = pe.matmul(Sb[g * MG:(g + 1) * MG, 0:KW], q, kT[:, u % 4, g, :], start=True, stop=True)
                m.then_inc(s_done.sem, 1)

            def transpose_probs(t, u):
                b, v = u // UNITS, u % UNITS
                pe.wait_ge(pn_done.sem, pn_done.now(t, u + 1))
                pe.wait_ge(pt_copied.sem, pt_copied.after(t, u))
                if v == 0:
                    pe.wait_ge(pl_copied.sem, pl_copied.after(t, b))
                for c in range(2):
                    pe.transpose(PTb[:, c * P:(c + 1) * P], pr[:, u % 4, c * P:(c + 1) * P], ident[:])
                pe.transpose(Lb[0:CW[2], v * P:(v + 1) * P], pr[:, u % 4, 2 * P:SE], ident[:]
                             ).then_inc(pt_done.sem, 1)

            def weigh_context(t, b):
                pe.wait_ge(pt_copied.sem, pt_copied.now(t, UNITS * (b + 1)))
                pe.wait_ge(pl_copied.sem, pl_copied.now(t, b + 1))
                pe.wait_ge(pc0_read.sem, pc0_read.after(t, b))
                for h in range(HC):
                    for c in range(3):
                        m = pe.matmul(PC[h][:, :], cn[0:CW[c], b, c, h * P:(h + 1) * P],
                                      pT[0:CW[c], b % 2, c, :], start=c == 0, stop=c == 2)
                    m.then_inc(pc_done.sem, 1)

            def project_values(t, b, first=False):
                if first:
                    pe.wait_ge(late_weights, 16 * 2)
                pe.wait_ge(pc_copied.sem, pc_copied.now(t, HC * (b + 1)))
                for g in range(G):
                    w = UNITS * P // G
                    for c in range(HC):
                        m = pe.matmul(PC[0][:, g * w:(g + 1) * w], wv[:, c, g * HD:(g + 1) * HD],
                                      pcT[:, c, g * w:(g + 1) * w], start=c == 0, stop=c == HC - 1)
                m.then_inc(o_done.sem, 1)

            def project_out(t):
                pe.wait_ge(o_copied.sem, o_copied.now(t, BT))
                for h in range(NH):
                    m = pe.matmul(PC[1][:, 0:H], oT[:, h, :], wo[:, h, :], start=h == 0, stop=h == NH - 1)
                m.then_inc(y_done.sem, 1)

            def tile(i, cur, prev, nxt):
                for u in steps(cur):
                    for g in range(GU):
                        if cur:
                            project_key(i, GU * u + g)
                        for t, v in lagging(i, u, 1, cur, prev):
                            sum_squares(t, GU * v + g)
                    if u == 3 and cur:
                        if prev:
                            pe.wait_ge(pc0_read.sem, pc0_read.now(i - 1, 3))
                        if nxt:
                            pe.wait_ge(xt_copied.sem, xt_copied.now(i + 1, 1))
                        transpose_context(i, 1)
                    if u == 7 and cur:
                        if nxt:
                            pe.wait_ge(q_in.sem, q_in.now(i + 1, 2))
                        if prev:
                            pe.wait_ge(x_added.sem, x_added.now(i - 1, 1))
                        transpose_context(i, 2)
                    if u == 11 and cur:
                        if nxt:
                            pe.wait_ge(q_in.sem, q_in.now(i + 1, 4))
                            pe.wait_ge(qt_copied.sem, qt_copied.now(i + 1, 1))
                        pe.wait_ge(pc0_read.sem, pc0_read.now(i, 1))
                        transpose_context(i, 3)
                    if u == 15 and nxt:
                        pe.wait_ge(qt_copied.sem, qt_copied.now(i + 1, 4))
                        transpose_context(i + 1, 0)
                    for t, v in lagging(i, u, 2, cur, prev):
                        scores(t, v)
                    for t, v in lagging(i, u, 4, cur, prev):
                        transpose_probs(t, v)
                    for t, b in batch_at(i, u, 8, cur, prev):
                        weigh_context(t, b)
                    for t, b in batch_at(i, u, 9, cur, prev):
                        project_values(t, b, first=not prev)
                    if u == 1 and nxt:
                        transpose_tokens(i + 1)
                    if u == 5 and nxt:
                        project_query(i + 1, 0)
                    if u == 6 and nxt:
                        if prev:
                            pe.wait_ge(pc0_read.sem, pc0_read.now(i - 1, 4))
                        project_query(i + 1, 1)
                    if u == 6 and prev:
                        if nxt:
                            pe.wait_ge(q_in.sem, q_in.now(i + 1, 1))
                        project_out(i - 1)
                    if u == 9 and nxt:
                        project_query(i + 1, 2)
                    if u == 10 and nxt:
                        pe.wait_ge(pc0_read.sem, pc0_read.now(i, 1))
                        project_query(i + 1, 3)
                        transpose_query(i + 1, 0)
                    if u == 13 and nxt:
                        transpose_query(i + 1, 1)
                    if u == 14 and nxt:
                        pe.wait_ge(pc0_read.sem, pc0_read.now(i, 2))
                        transpose_query(i + 1, 2)
                        transpose_query(i + 1, 3)

            transpose_tokens(0)
            for k in range(4):
                project_query(0, k)
            for k in range(4):
                transpose_query(0, k)
            pe.wait_ge(qt_copied.sem, qt_copied.now(0, 4))
            transpose_context(0, 0)
            pe.wait_ge(key_weights, 16)
            run(pe, tile)

        @block.scalar
        def _(act):
            for s in (xt_copied, q_sq, q_log, q_rs, qt_copied, ct_copied, k_sq, k_log, k_rs, e_done, ln_log, ln_rs):
                s.prime(act)
            act.preload_act_table_set(EXPLN)
            act.wait_ge(ready, 1)

            def rsqrt_tokens(t, k):
                act.wait_ge(ln_agg.sem, ln_agg.now(t, k + 1))
                act.activation(lr[:], mv[:, 1:2], ACT.Ln, bias=eps_ln[:]).then_inc(ln_log.sem, 1)
                act.wait_ge(ln_log.sem, ln_log.now(t, k + 1))
                act.activation(lr[:], lr[:], ACT.Exp, scale=-0.5).then_inc(ln_rs.sem, 1)

            def copy_tokens(t):
                act.wait_ge(xt_done.sem, xt_done.now(t, 1))
                if L1:
                    act.wait_ge(xq_done.sem, xq_done.before(t, 1))
                else:
                    act.wait_ge(q_done.sem, q_done.before(t, 4))
                act.activation((lnT if L1 else xnT)[:], PC[1][:, 0:H].rearrange("p (c t) -> p c t", c=HC), ACT.Copy
                               ).then_inc(xt_copied.sem, 1)

            def square_query(t, k):
                act.wait_ge(q_in.sem, q_in.now(t, k + 1))
                act.wait_ge(q_sum.sem, q_sum.after(t, k))
                act.activation(qsq[:], qn[:, 4 * k:4 * k + 4, :], ACT.Square).then_inc(q_sq.sem, 1)

            def rsqrt_query(t, k):
                hs = slice(4 * k, 4 * k + 4)
                act.wait_ge(q_sum.sem, q_sum.now(t, k + 1))
                act.activation(qr[:, hs], qss[:, hs], ACT.Ln, bias=eps_h[:], scale=1.0 / HD).then_inc(q_log.sem, 1)
                act.wait_ge(q_log.sem, q_log.now(t, k + 1))
                act.activation(qr[:, hs], qr[:, hs], ACT.Exp, scale=-0.5).then_inc(q_rs.sem, 1)

            def copy_query(t, k):
                act.wait_ge(qt_done.sem, qt_done.now(t, k + 1))
                act.wait_ge(qT_ready.sem, qT_ready.before(t, BT))
                src = TB[k][:, :].rearrange("p (h b q) -> p h b q", h=4, b=BT)
                dst = qTn[:, :, 4 * k:4 * k + 4, :].rearrange("p b h q -> p h b q")
                if L1:
                    act.activation(dst, src, ACT.Identity, scale=qscale[:], bias=qbias[:]).then_inc(qt_copied.sem, 1)
                else:
                    act.activation(dst, src, ACT.Copy, scale=qscale[:]).then_inc(qt_copied.sem, 1)

            def copy_context(t, b):
                act.wait_ge(ct_done.sem, ct_done.now(t, b + 1))
                act.wait_ge(k_done.sem, k_done.after(t, G * (b - 1)))
                act.activation(cT[:, b % 2, 0, :], PC[0][:, 0:SE], ACT.Copy)
                act.activation(cT[:, b % 2, 1, :], PC[1][:, 0:SE], ACT.Copy).then_inc(ct_copied.sem, 1)

            def square_key(t, j):
                act.wait_ge(k_raw.sem, k_raw.now(t, j + 1))
                act.wait_ge(ss_done.sem, ss_done.after(t, j + 1 - 2 * GU))
                dst = sq[:, j % (2 * GU), :]
                if L1:
                    act.activation(dst, Kb[j % 2][:, 0:SE], ACT.Square).then_inc(k_sq.sem, 1)
                else:
                    act.activation(dst, Kb[j % 2][:, 0:SE], ACT.Square, bias=bkv[:, 0, j % G:j % G + 1]
                                   ).then_inc(k_sq.sem, 1)

            def rsqrt_key(t, j):
                r = rs[:, j % (2 * GU), :]
                act.wait_ge(ss_done.sem, ss_done.now(t, j + 1))
                act.wait_ge(kt_done.sem, kt_done.after(t, j + 1 - 2 * GU))
                act.activation(r, SSb[:, 0:SE], ACT.Ln, bias=eps_h[:]).then_inc(k_log.sem, 1)
                act.wait_ge(k_log.sem, k_log.now(t, j + 1))
                act.activation(r, r, ACT.Exp, scale=-0.5).then_inc(k_rs.sem, 1)

            def exp_scores(t, u):
                act.wait_ge(top_done.sem, top_done.now(t, u + 1))
                act.wait_ge(pt_done.sem, pt_done.after(t, u - 3))
                src = Sb[:, 0:SE] if L1 else sm[:, u % 2, :]
                act.activation(pr[:, u % 4, :], src, ACT.Exp, bias=ntop[:, u:u + 1],
                               accum_out=ps[:, u:u + 1]).then_inc(e_done.sem, 1)

            def tile(i, cur, prev, nxt):
                for u in steps(cur):
                    if u == 1 and nxt and L1:
                        rsqrt_tokens(i + 1, 1)
                    for g in range(GU):
                        for t, v in lagging(i, u, 1, cur, prev):
                            rsqrt_key(t, GU * v + g)
                        if cur:
                            square_key(i, GU * u + g)
                    if u in (3, 7, 11) and cur:
                        copy_context(i, u // 4 + 1)
                    if u == 15 and nxt:
                        copy_context(i + 1, 0)
                    for t, v in lagging(i, u, 2, cur, prev):
                        exp_scores(t, v)
                    if u == 0 and nxt:
                        rsqrt_tokens(i + 1, 0)
                    if u == 1 and nxt:
                        copy_tokens(i + 1)
                    if u in (7, 8, 11, 12) and nxt:
                        rsqrt_query(i + 1, {7: 0, 8: 1, 11: 2, 12: 3}[u])
                    if u in (6, 7, 10, 11) and nxt:
                        square_query(i + 1, {6: 0, 7: 1, 10: 2, 11: 3}[u])
                    if u == 10 and nxt:
                        copy_query(i + 1, 0)
                    if u == 13 and nxt:
                        copy_query(i + 1, 1)
                    if u == 14 and nxt:
                        copy_query(i + 1, 2)
                        copy_query(i + 1, 3)

            for k in range(NLN):
                rsqrt_tokens(0, k)
            copy_tokens(0)
            for k in range(4):
                square_query(0, k)
                rsqrt_query(0, k)
            for k in range(4):
                copy_query(0, k)
            copy_context(0, 0)
            run(act, tile)

        @block.gpsimd
        def _(pool):
            for s in (kt_done, qT_ready):
                s.prime(pool)
            pool.wait_ge(ready, 1)

            def norm_key(t, j):
                k = kT[:, j // GU % 4, j % GU, 0:SE]
                pool.wait_ge(k_raw.sem, k_raw.now(t, j + 1))
                pool.wait_ge(k_rs.sem, k_rs.now(t, j + 1))
                pool.tensor_tensor(k, k, rs[:, j % (2 * GU), :], ALU.mult).then_inc(kt_done.sem, 1)

            def queries_of_batch(t, b):
                pool.wait_ge(qt_copied.sem, qt_copied.now(t, 4))
                pool.wait_ge(s_done.sem, s_done.before(t, UNITS * (b + 1)))
                pool.sem_inc(gate, 1)
                pool.tensor_copy(qT[:, b, :, :], qTn[:, b, :, :]).then_inc(qT_ready.sem, 1)

            def tile(i, cur, prev, nxt):
                for u in steps(cur):
                    for t, v in lagging(i, u, 1, cur, prev):
                        for g in range(GU):
                            norm_key(t, GU * v + g)
                    if u == 2 and cur:
                        queries_of_batch(i, 3)
                    if u == 15 and nxt:
                        for b in range(3):
                            queries_of_batch(i + 1, b)

            for b in range(3):
                queries_of_batch(0, b)
            run(pool, tile)

        @block.vector
        def _(dve):
            for s in (xn_done, xq_done, q_in, q_sum, qn_done, k_raw, top_found, top_done, r_done, pn_done, pt_copied,
                      pl_copied, pc_copied, o_read, oq_steps, o_copied, y_summed, x_added, ln_sum, ln_agg, x_mid,
                      xq_steps):
                s.prime(dve)
            dve.memset(ones[:], 1.0 / HD)
            dve.memset(eps_ln[:], 1e-5)
            dve.memset(eps_h[:], EPS)
            dve.wait_ge(weights, 16 * NLOADS)
            step = [0]

            def then(ins):
                step[0] += 1
                ins.then_inc(setup, 1)
                dve.wait_ge(setup, step[0])

            if L1:
                for w, nh in ((wq, NH), (wk, G)):
                    if w is wk:
                        dve.wait_ge(key_weights, 16)
                    wr = w[:].rearrange("p c (h e) -> p (c h) e", e=HD)
                    mean = wmean[:].rearrange("p c h -> p (c h)")[:, 0:HC * nh]
                    then(dve.tensor_reduce(mean, wr, AX.X, ALU.add))
                    then(dve.tensor_scalar(mean, mean, 1.0 / HD, None, ALU.mult))
                    then(dve.tensor_tensor(wr, wr, mean.unsqueeze(2).to_broadcast([P, HC * nh, HD]), ALU.subtract))
                then(dve.reciprocal(inv_in[:], vecs[:, 4:6]))
                then(dve.reciprocal(inv_sm[:], smooth[:]))
                then(dve.tensor_scalar(qscale[:], vecs[:, 6:7], SCALE, None, ALU.mult))
                then(dve.tensor_scalar(qbias[:], vecs[:, 7:8], SCALE, None, ALU.mult))
                then(dve.tensor_tensor(yscale[:], vecs[:, 11:12], vecs[:, 12:13], ALU.mult))
                for r in range(4 * GU):
                    then(dve.tensor_copy(kT[:, r // GU, r % GU, SE:KW], vecs[:, 9:10]))
            else:
                then(dve.scalar_tensor_tensor(qscale[:], nw[:, 0:1], SCALE, nw[:, 1:2], ALU.mult, ALU.mult))
            dve.sem_inc(ready, 1)

            def token_stats(t, k):
                dve.bn_stats(stats[:], xn[:] if k else X[:, t, :]).then_inc(ln_sum.sem, 1)
                dve.wait_ge(ln_sum.sem, ln_sum.now(t, k + 1))
                dve.sem_inc(gate, 1)
                dve.bn_aggr(mv[:], stats[:]).then_inc(ln_agg.sem, 1)

            def norm_tokens(t, k):
                dve.wait_ge(ln_rs.sem, ln_rs.now(t, k + 1))
                if k == 0:
                    dve.wait_ge(xt_done.sem, xt_done.before(t, 1))
                src = xn[:] if k else X[:, t, :]
                norm = dve.tensor_scalar(xn[:], src, mv[:, 0:1], lr[:], ALU.subtract, ALU.mult)
                if k == NLN - 1:
                    norm.then_inc(xn_done.sem, 1)
                else:
                    norm.then_inc(x_mid.sem, 1)
                    dve.wait_ge(x_mid.sem, x_mid.now(t, 1))

            def quantise_tokens(t):
                dve.wait_ge(xt_copied.sem, xt_copied.now(t, 1))
                a, b = qa[:, 0:H], qb[:, 0:H]
                wide = lambda x: x.rearrange("p (c t) -> p c t", c=HC)
                for c in range(HC):
                    w = dve.tensor_scalar(lnT[:, c, :], lnT[:, c, :], vecs[:, c:c + 1], vecs[:, 2 + c:3 + c],
                                          ALU.mult, ALU.add)
                w.then_inc(xq_steps.sem, 1)
                dve.wait_ge(xq_steps.sem, xq_steps.now(t, 1))
                dve.tensor_tensor(wide(a), lnT[:], inv_in[:].unsqueeze(2).to_broadcast([P, HC, P]), ALU.mult
                                  ).then_inc(xq_steps.sem, 1)
                dve.wait_ge(xq_steps.sem, xq_steps.now(t, 2))
                dve.tensor_scalar(b, a, FP8_MAX, -FP8_MAX, ALU.min, ALU.max).then_inc(xq_steps.sem, 1)

            def round_tokens(t):
                a, b, e, m = qa[:, 0:H], qb[:, 0:H], qe[:, 0:H], qm[:, 0:H]
                wide = lambda x: x.rearrange("p (c t) -> p c t", c=HC)
                dve.wait_ge(xq_steps.sem, xq_steps.now(t, 3))
                dve.tensor_scalar(e.bitcast(U16), b.bitcast(U16), 0x7F80, None, ALU.bitwise_and
                                  ).then_inc(xq_steps.sem, 1)
                dve.wait_ge(xq_steps.sem, xq_steps.now(t, 4))
                dve.tensor_scalar(m, e, FP8_SMALLEST, FP8_ROUND, ALU.max, ALU.mult).then_inc(xq_steps.sem, 1)
                dve.wait_ge(xq_steps.sem, xq_steps.now(t, 5))
                dve.tensor_tensor(a, b, m, ALU.add).then_inc(xq_steps.sem, 1)
                dve.wait_ge(xq_steps.sem, xq_steps.now(t, 6))
                dve.tensor_tensor(a, a, m, ALU.subtract).then_inc(xq_steps.sem, 1)
                dve.wait_ge(xq_steps.sem, xq_steps.now(t, 7))
                dve.wait_ge(q_done.sem, q_done.before(t, 4))
                dve.tensor_tensor(xnT[:], wide(a), vecs[:, 4:6].unsqueeze(2).to_broadcast([P, HC, P]), ALU.mult
                                  ).then_inc(xq_done.sem, 1)

            def copy_queries(t, k):
                dst = qn[:, 4 * k:4 * k + 4, :].rearrange("p h e -> p (h e)")
                dve.wait_ge(q_done.sem, q_done.now(t, k + 1))
                dve.wait_ge(qt_done.sem, qt_done.before(t, k + 1))
                if L1:
                    dve.tensor_scalar(dst, QB[k][:, :], vecs[:, 10:11], None, ALU.mult).then_inc(q_in.sem, 1)
                else:
                    dve.tensor_tensor(dst, QB[k][:, :], bq[:, k * 512:(k + 1) * 512], ALU.add).then_inc(q_in.sem, 1)

            def sum_queries(t, k):
                dve.wait_ge(q_sq.sem, q_sq.now(t, k + 1))
                dve.tensor_reduce(qss[:, 4 * k:4 * k + 4], qsq[:], AX.X, ALU.add).then_inc(q_sum.sem, 1)

            def norm_queries(t, k):
                q = qn[:, 4 * k:4 * k + 4, :]
                dve.wait_ge(q_rs.sem, q_rs.now(t, k + 1))
                dve.tensor_tensor(q, q, qr[:, 4 * k:4 * k + 4].unsqueeze(2).to_broadcast([P, 4, HD]), ALU.mult
                                  ).then_inc(qn_done.sem, 1)

            def copy_key(t, j):
                u, g = j // GU, j % GU
                dve.wait_ge(k_done.sem, k_done.now(t, j + 1))
                dve.wait_ge(s_done.sem, s_done.after(t, u - 3))
                if L1:
                    dve.tensor_scalar(kT[:, u % 4, g, 0:SE], Kb[j % 2][:, 0:SE], vecs[:, 8:9], None, ALU.mult
                                      ).then_inc(k_raw.sem, 1)
                else:
                    dve.tensor_scalar(kT[:, u % 4, g, 0:SE], Kb[j % 2][:, 0:SE], bkv[:, 0, j % G:j % G + 1], None,
                                      ALU.add).then_inc(k_raw.sem, 1)

            def max_scores(t, u):
                dve.wait_ge(s_done.sem, s_done.now(t, u + 1))
                if L1:
                    dve.tensor_reduce(top[:, u:u + 1], Sb[:, 0:SE], AX.X, ALU.max, negate=True
                                      ).then_inc(top_found.sem, 1)
                    dve.wait_ge(top_found.sem, top_found.now(t, u + 1))
                    qkb = Sb[:, SE:KW]
                    dve.tensor_scalar(ntop[:, u:u + 1], top[:, u:u + 1], qkb, qkb, ALU.subtract, ALU.add
                                      ).then_inc(top_done.sem, 1)
                else:
                    dve.wait_ge(e_done.sem, e_done.after(t, u - 1))
                    dve.sem_inc(gate, 1)
                    dve.tensor_tensor_reduce(sm[:, u % 2, :], Sb[:, 0:SE], mask[:], 1.0, -3.0e38, ALU.add, ALU.max,
                                             top[:, u:u + 1]).then_inc(top_found.sem, 1)
                    dve.wait_ge(top_found.sem, top_found.now(t, u + 1))
                    dve.tensor_scalar(ntop[:, u:u + 1], top[:, u:u + 1], -1.0, None, ALU.mult
                                      ).then_inc(top_done.sem, 1)

            def norm_probs(t, u):
                dve.wait_ge(e_done.sem, e_done.now(t, u + 1))
                dve.reciprocal(rps[:, u:u + 1], ps[:, u:u + 1]).then_inc(r_done.sem, 1)
                dve.wait_ge(r_done.sem, r_done.now(t, u + 1))
                dve.tensor_scalar(pr[:, u % 4, :], pr[:, u % 4, :], rps[:, u:u + 1], None, ALU.mult
                                  ).then_inc(pn_done.sem, 1)

            def copy_probs(t, u):
                b, v = u // UNITS, u % UNITS
                dve.wait_ge(pt_done.sem, pt_done.now(t, u + 1))
                if v == 0:
                    dve.wait_ge(pc_done.sem, pc_done.after(t, HC * (b - 1)))
                dve.tensor_copy(pT[:, b % 2, 0:2, v * P:(v + 1) * P],
                                PTb[:, 0:2 * P].rearrange("p (c r) -> p c r", c=2)).then_inc(pt_copied.sem, 1)
                if v == UNITS - 1:
                    dve.tensor_copy(pT[0:CW[2], b % 2, 2, :], Lb[0:CW[2], :]).then_inc(pl_copied.sem, 1)

            def copy_weighed(t, b):
                dve.wait_ge(o_done.sem, o_done.after(t, b))
                for h in range(HC):
                    dve.wait_ge(pc_done.sem, pc_done.now(t, HC * b + h + 1))
                    dve.tensor_copy(pcT[:, h, :], PC[h][:, :]).then_inc(pc_copied.sem, 1)

            def copy_heads(t, b):
                dve.wait_ge(o_done.sem, o_done.now(t, b + 1))
                if b == 0:
                    dve.wait_ge(y_done.sem, y_done.before(t, 1))
                src = PC[0][:, :].rearrange("p (h q) -> p h q", h=NH)
                dst = oT[:, :, b * S:(b + 1) * S]
                if not L1:
                    for g in range(G):
                        a = dve.tensor_scalar(dst[:, 4 * g:4 * g + 4, :], src[:, 4 * g:4 * g + 4, :],
                                              bkv[:, 1, g:g + 1], None, ALU.add)
                    a.then_inc(o_copied.sem, 1)
                    return
                wide = lambda x: x[:].rearrange("p (h q) -> p h q", h=NH)
                dve.tensor_tensor(wide(qa), src, inv_sm[:].unsqueeze(2).to_broadcast([P, NH, S]), ALU.mult
                                  ).then_inc(o_read.sem, 1)
                dve.wait_ge(o_read.sem, o_read.now(t, b + 1))
                dve.tensor_scalar(qb[:], qa[:], FP8_MAX, -FP8_MAX, ALU.min, ALU.max).then_inc(oq_steps.sem, 1)

            def round_heads(t, b):
                wide = lambda x: x[:].rearrange("p (h q) -> p h q", h=NH)
                dve.wait_ge(oq_steps.sem, oq_steps.now(t, 4 * b + 1))
                dve.tensor_scalar(qe[:].bitcast(U16), qb[:].bitcast(U16), 0x7F80, None, ALU.bitwise_and
                                  ).then_inc(oq_steps.sem, 1)
                dve.wait_ge(oq_steps.sem, oq_steps.now(t, 4 * b + 2))
                dve.tensor_scalar(qm[:], qe[:], FP8_SMALLEST, FP8_ROUND, ALU.max, ALU.mult).then_inc(oq_steps.sem, 1)
                dve.wait_ge(oq_steps.sem, oq_steps.now(t, 4 * b + 3))
                dve.tensor_tensor(qa[:], qb[:], qm[:], ALU.add).then_inc(oq_steps.sem, 1)
                dve.wait_ge(oq_steps.sem, oq_steps.now(t, 4 * b + 4))
                dve.tensor_tensor(oT[:, :, b * S:(b + 1) * S], wide(qa), wide(qm), ALU.subtract).then_inc(o_copied.sem, 1)

            def add_output(t):
                dve.wait_ge(y_done.sem, y_done.now(t, 1))
                if L1:
                    dve.scalar_tensor_tensor(ysum[:], PC[1][:, 0:H], yscale[:], Yc[:, t, :], ALU.mult, ALU.add
                                             ).then_inc(y_summed.sem, 1)
                    dve.wait_ge(y_summed.sem, y_summed.now(t, 1))
                    dve.tensor_tensor(X[:, t, :], X[:, t, :], ysum[:], ALU.add).then_inc(x_added.sem, 1)
                else:
                    dve.tensor_tensor(X[:, t, :], X[:, t, :], PC[1][:, 0:H], ALU.add).then_inc(x_added.sem, 1)

            def tile(i, cur, prev, nxt):
                for u in steps(cur):
                    if cur:
                        for g in range(GU):
                            copy_key(i, GU * u + g)
                    if u in (8, 9, 12, 13) and nxt:
                        norm_queries(i + 1, {8: 0, 9: 1, 12: 2, 13: 3}[u])
                    if u in (7, 8, 11, 12) and nxt:
                        sum_queries(i + 1, {7: 0, 8: 1, 11: 2, 12: 3}[u])
                    for t, b in batch_at(i, u, 10, cur, prev):
                        if L1:
                            round_heads(t, b)
                    if u == 7 and prev:
                        add_output(i - 1)
                    if u == 0 and nxt:
                        token_stats(i + 1, 0)
                    if u == 1 and nxt:
                        norm_tokens(i + 1, NLN - 1)
                    for t, v in lagging(i, u, 3, cur, prev):
                        norm_probs(t, v)
                    for t, v in lagging(i, u, 2, cur, prev):
                        max_scores(t, v)
                    if u == 0 and nxt and L1:
                        norm_tokens(i + 1, 0)
                        token_stats(i + 1, 1)
                    if u == 2 and nxt and L1:
                        quantise_tokens(i + 1)
                    if u == 3 and nxt and L1:
                        round_tokens(i + 1)
                    for t, v in lagging(i, u, 4, cur, prev):
                        copy_probs(t, v)
                    for t, b in batch_at(i, u, 8, cur, prev):
                        copy_weighed(t, b)
                    for t, b in batch_at(i, u, 9, cur, prev):
                        copy_heads(t, b)
                    if u in (5, 6, 9, 10) and nxt:
                        copy_queries(i + 1, {5: 0, 6: 1, 9: 2, 10: 3}[u])

            token_stats(0, 0)
            norm_tokens(0, 0)
            if L1:
                token_stats(0, 1)
                norm_tokens(0, 1)
                quantise_tokens(0)
                round_tokens(0)
            for k in range(4):
                copy_queries(0, k)
                sum_queries(0, k)
                norm_queries(0, k)
            run(dve, tile)


PT = 4


class TokenNorm:

    def __init__(self, ctx, nc, n, X, ident, pt=PT):
        def sb(name, shape):
            return ctx.enter_context(nc.sbuf_tensor(n + name, shape, F32))

        self.X, self.ident, self.pt = X, ident, pt
        self.stats = sb("ln_stats", [P, pt, 6])
        self.mv = sb("ln_mv", [P, pt, 2])
        self.lr = sb("ln_r", [P, pt])
        self.eps = sb("ln_eps", [P, 1])
        self.xn = sb("xn", [P, pt, H])
        self.xnT = sb("xnT", [P, HC, pt * P])
        self.gate = ctx.semaphore(n + "ln_gate")
        self.eps_set = ctx.semaphore(n + "ln_eps_set")
        self.summed = Signal(ctx, nc, n + "ln_summed", 1)
        self.aggregated = Signal(ctx, nc, n + "ln_aggregated", 1)
        self.logged = Signal(ctx, nc, n + "ln_logged", 1)
        self.scaled = Signal(ctx, nc, n + "ln_rsqrt", 1)
        self.normed = Signal(ctx, nc, n + "ln_normed", 1)
        self.turned = Signal(ctx, nc, n + "ln_transposed", HC)
        self.copied = Signal(ctx, nc, n + "ln_copied", HC)

    def vector_setup(self, dve):
        for s in (self.summed, self.aggregated, self.normed):
            s.prime(dve)
        dve.memset(self.eps[:], 1e-5).then_inc(self.eps_set, 1)

    def scalar_setup(self, act):
        for s in (self.logged, self.scaled, self.copied):
            s.prime(act)
        act.wait_ge(self.eps_set, 1)

    def vector(self, dve, i):
        for t in range(self.pt):
            a = dve.bn_stats(self.stats[:, t, :], self.X[:, i * self.pt + t, :])
        a.then_inc(self.summed.sem, 1)
        dve.wait_ge(self.summed.sem, self.summed.now(i, 1))
        dve.sem_inc(self.gate, 1)
        for t in range(self.pt):
            a = dve.bn_aggr(self.mv[:, t, :], self.stats[:, t, :])
        a.then_inc(self.aggregated.sem, 1)
        dve.wait_ge(self.scaled.sem, self.scaled.now(i, 1))
        dve.wait_ge(self.turned.sem, self.turned.before(i, HC))
        for t in range(self.pt):
            a = dve.tensor_scalar(self.xn[:, t, :], self.X[:, i * self.pt + t, :], self.mv[:, t, 0:1],
                                  self.lr[:, t:t + 1], ALU.subtract, ALU.mult)
        a.then_inc(self.normed.sem, 1)

    def scalar_rsqrt(self, act, i):
        act.wait_ge(self.aggregated.sem, self.aggregated.now(i, 1))
        act.activation(self.lr[:], self.mv[:, :, 1], ACT.Ln, bias=self.eps[:]).then_inc(self.logged.sem, 1)
        act.wait_ge(self.logged.sem, self.logged.now(i, 1))
        act.activation(self.lr[:], self.lr[:], ACT.Exp, scale=-0.5).then_inc(self.scaled.sem, 1)

    def tensor(self, pe, i, banks):
        pe.wait_ge(self.normed.sem, self.normed.now(i, 1))
        for c in range(HC):
            for t in range(self.pt):
                m = pe.transpose(banks[c][:, t * P:(t + 1) * P], self.xn[:, t, c * P:(c + 1) * P], self.ident[:])
            m.then_inc(self.turned.sem, 1)

    def scalar_copy(self, act, i, banks):
        for c in range(HC):
            act.wait_ge(self.turned.sem, self.turned.now(i, c + 1))
            act.activation(self.xnT[:, c, :], banks[c][:, 0:self.pt * P], ACT.Copy).then_inc(self.copied.sem, 1)


def product_attention(nc, d, X, ident, tiles):
    n = "a0_"
    M = 512
    MC = M // P
    NHQ = 4
    DK = 16
    SLOT = 32
    KSCALE = float(DK) ** 0.5
    STEPS = NHQ * MC * 4
    passes = tiles // PT
    N = PT * P
    with Part(nc) as ctx:
        def sb(name, shape, dt=F32):
            return ctx.enter_context(nc.sbuf_tensor(n + name, shape, dt))

        def bank(name):
            return ctx.enter_context(nc.psum_tensor(n + name, [P, 512], F32))

        def sig(name, per, unit=1):
            return Signal(ctx, nc, n + name, per, unit)

        wq = sb("wq", [P, HC, NHQ * P])
        kT = sb("kT", [P, NHQ, M])
        vw = sb("vw", [P, MC, 512])
        wg = sb("wg", [P, HC, 512])
        wo = sb("wo", [P, NHQ, H])
        qT = sb("qT", [P, NHQ, N])
        eT = sb("eT", [P, 4, N])
        gT = sb("gT", [P, 2, N])
        og = sb("og", [P, NHQ, N])
        Eb = [bank(f"E{k}") for k in range(4)]
        Ob = [bank("O0"), bank("O1")]
        Tb = [bank("T0"), bank("T1")]
        ln = TokenNorm(ctx, nc, n, X, ident)
        weights = ctx.semaphore(n + "weights")
        late_weights = ctx.semaphore(n + "late_weights")
        q_done = sig("q_done", NHQ)
        q_copied = sig("q_copied", NHQ)
        g_done = sig("gate_done", NHQ)
        g_copied = sig("gate_silu", NHQ)
        e_done = sig("energy_done", STEPS)
        e_silu = sig("energy_silu", STEPS)
        pv_done = sig("pv_done", STEPS)
        og_done = sig("gated", NHQ)
        y_done = sig("y_done", 2)
        x_added = sig("x_added", 2)
        block = ctx.open_block()

        @block.sync
        def _(sp):
            for dst, src in ((wq, d["wq"].rearrange("(c p) n -> p c n", p=P)),
                             (wg, d["wg"].rearrange("(c p) n -> p c n", p=P))):
                sp.dma_start(dst[:], src).then_inc(weights, 16)
            for dst, src in ((kT, d["kT"].rearrange("j p m -> p j m")),
                             (vw, d["vw"].rearrange("(c p) n -> p c n", p=P)),
                             (wo, d["wo"].rearrange("(c p) n -> p c n", p=P))):
                sp.dma_start(dst[:], src).then_inc(late_weights, 16)

        @block.tensor
        def _(pe):
            for s in (ln.turned, q_done, g_done, e_done, pv_done, y_done):
                s.prime(pe)

            def energy(i, s):
                hq, c, r = s // 16, s // 4 % 4, s % 4
                at = slice(SLOT * r, SLOT * r + DK)
                pe.matmul(Eb[r][:, :], kT[at, hq, c * P:(c + 1) * P], qT[at, hq, :], start=True, stop=True
                          ).then_inc(e_done.sem, 1)

            def weigh(i, s):
                hq, c, r = s // 16, s // 4 % 4, s % 4
                pe.wait_ge(e_silu.sem, e_silu.now(i, s + 1))
                if s % 16 == 0:
                    pe.wait_ge(og_done.sem, og_done.after(i, hq - 1))
                h = 4 * hq + r
                pe.matmul(Ob[hq % 2][32 * r:32 * r + 32, :], vw[:, c, 32 * h:32 * h + 32], eT[:, r, :],
                          start=c == 0, stop=c == MC - 1).then_inc(pv_done.sem, 1)

            with pe.Fori(0, passes) as i:
                pe.wait_ge(x_added.sem, x_added.before(i, 2))
                ln.tensor(pe, i, Tb)
                pe.wait_ge(ln.copied.sem, ln.copied.now(i, HC))
                pe.wait_ge(weights, 16 * 2)
                for j in range(NHQ):
                    for c in range(HC):
                        m = pe.matmul(Eb[j][:, :], wq[:, c, j * P:(j + 1) * P], ln.xnT[:, c, :],
                                      start=c == 0, stop=c == HC - 1)
                    m.then_inc(q_done.sem, 1)
                for s in range(STEPS + 2):
                    if s < STEPS and s % 16 == 0:
                        j = s // 16
                        if j >= 2:
                            pe.wait_ge(g_copied.sem, g_copied.now(i, j - 1))
                        for c in range(HC):
                            m = pe.matmul(Tb[j % 2][:, :], wg[:, c, j * P:(j + 1) * P], ln.xnT[:, c, :],
                                          start=c == 0, stop=c == HC - 1)
                        m.then_inc(g_done.sem, 1)
                        if j == 0:
                            pe.wait_ge(q_copied.sem, q_copied.now(i, NHQ))
                            pe.wait_ge(late_weights, 16 * 3)
                    if s < STEPS:
                        energy(i, s)
                    if s >= 2:
                        weigh(i, s - 2)
                pe.wait_ge(og_done.sem, og_done.now(i, NHQ))
                pe.wait_ge(g_copied.sem, g_copied.now(i, NHQ))
                for k in range(2):
                    for t in (2 * k, 2 * k + 1):
                        for j in range(NHQ):
                            m = pe.matmul(Tb[k][:, t % 2 * H:t % 2 * H + H], og[:, j, t * P:(t + 1) * P], wo[:, j, :],
                                          start=j == 0, stop=j == NHQ - 1)
                    m.then_inc(y_done.sem, 1)

        @block.scalar
        def _(act):
            ln.scalar_setup(act)
            for s in (q_copied, g_copied, e_silu):
                s.prime(act)
            def one_pass(i, nxt):
                act.wait_ge(g_done.sem, g_done.before(i, NHQ))
                ln.scalar_copy(act, i, Tb)
                act.wait_ge(e_done.sem, e_done.before(i, STEPS))
                for j in range(NHQ):
                    act.wait_ge(q_done.sem, q_done.now(i, j + 1))
                    act.activation(qT[:, j, :], Eb[j][:, :], ACT.Copy).then_inc(q_copied.sem, 1)
                for s in range(STEPS):
                    if s % 16 == 0:
                        j = s // 16
                        act.wait_ge(g_done.sem, g_done.now(i, j + 1))
                        act.wait_ge(og_done.sem, og_done.after(i, j - 1))
                        act.activation(gT[:, j % 2, :], Tb[j % 2][:, :], ACT.Silu).then_inc(g_copied.sem, 1)
                    act.wait_ge(e_done.sem, e_done.now(i, s + 1))
                    act.wait_ge(pv_done.sem, pv_done.after(i, s - 3))
                    act.activation(eT[:, s % 4, :], Eb[s % 4][:, :], ACT.Silu, scale=KSCALE
                                   ).then_inc(e_silu.sem, 1)
                if nxt:
                    ln.scalar_rsqrt(act, i + 1)

            ln.scalar_rsqrt(act, 0)
            with act.Fori(0, passes - 1) as i:
                one_pass(i, True)
            one_pass(passes - 1, False)

        @block.vector
        def _(dve):
            ln.vector_setup(dve)
            for s in (og_done, x_added):
                s.prime(dve)
            def one_pass(i, nxt):
                for j in range(NHQ):
                    dve.wait_ge(g_copied.sem, g_copied.now(i, j + 1))
                    dve.wait_ge(pv_done.sem, pv_done.now(i, 16 * (j + 1)))
                    if j == 0:
                        dve.wait_ge(y_done.sem, y_done.before(i, 2))
                    dve.scalar_tensor_tensor(og[:, j, :], Ob[j % 2][:, :], KSCALE, gT[:, j % 2, :],
                                             ALU.mult, ALU.mult).then_inc(og_done.sem, 1)
                if nxt:
                    ln.vector(dve, i + 1)
                for k in range(2):
                    dve.wait_ge(y_done.sem, y_done.now(i, k + 1))
                    for t in (2 * k, 2 * k + 1):
                        Xt = X[:, i * PT + t, :]
                        a = dve.tensor_tensor(Xt, Xt, Tb[k][:, t % 2 * H:t % 2 * H + H], ALU.add)
                    a.then_inc(x_added.sem, 1)

            ln.vector(dve, 0)
            with dve.Fori(0, passes - 1) as i:
                one_pass(i, True)
            one_pass(passes - 1, False)


def experts(nc, d, X, ident, tiles):
    n = "e0_"
    E = 8
    ALL = E + 1
    passes = tiles // PT
    N = PT * P
    with Part(nc) as ctx:
        def sb(name, shape, dt=F32):
            return ctx.enter_context(nc.sbuf_tensor(n + name, shape, dt))

        def bank(name):
            return ctx.enter_context(nc.psum_tensor(n + name, [P, 512], F32))

        def sig(name, per, unit=1):
            return Signal(ctx, nc, n + name, per, unit)

        w1 = sb("w1", [P, HC, ALL * P])
        w3 = sb("w3", [P, HC, ALL * P])
        w2 = sb("w2", [P, ALL, H])
        wr = sb("wr", [P, HC, E])
        places = sb("places", [P, E])
        lg = sb("lg", [P, PT, E])
        pe_ = sb("probs", [P, PT, E])
        m1 = sb("m1", [P, PT])
        sums = sb("sums", [P, PT])
        rsum = sb("rsum", [P, PT])
        best = sb("best", [P, PT, 8])
        at = sb("at", [P, PT, 8], U32)
        atf = sb("atf", [P, PT, 8])
        chosen = sb("chosen", [P, PT, E])
        comb = sb("comb", [P, PT, E])
        g1 = sb("g1", [P, 2, N])
        gT = sb("gT", [P, 2, N])
        Ab = [bank("A0"), bank("A1")]
        Bb = [bank("B0"), bank("B1")]
        Yb = [[bank("Y0"), bank("Y1")], [bank("T0"), bank("T1")]]
        Tb = Yb[1]
        ln = TokenNorm(ctx, nc, n, X, ident)
        weights = ctx.semaphore(n + "weights")
        late_weights = ctx.semaphore(n + "late_weights")
        r_done = sig("router_done", 1)
        r_shift = sig("router_shifted", 1)
        r_exp = sig("router_exp", 1)
        h_done = sig("hidden_done", 2 * ALL)
        h_silu = sig("hidden_silu", ALL)
        g_done = sig("gated", ALL)
        y_done = sig("y_done", ALL)
        x_added = sig("x_added", ALL)
        dchain = Chain(ctx, nc, n + "dve_chain", 8 + 2 * PT)
        block = ctx.open_block()

        @block.sync
        def _(sp):
            for dst, src in ((w1, d["w1"].rearrange("(c p) n -> p c n", p=P)),
                             (w3, d["w3"].rearrange("(c p) n -> p c n", p=P)),
                             (wr, d["wr"].rearrange("(c p) n -> p c n", p=P)),
                             (places, d["places"])):
                sp.dma_start(dst[:], src).then_inc(weights, 16)
            sp.dma_start(w2[:], d["w2"].rearrange("(e p) n -> p e n", p=P)).then_inc(late_weights, 16)

        @block.tensor
        def _(pe):
            for s in (ln.turned, r_done, h_done, y_done):
                s.prime(pe)
            with pe.Fori(0, passes) as i:
                pe.wait_ge(x_added.sem, x_added.before(i, ALL - 1))
                ln.tensor(pe, i, Tb)
                pe.wait_ge(ln.copied.sem, ln.copied.now(i, HC))
                pe.wait_ge(weights, 16 * 4)
                for t in range(PT):
                    for c in range(HC):
                        m = pe.matmul(Tb[0][:, t * E:(t + 1) * E], ln.xnT[:, c, t * P:(t + 1) * P], wr[:, c, :],
                                      start=c == 0, stop=c == HC - 1)
                m.then_inc(r_done.sem, 1)
                for e in range(ALL + 1):
                    if e < ALL:
                        pe.wait_ge(g_done.sem, g_done.after(i, e - 1))
                        for w, b in ((w1, Ab), (w3, Bb)):
                            for c in range(HC):
                                m = pe.matmul(b[e % 2][:, :], w[:, c, e * P:(e + 1) * P], ln.xnT[:, c, :],
                                              start=c == 0, stop=c == HC - 1)
                            m.then_inc(h_done.sem, 1)
                    if e:
                        f = e - 1
                        pe.wait_ge(g_done.sem, g_done.now(i, e))
                        pe.wait_ge(x_added.sem, x_added.after(i, f - 1))
                        if f == 0:
                            pe.wait_ge(late_weights, 16)
                        if f == 1:
                            pe.wait_ge(r_shift.sem, r_shift.now(i, 1))
                        for t in range(PT):
                            m = pe.matmul(Yb[f % 2][t // 2][:, t % 2 * H:t % 2 * H + H],
                                          gT[:, f % 2, t * P:(t + 1) * P], w2[:, f, :], start=True, stop=True)
                        m.then_inc(y_done.sem, 1)

        @block.scalar
        def _(act):
            ln.scalar_setup(act)
            for s in (r_exp, h_silu):
                s.prime(act)
            def one_pass(i, nxt):
                act.wait_ge(h_done.sem, h_done.before(i, 2 * ALL))
                ln.scalar_copy(act, i, Tb)
                act.wait_ge(r_shift.sem, r_shift.now(i, 1))
                act.activation(pe_[:], lg[:], ACT.Exp).then_inc(r_exp.sem, 1)
                for e in range(ALL):
                    act.wait_ge(h_done.sem, h_done.now(i, 2 * e + 1))
                    act.wait_ge(g_done.sem, g_done.after(i, e - 1))
                    act.activation(g1[:, e % 2, :], Ab[e % 2][:, :], ACT.Silu).then_inc(h_silu.sem, 1)
                if nxt:
                    ln.scalar_rsqrt(act, i + 1)

            ln.scalar_rsqrt(act, 0)
            with act.Fori(0, passes - 1) as i:
                one_pass(i, True)
            one_pass(passes - 1, False)

        @block.vector
        def _(dve):
            ln.vector_setup(dve)
            for s in (r_shift, g_done, x_added, dchain):
                s.prime(dve)

            def link(i, ins):
                ins.then_inc(dchain.sem, 1)
                dve.wait_ge(dchain.sem, dchain.next(i))

            def add_expert(i, e):
                dve.wait_ge(y_done.sem, y_done.now(i, e + 1))
                if e:
                    dve.wait_ge(x_added.sem, x_added.now(i, e))
                for t in range(PT):
                    Xt = X[:, i * PT + t, :]
                    y = Yb[e % 2][t // 2][:, t % 2 * H:t % 2 * H + H]
                    if e < E:
                        a = dve.scalar_tensor_tensor(Xt, y, comb[:, t, e:e + 1], Xt, ALU.mult, ALU.add)
                    else:
                        a = dve.tensor_tensor(Xt, Xt, y, ALU.add)
                a.then_inc(x_added.sem, 1)

            def one_pass(i, nxt):
                dchain.k = 0
                dve.wait_ge(r_done.sem, r_done.now(i, 1))
                dve.wait_ge(weights, 16 * 4)
                scores = Tb[0][:, 0:PT * E].rearrange("p (t e) -> p t e", t=PT)
                link(i, dve.tensor_reduce(m1[:], scores, AX.X, ALU.max))
                dve.tensor_tensor(lg[:], scores, m1[:].unsqueeze(2).to_broadcast([P, PT, E]), ALU.subtract
                                  ).then_inc(r_shift.sem, 1)
                dve.wait_ge(r_exp.sem, r_exp.now(i, 1))
                link(i, dve.tensor_reduce(sums[:], pe_[:], AX.X, ALU.add))
                link(i, dve.reciprocal(rsum[:], sums[:]))
                link(i, dve.tensor_tensor(pe_[:], pe_[:], rsum[:].unsqueeze(2).to_broadcast([P, PT, E]), ALU.mult))
                dve.sem_inc(ln.gate, 1)
                for t in range(PT):
                    a = dve.max(best[:, t, :], pe_[:, t, :])
                link(i, a)
                dve.sem_inc(ln.gate, 1)
                for t in range(PT):
                    a = dve.max_index(at[:, t, :], best[:, t, :], pe_[:, t, :])
                link(i, a)
                link(i, dve.tensor_copy(atf[:], at[:]))
                for t in range(PT):
                    link(i, dve.tensor_scalar(chosen[:, t, :], places[:], atf[:, t, 0:1], None, ALU.is_equal))
                    link(i, dve.scalar_tensor_tensor(chosen[:, t, :], places[:], atf[:, t, 1:2], chosen[:, t, :],
                                                     ALU.is_equal, ALU.add))
                link(i, dve.tensor_tensor(comb[:], pe_[:], chosen[:], ALU.mult))
                for e in range(ALL + 1):
                    if e < ALL:
                        dve.wait_ge(h_silu.sem, h_silu.now(i, e + 1))
                        dve.wait_ge(h_done.sem, h_done.now(i, 2 * e + 2))
                        dve.wait_ge(y_done.sem, y_done.after(i, e - 1))
                        dve.tensor_tensor(gT[:, e % 2, :], g1[:, e % 2, :], Bb[e % 2][:, :], ALU.mult
                                          ).then_inc(g_done.sem, 1)
                    if e == ALL and nxt:
                        ln.vector(dve, i + 1)
                    if e:
                        add_expert(i, e - 1)
                dchain.done()

            ln.vector(dve, 0)
            with dve.Fori(0, passes - 1) as i:
                one_pass(i, True)
            one_pass(passes - 1, False)


def core_attention(nc, d, X, Yc, ident, tiles):
    n = "c1_"
    G = 8
    NK = NH + G
    KINDS = 3
    SCALE = HD ** -0.5
    with Part(nc) as ctx:
        def sb(name, shape, dt=F32):
            return ctx.enter_context(nc.sbuf_tensor(n + name, shape, dt))

        def sig(name, per, unit=1):
            return Signal(ctx, nc, n + name, per, unit)

        wqk = sb("wqk", [P, HC, NK * HD])
        wv = sb("wv", [P, HC, G * HD])
        wo = sb("wo", [P, NH, H])
        vecs = sb("vecs", [P, 20])
        smooth = sb("smooth", [P, NH])
        inv_in = sb("inv_in", [P, KINDS * HC])
        inv_sm = sb("inv_sm", [P, NH])
        qw = sb("qw", [P, 2])
        yscale = sb("yscale", [P, 1])
        wmean = sb("wmean", [P, HC * NK])
        eps = sb("eps", [P, 1])
        qa = sb("qa", [P, NH * P])
        qb = sb("qb", [P, NH * P], BF16)
        qe = sb("qe", [P, NH * P], BF16)
        qm = sb("qm", [P, NH * P])
        xa = sb("xa", [P, KINDS * HC * P])
        xb = sb("xb", [P, KINDS * HC * P], BF16)
        xe = sb("xe", [P, KINDS * HC * P], BF16)
        xm = sb("xm", [P, KINDS * HC * P])
        lnT = sb("lnT", [P, HC, P])
        xq = sb("xq", [P, KINDS * HC, P])
        qk = sb("qk", [P, NK, HD])
        qksq = sb("qksq", [P, NK, HD])
        ss = sb("ss", [P, NK])
        rs = sb("rs", [P, NK])
        vn = sb("vn", [P, G, HD])
        qkT = sb("qkT", [P, NK, P])
        ntop = sb("ntop", [P, NH])
        sums = sb("sums", [P, NH])
        rsum = sb("rsum", [P, NH])
        sc = sb("sc", [P, NH, S])
        pr = sb("pr", [P, NH, S])
        prT = sb("prT", [P, NH, S])
        oT = sb("oT", [P, NH, P])
        banks = [ctx.enter_context(nc.psum_tensor(f"{n}B{k}", [P, 512], F32)) for k in range(8)]
        ln = TokenNorm(ctx, nc, n, X, ident, pt=1)
        weights = ctx.semaphore(n + "weights")
        head_weights = [ctx.semaphore(f"{n}head_weights{c}") for c in range(HC)]
        value_weights = ctx.semaphore(n + "value_weights")
        late_weights = ctx.semaphore(n + "late_weights")
        ready = ctx.semaphore(n + "constants_ready")
        setup = ctx.semaphore(n + "setup_steps")
        lstats = sig("ln2_stats", 1)
        lr_done = sig("ln2_rsqrt", 1)
        xn_done = sig("xn_done", 1)
        xt_done = sig("x_transposed", 1)
        xt_copied = sig("xT_copied", 1)
        xq_done = sig("x_quantised", 1)
        p_done = sig("projected", 8)
        p_copied = sig("qk_copied", 6)
        v_copied = sig("v_copied", 2)
        ss_done = sig("squares_summed", 1)
        rs_done = sig("heads_rsqrt", 1)
        qn_done = sig("heads_normed", 1)
        t_done = sig("heads_transposed", 6)
        t_copied = sig("heads_copied", 6)
        s_done = sig("scores_done", 1)
        sub_done = sig("scores_shifted", 1)
        e_done = sig("exp_done", 1)
        pT_done = sig("probs_transposed", 1)
        o_done = sig("heads_out", 1)
        o_copied = sig("heads_quantised", 1)
        y_done = sig("y_done", 1)
        y_copied = sig("y_copied", 1)
        x_log = sig("ln2_log", 1)
        h_log = sig("heads_log", 1)
        x_steps = sig("x_quantise_steps", 8)
        sm_steps = sig("softmax_steps", 4)
        oq_steps = sig("out_quantise_steps", 4)
        oq_sum = sig("out_rounded_up", 1)
        gate = ctx.semaphore(n + "gate")

        block = ctx.open_block()

        @block.sync
        def _(sp):
            sp.dma_start(vecs[:], d["vecs"]).then_inc(weights, 16)
            sp.dma_start(smooth[:], d["smooth"]).then_inc(weights, 16)
            for c in range(HC):
                sp.dma_start(wqk[:, c, :], d["wqk"][c * P:(c + 1) * P, :]).then_inc(head_weights[c], 16)
            sp.dma_start(wv[:], d["wv"].rearrange("(c p) n -> p c n", p=P)).then_inc(value_weights, 16)
            sp.dma_start(wo[:], d["wo"].rearrange("(h p) n -> p h n", p=P)).then_inc(late_weights, 16)

        PB = [0, 1, 2, 0, 1, 2, 3, 0]
        TB = [1, 2, 0, 1, 2, 0]
        XB, YB, SB = banks[5], banks[3], banks[4]
        OB = banks[4:8]

        def run(eng, tile):
            tile(0, None, True, True, True)
            with eng.Fori(0, tiles - 3) as h:
                tile(h + 1, h, True, True, True)
            tile(tiles - 2, tiles - 3, True, True, False)
            tile(tiles - 1, tiles - 2, True, False, False)
            tile(tiles, tiles - 1, False, False, False)

        @block.tensor
        def _(pe):
            for s in (xt_done, p_done, t_done, s_done, o_done, y_done):
                s.prime(pe)
            pe.wait_ge(ready, 1)

            def transpose_tokens(t):
                pe.wait_ge(xn_done.sem, xn_done.now(t, 1))
                for c in range(HC):
                    m = pe.transpose(XB[:, c * P:(c + 1) * P], ln.xn[:, 0, c * P:(c + 1) * P], ident[:])
                m.then_inc(xt_done.sem, 1)

            def project(t, k, h=None):
                kind = (0, 0, 0, 0, 1, 1, 2, 2)[k]
                w = wqk[:, :, k * 512:(k + 1) * 512] if k < 6 else wv[:, :, (k - 6) * 512:(k - 5) * 512]
                if k == 0:
                    pe.wait_ge(xq_done.sem, xq_done.now(t, 1))
                if k == 6 and h is not None:
                    pe.wait_ge(y_copied.sem, y_copied.now(h, 1))
                if k in (3, 4, 5, 7):
                    pe.wait_ge(p_copied.sem, p_copied.now(t, {3: 1, 4: 2, 5: 3, 7: 4}[k]))
                for c in range(HC):
                    m = pe.matmul(banks[PB[k]][:, :], xq[:, kind * HC + c, :], w[:, c, :], start=c == 0,
                                  stop=c == HC - 1)
                m.then_inc(p_done.sem, 1)

            def transpose_heads(t, k):
                if k == 0:
                    pe.wait_ge(qn_done.sem, qn_done.now(t, 1))
                    pe.wait_ge(v_copied.sem, v_copied.now(t, 2))
                if k >= 3:
                    pe.wait_ge(t_copied.sem, t_copied.now(t, k - 2))
                for h in range(4):
                    m = pe.transpose(banks[TB[k]][:, h * P:(h + 1) * P], qk[:, 4 * k + h, :], ident[:])
                m.then_inc(t_done.sem, 1)

            def scores(t):
                pe.wait_ge(t_copied.sem, t_copied.now(t, 6))
                pe.wait_ge(oq_steps.sem, oq_steps.before(t, 1))
                for h in range(NH):
                    for b in range(BT):
                        at = slice(b * S, (b + 1) * S)
                        m = pe.matmul(SB[at, h * S:(h + 1) * S], qkT[:, h, at], qkT[:, NH + h // 2, at],
                                      start=True, stop=True)
                m.then_inc(s_done.sem, 1)

            def weigh_values(t):
                pe.wait_ge(pT_done.sem, pT_done.now(t, 1))
                pe.wait_ge(v_copied.sem, v_copied.now(t, 2))
                for g in range(G):
                    for b in range(BT):
                        at = slice(b * S, (b + 1) * S)
                        m = pe.matmul(OB[b][:, g * 2 * S:(g + 1) * 2 * S], vn[at, g, :],
                                      prT[at, 2 * g:2 * g + 2, :].rearrange("p h q -> p (h q)"),
                                      start=True, stop=True)
                m.then_inc(o_done.sem, 1)

            def project_out(t):
                pe.wait_ge(o_copied.sem, o_copied.now(t, 1))
                for h in range(NH):
                    m = pe.matmul(YB[:, 0:H], oT[:, h, :], wo[:, h, :], start=h == 0, stop=h == NH - 1)
                m.then_inc(y_done.sem, 1)

            def tile(i, h, cur, one, two):
                if cur:
                    scores(i)
                if one:
                    project(i + 1, 0)
                    project(i + 1, 1)
                if h is not None:
                    project_out(h)
                for k in range(2, 7 if one else 2):
                    project(i + 1, k, h)
                if two:
                    transpose_tokens(i + 2)
                if one:
                    project(i + 1, 7)
                if two:
                    pe.wait_ge(xt_copied.sem, xt_copied.now(i + 2, 1))
                if cur:
                    weigh_values(i)
                for k in range(6 if one else 0):
                    transpose_heads(i + 1, k)

            transpose_tokens(0)
            for k in range(8):
                if k == 6:
                    pe.wait_ge(value_weights, 16)
                project(0, k)
            for k in range(6):
                transpose_heads(0, k)
            transpose_tokens(1)
            pe.wait_ge(late_weights, 16)
            run(pe, tile)

        @block.scalar
        def _(act):
            for s in (ln.logged, ln.scaled, x_log, lr_done, xt_copied, ss_done, h_log, rs_done, t_copied, e_done,
                      v_copied):
                s.prime(act)
            act.preload_act_table_set(EXPLN)
            act.wait_ge(ready, 1)

            def rsqrt_tokens(t, k):
                if k == 0:
                    ln.scalar_rsqrt(act, t)
                    return
                act.wait_ge(lstats.sem, lstats.now(t, 1))
                act.activation(ln.lr[:], ln.mv[:, :, 1], ACT.Ln, bias=eps[:]).then_inc(x_log.sem, 1)
                act.wait_ge(x_log.sem, x_log.now(t, 1))
                act.activation(ln.lr[:], ln.lr[:], ACT.Exp, scale=-0.5).then_inc(lr_done.sem, 1)

            def copy_tokens(t):
                act.wait_ge(xt_done.sem, xt_done.now(t, 1))
                act.wait_ge(xq_done.sem, xq_done.before(t, 1))
                act.activation(lnT[:], XB[:, 0:H].rearrange("p (c t) -> p c t", c=HC), ACT.Copy
                               ).then_inc(xt_copied.sem, 1)

            def values(t):
                act.wait_ge(o_done.sem, o_done.before(t, 1))
                for k in range(2):
                    act.wait_ge(p_done.sem, p_done.now(t, 7 + k))
                    act.activation(vn[:, 4 * k:4 * k + 4, :].rearrange("p g e -> p (g e)"), banks[PB[6 + k]][:, :],
                                   ACT.Copy, scale=vecs[:, 16:17]).then_inc(v_copied.sem, 1)

            def square_heads(t, k):
                act.wait_ge(p_copied.sem, p_copied.now(t, k + 1))
                for h in range(4 * k, 4 * k + 4):
                    sq = act.activation(qksq[:, h, :], qk[:, h, :], ACT.Square, accum_out=ss[:, h:h + 1])
                if k == 5:
                    sq.then_inc(ss_done.sem, 1)

            def heads_rsqrt(t):
                act.wait_ge(ss_done.sem, ss_done.now(t, 1))
                act.activation(rs[:], ss[:], ACT.Ln, bias=eps[:], scale=1.0 / HD).then_inc(h_log.sem, 1)
                act.wait_ge(h_log.sem, h_log.now(t, 1))
                act.activation(rs[:], rs[:], ACT.Exp, scale=-0.5).then_inc(rs_done.sem, 1)

            def heads_copy(t):
                act.wait_ge(s_done.sem, s_done.before(t, 1))
                for k in range(6):
                    act.wait_ge(t_done.sem, t_done.now(t, k + 1))
                    w, b = (qw[:, 0:1], qw[:, 1:2]) if k < 4 else (vecs[:, 12:13], vecs[:, 13:14])
                    act.activation(qkT[:, 4 * k:4 * k + 4, :].rearrange("p h t -> p (h t)"), banks[TB[k]][:, :],
                                   ACT.Identity, scale=w, bias=b).then_inc(t_copied.sem, 1)

            def tile(i, h, cur, one, two):
                if cur:
                    act.wait_ge(sub_done.sem, sub_done.now(i, 1))
                    act.activation(pr[:], sc[:], ACT.Exp).then_inc(e_done.sem, 1)
                if one:
                    for k in range(6):
                        square_heads(i + 1, k)
                        if k in (2, 3) and two:
                            rsqrt_tokens(i + 2, k - 2)
                    heads_rsqrt(i + 1)
                if two:
                    copy_tokens(i + 2)
                if one:
                    values(i + 1)
                    heads_copy(i + 1)

            def all_tokens(t):
                rsqrt_tokens(t, 0)
                rsqrt_tokens(t, 1)
                copy_tokens(t)

            all_tokens(0)
            for k in range(6):
                square_heads(0, k)
            heads_rsqrt(0)
            values(0)
            heads_copy(0)
            all_tokens(1)
            run(act, tile)

        @block.gpsimd
        def _(pool):
            for s in (oq_sum, o_copied):
                s.prime(pool)

            def tile(i):
                pool.wait_ge(oq_steps.sem, oq_steps.now(i, 4))
                pool.tensor_tensor(qa[:], qb[:], qm[:], ALU.add).then_inc(oq_sum.sem, 1)
                pool.wait_ge(oq_sum.sem, oq_sum.now(i, 1))
                pool.wait_ge(y_done.sem, y_done.before(i, 1))
                pool.tensor_tensor(oT[:].rearrange("p h t -> p (h t)"), qa[:], qm[:], ALU.subtract
                                   ).then_inc(o_copied.sem, 1)

            with pool.Fori(0, tiles) as i:
                tile(i)

        @block.vector
        def _(dve):
            ln.vector_setup(dve)
            for s in (lstats, xn_done, xq_done, p_copied, qn_done, sub_done, pT_done, y_copied,
                      x_steps, sm_steps, oq_steps):
                s.prime(dve)
            dve.memset(eps[:], 1e-5)
            dve.wait_ge(weights, 16 * 2)
            step = [0]

            def then(ins):
                step[0] += 1
                ins.then_inc(setup, 1)
                dve.wait_ge(setup, step[0])

            for c in range(HC):
                wr = wqk[:, c, :].rearrange("p (h e) -> p h e", e=HD)
                mean = wmean[:, c * NK:(c + 1) * NK]
                dve.wait_ge(head_weights[c], 16)
                then(dve.tensor_reduce(mean, wr, AX.X, ALU.add))
                then(dve.tensor_scalar(mean, mean, 1.0 / HD, None, ALU.mult))
                then(dve.tensor_tensor(wr, wr, mean.unsqueeze(2).to_broadcast([P, NK, HD]), ALU.subtract))
            then(dve.reciprocal(inv_in[:], vecs[:, 4:10]))
            then(dve.reciprocal(inv_sm[:], smooth[:]))
            then(dve.tensor_scalar(qw[:], vecs[:, 10:12], SCALE, None, ALU.mult))
            then(dve.tensor_tensor(yscale[:], vecs[:, 17:18], vecs[:, 18:19], ALU.mult))
            dve.sem_inc(ready, 2)

            def token_stats(t):
                Xt = X[:, t, :]
                dve.bn_stats(ln.stats[:, 0, :], Xt).then_inc(ln.summed.sem, 1)
                dve.wait_ge(ln.summed.sem, ln.summed.now(t, 1))
                dve.sem_inc(gate, 1)
                dve.bn_aggr(ln.mv[:, 0, :], ln.stats[:, 0, :]).then_inc(ln.aggregated.sem, 1)

            def token_stats_again(t):
                Xt = X[:, t, :]
                dve.wait_ge(ln.scaled.sem, ln.scaled.now(t, 1))
                dve.wait_ge(xt_done.sem, xt_done.before(t, 1))
                dve.tensor_scalar(ln.xn[:, 0, :], Xt, ln.mv[:, 0, 0:1], ln.lr[:], ALU.subtract, ALU.mult
                                  ).then_inc(ln.normed.sem, 1)
                dve.wait_ge(ln.normed.sem, ln.normed.now(t, 1))
                dve.bn_stats(ln.stats[:, 0, :], ln.xn[:, 0, :]).then_inc(x_steps.sem, 1)
                dve.wait_ge(x_steps.sem, x_steps.now(t, 1))
                dve.sem_inc(gate, 1)
                dve.bn_aggr(ln.mv[:, 0, :], ln.stats[:, 0, :]).then_inc(lstats.sem, 1)

            def norm_tokens(t):
                dve.wait_ge(lr_done.sem, lr_done.now(t, 1))
                dve.tensor_scalar(ln.xn[:, 0, :], ln.xn[:, 0, :], ln.mv[:, 0, 0:1], ln.lr[:], ALU.subtract, ALU.mult
                                  ).then_inc(xn_done.sem, 1)

            def quantise_tokens(t):
                dve.wait_ge(xt_copied.sem, xt_copied.now(t, 1))
                for c in range(HC):
                    w = dve.tensor_scalar(lnT[:, c, :], lnT[:, c, :], vecs[:, c:c + 1], vecs[:, 2 + c:3 + c],
                                          ALU.mult, ALU.add)
                w.then_inc(x_steps.sem, 1)
                dve.wait_ge(x_steps.sem, x_steps.now(t, 2))
                N = KINDS * HC * P
                a, b, e, m = xa[:, 0:N], xb[:, 0:N], xe[:, 0:N], xm[:, 0:N]
                for k in range(KINDS * HC):
                    w = dve.tensor_scalar(xa[:, k * P:(k + 1) * P], lnT[:, k % HC, :], inv_in[:, k:k + 1], None,
                                          ALU.mult)
                w.then_inc(x_steps.sem, 1)
                dve.wait_ge(x_steps.sem, x_steps.now(t, 3))
                dve.tensor_scalar(b, a, FP8_MAX, -FP8_MAX, ALU.min, ALU.max).then_inc(x_steps.sem, 1)
                dve.wait_ge(x_steps.sem, x_steps.now(t, 4))
                dve.tensor_scalar(e.bitcast(U16), b.bitcast(U16), 0x7F80, None, ALU.bitwise_and
                                  ).then_inc(x_steps.sem, 1)
                dve.wait_ge(x_steps.sem, x_steps.now(t, 5))
                dve.tensor_scalar(m, e, FP8_SMALLEST, FP8_ROUND, ALU.max, ALU.mult).then_inc(x_steps.sem, 1)
                dve.wait_ge(x_steps.sem, x_steps.now(t, 6))
                dve.tensor_tensor(a, b, m, ALU.add).then_inc(x_steps.sem, 1)
                dve.wait_ge(x_steps.sem, x_steps.now(t, 7))
                dve.tensor_tensor(a, a, m, ALU.subtract).then_inc(x_steps.sem, 1)
                dve.wait_ge(x_steps.sem, x_steps.now(t, 8))
                dve.wait_ge(p_done.sem, p_done.before(t, 8))
                dve.tensor_tensor(xq[:], a.rearrange("p (k t) -> p k t", t=P),
                                  vecs[:, 4:10].unsqueeze(2).to_broadcast([P, KINDS * HC, P]), ALU.mult
                                  ).then_inc(xq_done.sem, 1)

            def copy_heads(t, k):
                if k == 0:
                    dve.wait_ge(t_done.sem, t_done.before(t, 6))
                dve.wait_ge(p_done.sem, p_done.now(t, k + 1))
                w = vecs[:, 14:15] if k < 4 else vecs[:, 15:16]
                dve.tensor_scalar(qk[:, 4 * k:4 * k + 4, :].rearrange("p h e -> p (h e)"), banks[PB[k]][:, :], w,
                                  None, ALU.mult).then_inc(p_copied.sem, 1)

            def norm_heads(t):
                dve.wait_ge(rs_done.sem, rs_done.now(t, 1))
                dve.tensor_tensor(qk[:], qk[:], rs[:].unsqueeze(2).to_broadcast([P, NK, HD]), ALU.mult
                                  ).then_inc(qn_done.sem, 1)

            def shift_scores(t):
                sview = SB[:, :].rearrange("p (h k) -> p h k", h=NH)
                dve.wait_ge(s_done.sem, s_done.now(t, 1))
                dve.tensor_reduce(ntop[:], sview, AX.X, ALU.max, negate=True).then_inc(sm_steps.sem, 1)
                dve.wait_ge(sm_steps.sem, sm_steps.now(t, 1))
                dve.tensor_tensor(sc[:], sview, ntop[:].unsqueeze(2).to_broadcast([P, NH, S]), ALU.add
                                  ).then_inc(sub_done.sem, 1)

            def norm_probs(t):
                dve.wait_ge(e_done.sem, e_done.now(t, 1))
                dve.tensor_reduce(sums[:], pr[:], AX.X, ALU.add).then_inc(sm_steps.sem, 1)
                dve.wait_ge(sm_steps.sem, sm_steps.now(t, 2))
                dve.reciprocal(rsum[:], sums[:]).then_inc(sm_steps.sem, 1)
                dve.wait_ge(sm_steps.sem, sm_steps.now(t, 3))
                dve.tensor_tensor(pr[:], pr[:], rsum[:].unsqueeze(2).to_broadcast([P, NH, S]), ALU.mult
                                  ).then_inc(sm_steps.sem, 1)
                dve.wait_ge(sm_steps.sem, sm_steps.now(t, 4))
                dve.wait_ge(o_done.sem, o_done.before(t, 1))
                dve.transpose(prT[:].rearrange("p h k -> p (h k)"), pr[:].rearrange("p h k -> p (h k)")
                              ).then_inc(pT_done.sem, 1)

            def quantise_heads(t):
                wide = qa[:].rearrange("p (h t) -> p h t", h=NH)
                dve.wait_ge(o_done.sem, o_done.now(t, 1))
                dve.wait_ge(o_copied.sem, o_copied.before(t, 1))
                for b in range(BT):
                    w = dve.tensor_tensor(wide[:, :, b * S:(b + 1) * S], OB[b][:, :].rearrange("p (h q) -> p h q", h=NH),
                                          inv_sm[:].unsqueeze(2).to_broadcast([P, NH, S]), ALU.mult)
                w.then_inc(oq_steps.sem, 1)
                dve.wait_ge(oq_steps.sem, oq_steps.now(t, 1))
                dve.tensor_scalar(qb[:], qa[:], FP8_MAX, -FP8_MAX, ALU.min, ALU.max).then_inc(oq_steps.sem, 1)
                dve.wait_ge(oq_steps.sem, oq_steps.now(t, 2))
                dve.tensor_scalar(qe[:].bitcast(U16), qb[:].bitcast(U16), 0x7F80, None, ALU.bitwise_and
                                  ).then_inc(oq_steps.sem, 1)
                dve.wait_ge(oq_steps.sem, oq_steps.now(t, 3))
                dve.tensor_scalar(qm[:], qe[:], FP8_SMALLEST, FP8_ROUND, ALU.max, ALU.mult).then_inc(oq_steps.sem, 1)

            def copy_output(t):
                dve.wait_ge(y_done.sem, y_done.now(t, 1))
                dve.tensor_scalar(Yc[:, t, :], YB[:, 0:H], yscale[:], None, ALU.mult).then_inc(y_copied.sem, 1)

            def tile(i, h, cur, one, two):
                if cur:
                    shift_scores(i)
                if one:
                    copy_heads(i + 1, 0)
                if cur:
                    norm_probs(i)
                if one:
                    copy_heads(i + 1, 1)
                if h is not None:
                    copy_output(h)
                if one:
                    copy_heads(i + 1, 2)
                if two:
                    token_stats(i + 2)
                if one:
                    copy_heads(i + 1, 3)
                if two:
                    token_stats_again(i + 2)
                if one:
                    copy_heads(i + 1, 4)
                if two:
                    norm_tokens(i + 2)
                if one:
                    copy_heads(i + 1, 5)
                    norm_heads(i + 1)
                if two:
                    quantise_tokens(i + 2)
                if cur:
                    quantise_heads(i)

            def all_tokens(t):
                token_stats(t)
                token_stats_again(t)
                norm_tokens(t)
                quantise_tokens(t)

            all_tokens(0)
            for k in range(6):
                copy_heads(0, k)
            norm_heads(0)
            all_tokens(1)
            run(dve, tile)


def difference_attention(nc, d, X, ident, tiles):
    n = "a1_"
    NHA = 16
    HALVES = 2 * NHA
    DH = 8
    DV = 2 * DH
    NJ = HALVES // 4
    LAMBDA_INIT = 0.8 - 0.6 * math.exp(-0.3 * 12)
    with Part(nc) as ctx:
        def sb(name, shape, dt=F32):
            return ctx.enter_context(nc.sbuf_tensor(n + name, shape, dt))

        def sig(name, per, unit=1):
            return Signal(ctx, nc, n + name, per, unit)

        wqk = sb("wqk", [P, HC, 2 * NJ * P])
        wv = sb("wv", [P, HC, H])
        wo = sb("wo", [P, HC, H])
        lam = sb("lam", [P, 4, DH])
        lamp = sb("lamp", [P, 2, DH])
        lams = sb("lams", [P, 2])
        lame = sb("lame", [P, 2])
        nlam = sb("nlam", [P, 1])
        subw = sb("subw", [P, DV])
        qkT = sb("qkT", [P, 2 * NJ, P])
        vn = sb("vn", [P, H])
        ntop = sb("ntop", [P, 4, NJ])
        sc = sb("sc", [P, 4, NJ, S])
        pr = sb("pr", [P, 4, NJ, S])
        sums = sb("sums", [P, 4, NJ])
        rsum = sb("rsum", [P, 4, NJ])
        df = sb("df", [P, 2, NJ, S])
        dfT = sb("dfT", [P, 2, NJ, S])
        at = sb("at", [P, H])
        asq = sb("asq", [P, H])
        ass = sb("ass", [P, NHA])
        ars = sb("ars", [P, NHA])
        aT = sb("aT", [P, HC, P])
        eps = sb("eps", [P, 1])
        banks = [ctx.enter_context(nc.psum_tensor(f"{n}B{k}", [P, 512], F32)) for k in range(8)]
        ln = TokenNorm(ctx, nc, n, X, ident, pt=1)
        weights = ctx.semaphore(n + "weights")
        late_weights = ctx.semaphore(n + "late_weights")
        setup = ctx.semaphore(n + "setup_steps")
        lam_exp = ctx.semaphore(n + "lambda_exp")
        gate = ctx.semaphore(n + "gate")
        p_done = sig("projected", 5)
        p_copied = sig("projected_copied", 5)
        s_done = sig("scores_done", 1)
        sub_done = sig("scores_shifted", 1)
        e_done = sig("exp_done", 1)
        dT_done = sig("difference_transposed", 1)
        o_done = sig("heads_out", 1)
        at_copied = sig("heads_read", 1)
        a_sum = sig("squares_summed", 1)
        a_log = sig("squares_log", 1)
        a_rs = sig("heads_rsqrt", 1)
        a_done = sig("heads_normed", 1)
        aT_done = sig("heads_transposed", 1)
        aT_copied = sig("heads_copied", 1)
        y_done = sig("y_done", 1)
        x_added = sig("x_added", 1)
        dchain = Chain(ctx, nc, n + "dve_chain", 1 + 5 + 2)
        block = ctx.open_block()

        @block.sync
        def _(sp):
            for dst, src in ((wqk, d["wqk"].rearrange("(c p) n -> p c n", p=P)),
                             (wv, d["wv"].rearrange("(c p) n -> p c n", p=P)),
                             (lam, d["lam"]), (subw, d["subw"])):
                sp.dma_start(dst[:], src).then_inc(weights, 16)
            sp.dma_start(wo[:], d["wo"].rearrange("(c p) n -> p c n", p=P)).then_inc(late_weights, 16)

        PB = banks[4:6]
        TB, YB = banks[6], banks[7]

        def run(eng, tile):
            tile(0, None, True, True, True)
            with eng.Fori(0, tiles - 3) as h:
                tile(h + 1, h, True, True, True)
            tile(tiles - 2, tiles - 3, True, True, False)
            tile(tiles - 1, tiles - 2, True, False, False)
            tile(tiles, tiles - 1, False, False, False)

        @block.tensor
        def _(pe):
            for s in (ln.turned, p_done, s_done, o_done, aT_done, y_done):
                s.prime(pe)

            def transpose_tokens(t, h=None):
                if h is not None:
                    pe.wait_ge(aT_copied.sem, aT_copied.now(h, 1))
                pe.wait_ge(ln.normed.sem, ln.normed.now(t, 1))
                for c in range(HC):
                    m = pe.transpose(TB[:, c * P:(c + 1) * P], ln.xn[:, 0, c * P:(c + 1) * P], ident[:])
                    m.then_inc(ln.turned.sem, 1)

            def project(t, k):
                if k == 0:
                    pe.wait_ge(ln.copied.sem, ln.copied.now(t, HC))
                pe.wait_ge(p_copied.sem, p_copied.after(t, k - 1))
                for j in range(4 * k, 4 * k + 4):
                    for c in range(HC):
                        m = pe.matmul(PB[k % 2][:, j % 4 * P:(j % 4 + 1) * P], wqk[:, c, j * P:(j + 1) * P],
                                      ln.xnT[:, c, :], start=c == 0, stop=c == HC - 1)
                m.then_inc(p_done.sem, 1)

            def project_values(t):
                pe.wait_ge(p_copied.sem, p_copied.now(t, 3))
                for c in range(HC):
                    m = pe.matmul(PB[0][:, 0:H], ln.xnT[:, c, :], wv[:, c, :], start=c == 0, stop=c == HC - 1)
                m.then_inc(p_done.sem, 1)

            def scores(t):
                pe.wait_ge(p_copied.sem, p_copied.now(t, 4))
                pe.wait_ge(at_copied.sem, at_copied.before(t, 1))
                pe.sem_inc(gate, 1)
                for j in range(NJ):
                    for r in range(4):
                        for b in range(BT):
                            rows, tok = slice(32 * r, 32 * r + DH), slice(b * S, (b + 1) * S)
                            m = pe.matmul(banks[r][tok, j * S:(j + 1) * S], qkT[rows, j, tok], qkT[rows, NJ + j, tok],
                                          start=True, stop=True)
                m.then_inc(s_done.sem, 1)

            def weigh_values(t):
                pe.wait_ge(p_copied.sem, p_copied.now(t, 5))
                pe.wait_ge(dT_done.sem, dT_done.now(t, 1))
                pe.sem_inc(gate, 1)
                for h in range(NHA):
                    for b in range(BT):
                        tok = slice(b * S, (b + 1) * S)
                        m = pe.matmul(banks[b][tok, h * DV:(h + 1) * DV], dfT[tok, h % 2, h // 2, :],
                                      vn[tok, h * DV:(h + 1) * DV], start=True, stop=True)
                m.then_inc(o_done.sem, 1)

            def transpose_heads(t):
                pe.wait_ge(a_done.sem, a_done.now(t, 1))
                for c in range(HC):
                    m = pe.transpose(TB[:, c * P:(c + 1) * P], at[:, c * P:(c + 1) * P], ident[:])
                m.then_inc(aT_done.sem, 1)

            def project_out(t):
                pe.wait_ge(aT_copied.sem, aT_copied.now(t, 1))
                pe.wait_ge(x_added.sem, x_added.before(t, 1))
                for c in range(HC):
                    m = pe.matmul(YB[:, 0:H], aT[:, c, :], wo[:, c, :], start=c == 0, stop=c == HC - 1)
                m.then_inc(y_done.sem, 1)

            def tile(i, h, cur, one, two):
                if cur:
                    scores(i)
                for k in range(2 if one else 0):
                    project(i + 1, k)
                if h is not None:
                    if one:
                        pe.wait_ge(ln.copied.sem, ln.copied.now(i + 1, HC))
                    transpose_heads(h)
                for k in range(2, 4 if one else 2):
                    project(i + 1, k)
                if h is not None:
                    project_out(h)
                if cur:
                    weigh_values(i)
                if one:
                    project_values(i + 1)
                if two:
                    transpose_tokens(i + 2, h)

            transpose_tokens(0)
            pe.wait_ge(weights, 16 * 4)
            for k in range(4):
                project(0, k)
            project_values(0)
            transpose_tokens(1)
            pe.wait_ge(late_weights, 16)
            run(pe, tile)

        @block.scalar
        def _(act):
            ln.scalar_setup(act)
            for s in (p_copied, e_done, a_log, a_rs, aT_copied):
                s.prime(act)
            act.preload_act_table_set(EXPLN)
            act.wait_ge(setup, 2)
            act.activation(lame[:], lams[:], ACT.Exp).then_inc(lam_exp, 1)

            def copy_tokens(t):
                act.wait_ge(p_done.sem, p_done.before(t, 5))
                act.wait_ge(ln.turned.sem, ln.turned.now(t, HC))
                for c in range(HC):
                    act.activation(ln.xnT[:, c, :], TB[:, c * P:(c + 1) * P], ACT.Copy).then_inc(ln.copied.sem, 1)

            def copy_projected(t, k):
                act.wait_ge(p_done.sem, p_done.now(t, k + 1))
                if k == 0:
                    act.wait_ge(s_done.sem, s_done.before(t, 1))
                act.activation(qkT[:, 4 * k:4 * k + 4, :].rearrange("p j t -> p (j t)"), PB[k % 2][:, :], ACT.Copy
                               ).then_inc(p_copied.sem, 1)

            def copy_values(t):
                act.wait_ge(p_done.sem, p_done.now(t, 5))
                act.wait_ge(o_done.sem, o_done.before(t, 1))
                act.activation(vn[:], PB[0][:, 0:H], ACT.Copy).then_inc(p_copied.sem, 1)

            def exp_scores(t):
                act.wait_ge(sub_done.sem, sub_done.now(t, 1))
                act.activation(pr[:], sc[:], ACT.Exp, scale=DH ** -0.5).then_inc(e_done.sem, 1)

            def rsqrt_heads(t):
                act.wait_ge(a_sum.sem, a_sum.now(t, 1))
                act.activation(ars[:], ass[:], ACT.Ln, bias=eps[:], scale=1.0 / DV).then_inc(a_log.sem, 1)
                act.wait_ge(a_log.sem, a_log.now(t, 1))
                act.activation(ars[:], ars[:], ACT.Exp, scale=-0.5).then_inc(a_rs.sem, 1)

            def copy_heads(t):
                act.wait_ge(aT_done.sem, aT_done.now(t, 1))
                act.wait_ge(y_done.sem, y_done.before(t, 1))
                act.activation(aT[:].rearrange("p c t -> p (c t)"), TB[:, 0:H], ACT.Copy
                               ).then_inc(aT_copied.sem, 1)

            def tile(i, h, cur, one, two):
                if one:
                    copy_projected(i + 1, 0)
                if cur:
                    exp_scores(i)
                if one:
                    copy_projected(i + 1, 1)
                if h is not None:
                    copy_heads(h)
                if two:
                    ln.scalar_rsqrt(act, i + 2)
                if one:
                    copy_projected(i + 1, 2)
                    copy_projected(i + 1, 3)
                if cur:
                    rsqrt_heads(i)
                if one:
                    copy_values(i + 1)
                if two:
                    copy_tokens(i + 2)

            ln.scalar_rsqrt(act, 0)
            copy_tokens(0)
            for k in range(4):
                copy_projected(0, k)
            copy_values(0)
            ln.scalar_rsqrt(act, 1)
            copy_tokens(1)
            run(act, tile)

        @block.vector
        def _(dve):
            ln.vector_setup(dve)
            for s in (sub_done, dT_done, at_copied, a_sum, a_done, x_added, dchain):
                s.prime(dve)
            dve.memset(eps[:], 1e-5)
            dve.wait_ge(weights, 16 * 4)
            step = [0]

            def then(ins):
                step[0] += 1
                ins.then_inc(setup, 1)
                dve.wait_ge(setup, step[0])

            then(dve.tensor_tensor(lamp[:], lam[:, 0:4:2, :], lam[:, 1:4:2, :], ALU.mult))
            then(dve.tensor_reduce(lams[:], lamp[:], AX.X, ALU.add))
            dve.wait_ge(lam_exp, 1)
            then(dve.tensor_tensor(nlam[:], lame[:, 1:2], lame[:, 0:1], ALU.subtract))
            then(dve.tensor_scalar(nlam[:], nlam[:], LAMBDA_INIT, None, ALU.subtract))
            then(dve.tensor_scalar(subw[:], subw[:], 1.0 - LAMBDA_INIT, None, ALU.mult))

            def link(i, ins):
                ins.then_inc(dchain.sem, 1)
                dve.wait_ge(dchain.sem, dchain.next(i))

            def token_stats(t):
                dve.bn_stats(ln.stats[:, 0, :], X[:, t, :]).then_inc(ln.summed.sem, 1)
                dve.wait_ge(ln.summed.sem, ln.summed.now(t, 1))
                dve.sem_inc(gate, 1)
                dve.bn_aggr(ln.mv[:, 0, :], ln.stats[:, 0, :]).then_inc(ln.aggregated.sem, 1)

            def norm_tokens(t):
                dve.wait_ge(ln.scaled.sem, ln.scaled.now(t, 1))
                dve.wait_ge(ln.turned.sem, ln.turned.before(t, HC))
                dve.tensor_scalar(ln.xn[:, 0, :], X[:, t, :], ln.mv[:, 0, 0:1], ln.lr[:], ALU.subtract, ALU.mult
                                  ).then_inc(ln.normed.sem, 1)

            def shift_scores(i):
                dchain.k = 0
                dve.wait_ge(s_done.sem, s_done.now(i, 1))
                for r in range(4):
                    view = banks[r][:, 0:NJ * S].rearrange("p (j k) -> p j k", j=NJ)
                    a = dve.tensor_reduce(ntop[:, r, :], view, AX.X, ALU.max, negate=True)
                link(i, a)
                for r in range(4):
                    view = banks[r][:, 0:NJ * S].rearrange("p (j k) -> p j k", j=NJ)
                    a = dve.tensor_tensor(sc[:, r, :, :], view, ntop[:, r, :].unsqueeze(2).to_broadcast([P, NJ, S]),
                                          ALU.add)
                a.then_inc(sub_done.sem, 1)

            def difference(i):
                rows = lambda t: t[:].rearrange("p r j -> p (r j)")
                wide = pr[:].rearrange("p r j k -> p (r j) k")
                dve.wait_ge(e_done.sem, e_done.now(i, 1))
                link(i, dve.tensor_reduce(rows(sums), wide, AX.X, ALU.add))
                link(i, dve.reciprocal(rows(rsum), rows(sums)))
                link(i, dve.tensor_scalar(rsum[:, 1:4:2, :], rsum[:, 1:4:2, :], nlam[:], None, ALU.mult))
                link(i, dve.tensor_tensor(wide, wide, rows(rsum).unsqueeze(2).to_broadcast([P, 4 * NJ, S]), ALU.mult))
                for e in range(2):
                    a = dve.tensor_tensor(df[:, e, :, :], pr[:, 2 * e, :, :], pr[:, 2 * e + 1, :, :], ALU.add)
                link(i, a)
                dve.wait_ge(o_done.sem, o_done.before(i, 1))
                dve.transpose(dfT[:].rearrange("p e j k -> p (e j k)"), df[:].rearrange("p e j k -> p (e j k)")
                              ).then_inc(dT_done.sem, 1)

            def norm_heads(i):
                heads = lambda t: t[:].rearrange("p (h e) -> p h e", h=NHA)
                dve.wait_ge(o_done.sem, o_done.now(i, 1))
                dve.wait_ge(aT_done.sem, aT_done.before(i, 1))
                for b in range(BT):
                    tok = slice(b * S, (b + 1) * S)
                    a = dve.tensor_copy(at[tok, :], banks[b][tok, 0:H])
                a.then_inc(at_copied.sem, 1)
                dve.wait_ge(at_copied.sem, at_copied.now(i, 1))
                link(i, dve.tensor_tensor(asq[:], at[:], at[:], ALU.mult))
                dve.tensor_reduce(ass[:], heads(asq), AX.X, ALU.add).then_inc(a_sum.sem, 1)
                dve.wait_ge(a_rs.sem, a_rs.now(i, 1))
                link(i, dve.tensor_tensor(heads(at), heads(at), ars[:].unsqueeze(2).to_broadcast([P, NHA, DV]),
                                          ALU.mult))
                dve.tensor_tensor(heads(at), heads(at), subw[:].unsqueeze(1).to_broadcast([P, NHA, DV]), ALU.mult
                                  ).then_inc(a_done.sem, 1)
                dchain.done()

            def add_output(t):
                dve.wait_ge(y_done.sem, y_done.now(t, 1))
                dve.tensor_tensor(X[:, t, :], X[:, t, :], YB[:, 0:H], ALU.add).then_inc(x_added.sem, 1)

            def tile(i, h, cur, one, two):
                if cur:
                    shift_scores(i)
                if two:
                    token_stats(i + 2)
                if cur:
                    difference(i)
                if two:
                    norm_tokens(i + 2)
                if h is not None:
                    add_output(h)
                if cur:
                    norm_heads(i)

            for t in range(2):
                token_stats(t)
                norm_tokens(t)
            run(dve, tile)


def hadamard_ffn(nc, d, X, ident, tiles):
    n = "f1_"
    F = 1024
    FC = F // P
    GUARD = 64.0
    passes = tiles // PT
    N = PT * P
    with Part(nc) as ctx:
        def sb(name, shape, dt=F32):
            return ctx.enter_context(nc.sbuf_tensor(n + name, shape, dt))

        def bank(name):
            return ctx.enter_context(nc.psum_tensor(n + name, [P, 512], F32))

        def sig(name, per, unit=1):
            return Signal(ctx, nc, n + name, per, unit)

        raw = sb("raw", [P, HC, 2 * F])
        rawd = sb("rawd", [P, FC, H])
        wug = sb("wug", [P, HC, 2 * F])
        wd = sb("wd", [P, FC, H])
        had = sb("had", [P, 2, P])
        cols = sb("cols", [P, HC + FC + 2 * FC])
        wsd = sb("wsd", [P, H])
        su = sb("su", [P, HC])
        sd = sb("sd", [P, FC])
        su64 = sb("su64", [P, 2 * FC])
        g1 = sb("g1", [P, 2, N])
        gT = sb("gT", [P, FC, N])
        Ab = [bank("A0"), bank("A1")]
        Bb = [bank("B0"), bank("B1")]
        Yb = [bank("Y0"), bank("Y1")]
        Tb = [bank("T0"), bank("T1")]
        ln = TokenNorm(ctx, nc, n, X, ident)
        weights = ctx.semaphore(n + "weights")
        late_weights = ctx.semaphore(n + "late_weights")
        folded = ctx.semaphore(n + "folded")
        fold_read = ctx.semaphore(n + "fold_read")
        scales = ctx.semaphore(n + "scales")
        h_done = sig("hidden_done", 2 * FC)
        h_silu = sig("hidden_silu", FC)
        g_done = sig("gated", FC)
        y_done = sig("y_done", 2)
        x_added = sig("x_added", 2)
        FOLDS = HC * 4 + FC
        block = ctx.open_block()

        @block.sync
        def _(sp):
            for dst, src in ((had, d["had"]), (cols, d["cols"]), (wsd, d["wsd"]),
                             (raw, d["raw"].rearrange("(c p) n -> p c n", p=P))):
                sp.dma_start(dst[:], src).then_inc(weights, 16)
            sp.dma_start(rawd[:], d["rawd"].rearrange("(c p) n -> p c n", p=P)).then_inc(late_weights, 16)

        @block.tensor
        def _(pe):
            for s in (ln.turned, h_done, y_done):
                s.prime(pe)
            pe.wait_ge(weights, 16 * 4)
            for f in range(FOLDS):
                if f >= 2:
                    pe.wait_ge(fold_read, f - 1)
                if f < HC * 4:
                    a, k = f // 4, f % 4
                    for c in range(HC):
                        m = pe.matmul(Ab[f % 2][:, :], had[:, a & c, :], raw[:, c, k * 512:(k + 1) * 512],
                                      start=c == 0, stop=c == HC - 1)
                else:
                    a = f - HC * 4
                    if a == 0:
                        pe.wait_ge(late_weights, 16)
                    for c in range(FC):
                        m = pe.matmul(Ab[f % 2][:, 0:H], had[:, bin(a & c).count("1") % 2, :], rawd[:, c, :],
                                      start=c == 0, stop=c == FC - 1)
                m.then_inc(folded, 1)
            pe.wait_ge(fold_read, FOLDS)
            def one_pass(i, nxt):
                pe.wait_ge(ln.copied.sem, ln.copied.now(i, HC))
                for k in range(FC):
                    pe.wait_ge(g_done.sem, g_done.after(i, k - 1))
                    for w, b in ((F, Ab), (0, Bb)):
                        for c in range(HC):
                            m = pe.matmul(b[k % 2][:, :], wug[:, c, w + k * P:w + (k + 1) * P], ln.xnT[:, c, :],
                                          start=c == 0, stop=c == HC - 1)
                        m.then_inc(h_done.sem, 1)
                pe.wait_ge(g_done.sem, g_done.now(i, FC))
                for y in range(2):
                    if y == 1 and nxt:
                        ln.tensor(pe, i + 1, Tb)
                    pe.wait_ge(x_added.sem, x_added.before(i, y + 1))
                    for t in (2 * y, 2 * y + 1):
                        for k in range(FC):
                            m = pe.matmul(Yb[y][:, t % 2 * H:t % 2 * H + H], gT[:, k, t * P:(t + 1) * P], wd[:, k, :],
                                          start=k == 0, stop=k == FC - 1)
                    m.then_inc(y_done.sem, 1)

            ln.tensor(pe, 0, Tb)
            with pe.Fori(0, passes - 1) as i:
                one_pass(i, True)
            one_pass(passes - 1, False)

        @block.scalar
        def _(act):
            ln.scalar_setup(act)
            h_silu.prime(act)
            act.wait_ge(scales, 4)
            def one_pass(i, nxt):
                for k in range(FC):
                    act.wait_ge(h_done.sem, h_done.now(i, 2 * k + 1))
                    act.wait_ge(g_done.sem, g_done.after(i, k - 1))
                    act.activation(g1[:, k % 2, :], Ab[k % 2][:, :], ACT.Silu, scale=su64[:, FC + k:FC + k + 1]
                                   ).then_inc(h_silu.sem, 1)
                if nxt:
                    ln.scalar_rsqrt(act, i + 1)
                    act.wait_ge(h_done.sem, h_done.now(i, 2 * FC))
                    ln.scalar_copy(act, i + 1, Tb)

            ln.scalar_rsqrt(act, 0)
            ln.scalar_copy(act, 0, Tb)
            with act.Fori(0, passes - 1) as i:
                one_pass(i, True)
            one_pass(passes - 1, False)

        @block.vector
        def _(dve):
            ln.vector_setup(dve)
            for s in (g_done, x_added):
                s.prime(dve)
            dve.wait_ge(weights, 16 * 4)
            dve.tensor_scalar(su[:], cols[:, 0:HC], 1.0 / (H ** 0.5 * GUARD), None, ALU.mult).then_inc(scales, 1)
            dve.tensor_scalar(sd[:], cols[:, HC:HC + FC], 1.0 / (F ** 0.5 * GUARD), None, ALU.mult
                              ).then_inc(scales, 1)
            dve.tensor_scalar(su64[:], cols[:, HC + FC:], GUARD, None, ALU.mult).then_inc(scales, 1)
            dve.tensor_scalar(wsd[:], wsd[:], GUARD, None, ALU.mult).then_inc(scales, 1)
            dve.wait_ge(scales, 4)
            for f in range(FOLDS):
                dve.wait_ge(folded, f + 1)
                if f < HC * 4:
                    a, k = f // 4, f % 4
                    m = dve.tensor_scalar(wug[:, a, k * 512:(k + 1) * 512], Ab[f % 2][:, :], su[:, a:a + 1], None,
                                          ALU.mult)
                else:
                    a = f - HC * 4
                    m = dve.scalar_tensor_tensor(wd[:, a, :], Ab[f % 2][:, 0:H], sd[:, a:a + 1], wsd[:],
                                                 ALU.mult, ALU.mult)
                m.then_inc(fold_read, 1)
            def one_pass(i, nxt):
                for k in range(FC):
                    dve.wait_ge(h_silu.sem, h_silu.now(i, k + 1))
                    dve.wait_ge(h_done.sem, h_done.now(i, 2 * k + 2))
                    if k == 0:
                        dve.wait_ge(y_done.sem, y_done.before(i, 2))
                    dve.scalar_tensor_tensor(gT[:, k, :], Bb[k % 2][:, :], su64[:, k:k + 1], g1[:, k % 2, :],
                                             ALU.mult, ALU.mult).then_inc(g_done.sem, 1)
                if nxt:
                    ln.vector(dve, i + 1)
                for y in range(2):
                    dve.wait_ge(y_done.sem, y_done.now(i, y + 1))
                    for t in (2 * y, 2 * y + 1):
                        Xt = X[:, i * PT + t, :]
                        a = dve.tensor_tensor(Xt, Xt, Yb[y][:, t % 2 * H:t % 2 * H + H], ALU.add)
                    a.then_inc(x_added.sem, 1)

            ln.vector(dve, 0)
            with dve.Fori(0, passes - 1) as i:
                one_pass(i, True)
            one_pass(passes - 1, False)


def build(nc, d, out, n_batches):
    tiles = n_batches // BT
    with ExitStack() as ctx:
        X = ctx.enter_context(nc.sbuf_tensor("X", [P, tiles, H], F32))
        Yc = ctx.enter_context(nc.sbuf_tensor("Yc", [P, tiles, H], F32))
        ident = ctx.enter_context(nc.sbuf_tensor("ident", [P, P], F32))
        loaded = ctx.enter_context(nc.semaphore("loaded"))
        stored = ctx.enter_context(nc.semaphore("stored"))
        x_rows = d["x"].rearrange("(t b) s c -> (b s) t c", b=BT)
        out_rows = out.rearrange("(t b) s c -> (b s) t c", b=BT)
        with nc.Block() as block:
            @block.sync
            def _(sp):
                sp.dma_start(X[:], x_rows).then_inc(loaded, 16)
                sp.dma_start(ident[:], d["ident"]).then_inc(loaded, 16)
                sp.wait_ge(loaded, 32)
        cross_attention(nc, sub(d, "x0_"), X, Yc, ident, 0, tiles)
        product_attention(nc, sub(d, "a0_"), X, ident, tiles)
        experts(nc, sub(d, "e0_"), X, ident, tiles)
        core_attention(nc, sub(d, "c1_"), X, Yc, ident, tiles)
        cross_attention(nc, sub(d, "x1_"), X, Yc, ident, 1, tiles)
        difference_attention(nc, sub(d, "a1_"), X, ident, tiles)
        hadamard_ffn(nc, sub(d, "f1_"), X, ident, tiles)
        with nc.Block() as block:
            @block.sync
            def _(sp):
                sp.dma_start(out_rows, X[:]).then_inc(stored, 16)
                sp.wait_ge(stored, 16)


def sub(d, prefix):
    got = {k[len(prefix):]: v for k, v in d.items() if k.startswith(prefix)}
    got["ctx"] = d["ctx"]
    return got


def lay_out(inputs):
    import numpy as np
    g = {k: np.asarray(v) for k, v in inputs.items()}
    T = lambda a: np.ascontiguousarray(a.T)
    rows = lambda a, n=128: np.ascontiguousarray(np.broadcast_to(a, (n,) + a.shape))
    col = lambda a: np.ascontiguousarray(a.reshape(-1, 128).T)
    one = lambda a: np.ascontiguousarray(np.broadcast_to(a.reshape(1, 1), (128, 1)))
    a = {"x": g["x"], "ctx": g["ctx_2048"], "ident": np.eye(128, dtype=np.float32)}
    a["x0_wq"], a["x0_wk"], a["x0_wv"], a["x0_wo"] = (g["L0_xattn_" + w] for w in ("Wq", "Wk", "Wv", "Wo"))
    a["x0_bq"] = rows(g["L0_xattn_bq"])
    a["x0_bkv"] = np.stack([col(g["L0_xattn_bk"]), col(g["L0_xattn_bv"])], 1)
    a["x0_nw"] = np.stack([g["L0_xattn_qn_w"], g["L0_xattn_kn_w"]], 1)
    a["x0_mask"] = np.tile(g["mask_1xSxS2_ff0"][0], (4, 1))
    wkv = g["L1_xattn_w_kv_x"]
    a["x1_wq"], a["x1_wk"], a["x1_wv"] = T(g["L1_xattn_wqx"]), T(wkv[0:1024]), T(wkv[1024:2048])
    a["x1_wo"] = T(g["L1_xattn_wproj"][:, 2048:4096])
    a["x1_smooth"] = col(g["L1_xattn_proj_smooth"][2048:4096])
    a["x1_vecs"] = np.concatenate(
        [col(g["L1_xattn_ln_w"]), col(g["L1_xattn_ln_b"]), col(g["L1_xattn_qx_in_scale"]),
         col(g["L1_xattn_qxln_w"]), col(g["L1_xattn_qxln_b"]), col(g["L1_xattn_kxln_w"]), col(g["L1_xattn_kxln_b"]),
         one(g["L1_xattn_wqx_scale"]), one(g["L1_xattn_proj_in_scale"]), one(g["L1_xattn_proj_w_scale"]),
         np.zeros((128, 11), np.float32)], 1)
    def slots(w):
        out = np.zeros((16, 32, w.shape[1]), np.float32)
        out[:, 0:16] = w.reshape(16, 16, -1)
        return out.reshape(512, -1)
    a["a0_wq"], a["a0_kT"] = T(slots(g["L0_attn_Wq"])), slots(T(g["L0_attn_k_weight"])).reshape(4, 128, 512)
    a["a0_vw"], a["a0_wg"] = T(slots(T(g["L0_attn_v_weight"]))), T(slots(g["L0_attn_Wg"]))
    a["a0_wo"] = slots(T(g["L0_attn_Wout"]))
    for w in ("w1", "w3"):
        a["e0_" + w] = T(np.concatenate([g["L0_ffn_" + w].reshape(1024, 256), g["L0_ffn_ws" + w[1]]]))
    a["e0_w2"] = np.concatenate([g["L0_ffn_w2"].transpose(0, 2, 1).reshape(1024, 256), g["L0_ffn_ws2"].T])
    a["e0_wr"] = T(g["L0_ffn_gate_w"])
    a["e0_places"] = rows(np.arange(8, dtype=np.float32))
    a["c1_wqk"] = T(np.concatenate([g["L1_xattn_wq"], g["L1_xattn_wk"]]))
    a["c1_wv"], a["c1_wo"] = T(g["L1_xattn_wv"]), T(g["L1_xattn_wproj"][:, 0:2048])
    a["c1_smooth"] = col(g["L1_xattn_proj_smooth"][0:2048])
    a["c1_vecs"] = np.concatenate(
        [col(g["L1_xattn_" + k]) for k in ("ln_w", "ln_b", "q_in_scale", "k_in_scale", "v_in_scale",
                                           "qln_w", "qln_b", "kln_w", "kln_b")]
        + [one(g["L1_xattn_" + k]) for k in ("wq_scale", "wk_scale", "wv_scale", "proj_in_scale", "proj_w_scale")]
        + [np.zeros((128, 1), np.float32)], 1)
    def half_slots(w):
        out = np.zeros((32, 32, 256), np.float32)
        out[:, 0:8] = w.reshape(32, 8, 256)
        return T(out.reshape(1024, 256))
    a["a1_wqk"] = np.concatenate([half_slots(g["L1_attn_wq"]), half_slots(g["L1_attn_wk"])], 1)
    a["a1_wv"], a["a1_wo"] = T(g["L1_attn_wv"]), T(g["L1_attn_wo"])
    a["a1_lam"] = rows(np.stack([g["L1_attn_lambda_" + k] for k in ("q1", "k1", "q2", "k2")]))
    a["a1_subw"] = rows(g["L1_attn_subln_w"])
    had = np.ones((1, 1), np.float32)
    while len(had) < 128:
        had = np.block([[had, had], [had, -had]])
    a["f1_had"] = np.stack([had, -had], 1)
    a["f1_raw"] = np.concatenate([T(g["L1_ffn_W_up"]), T(g["L1_ffn_W_gate"])], 1)
    a["f1_rawd"] = T(g["L1_ffn_W_down"])
    a["f1_cols"] = np.concatenate([col(g["L1_ffn_SU_ug"]), col(g["L1_ffn_SU_dp"]), col(g["L1_ffn_Wscale_ug"])], 1)
    a["f1_wsd"] = rows(g["L1_ffn_Wscale_dp"])
    return {k: np.ascontiguousarray(v) for k, v in a.items()}


def kernel(**inputs):
    import concourse.bacc as bacc
    from concourse.bass_utils import run_bass_kernel_spmd as run

    arrays = lay_out(inputs)
    nc = bacc.Bacc("TRN2", target_bir_lowering=False, num_devices=1)
    d = {k: nc.dram_tensor("in_" + k, v.shape, mybir.dt.from_np(v.dtype), kind="ExternalInput").ap()
         for k, v in arrays.items()}
    shape = inputs["x"].shape
    out = nc.dram_tensor("out_x", tuple(shape), F32, kind="ExternalOutput").ap()
    build(nc, d, out, shape[0])
    r = run(nc, [{"in_" + k: v for k, v in arrays.items()}], core_ids=[0])
    return r.results[0]["out_x"]
```
